# Optimizing a Trainium2 kernel written in Bass

```python
import numpy as np
import jax
import jax.numpy as jnp

def _softmax(x, axis=-1):
    return jax.nn.softmax(x, axis=axis)

def _gelu(x):
    return jax.nn.gelu(x, approximate=True)

def _silu(x):
    return jax.nn.silu(x)

def _sigmoid(x):
    return jax.nn.sigmoid(x)

def _layernorm(x, axis=-1, eps=1e-05):
    m = jnp.mean(x, axis=axis, keepdims=True)
    v = jnp.var(x, axis=axis, keepdims=True)
    return (x - m) / jnp.sqrt(v + eps)

def _scatter_add(tgt, idx, src, axis=0):
    return tgt.at[idx].add(src)

def _segment_sum(src, seg, n):
    return jax.ops.segment_sum(src, seg, n)
kernel_name = 'mk_pixart_resid_d4_seqx_r8_13fe7b'

def setup_inputs(seed: int=0):
    np.random.seed(seed)
    _w = jnp.asarray

    def _rec_inputs():
        import jax
        import jax.numpy as jnp
        _rk = jax.random.key(seed)
        x = -0.0002928 + 1 * jax.random.normal(jax.random.fold_in(_rk, 1), (2, 512, 128), jnp.float32)
        _lenS = 512 - jax.random.randint(jax.random.fold_in(_rk, 7), (2,), 0, max(1, 512 // 4) + 1, jnp.int32)
        _lenS2 = 77 - jax.random.randint(jax.random.fold_in(_rk, 8), (2,), 0, max(1, 77 // 4) + 1, jnp.int32)
        _ctx_1024P = jax.random.normal(jax.random.fold_in(_rk, 11), (2, 16, 128), jnp.float32)
        _ctx_1024c = jax.random.dirichlet(jax.random.fold_in(_rk, 511), 0.3 * jnp.ones((16,), jnp.float32), (2, 77))
        _ctx_1024t = jnp.einsum('bsk,bkd->bsd', _ctx_1024c, _ctx_1024P)
        _ctx_1024t = _ctx_1024t * jax.lax.rsqrt(jnp.mean(jnp.square(_ctx_1024t)) + 1e-12) * 0.953939
        ctx_1024 = -1.39393e-06 + 0.999914 * (_ctx_1024t + 0.3 * jax.random.normal(jax.random.fold_in(_rk, 611), (2, 77, 128), jnp.float32))
        condB_tau = jax.random.uniform(jax.random.fold_in(_rk, 12), (2,), jnp.float32, 0.0, 1.23395)
        fside_BxS2_0 = -0.00205293 + 0.99739 * jax.random.normal(jax.random.fold_in(_rk, 13), (2, 77), jnp.float32)
        condB_pt = jax.random.uniform(jax.random.fold_in(_rk, 15), (2,), jnp.float32, 0.0, 226.919)
        return (x, ctx_1024, condB_tau, fside_BxS2_0, condB_pt, _lenS2)
    x, ctx_1024, condB_tau, fside_BxS2_0, condB_pt, _lenS2 = _rec_inputs()

    def _L0_xcond_setup():
        import jax, jax.numpy as jnp
        import numpy as np
        B, S, D, H = (2, 256, 128, 16)
        DK = D // H

        def _split_heads(x):
            b, s, _ = x.shape
            return x.reshape(b, s, H, DK).transpose(0, 2, 1, 3)
        key = jax.random.key(seed)
        ks = jax.random.split(key, 14)
        inp = {'query': jax.random.normal(ks[0], (B, S, D), jnp.float32), 'key': jax.random.normal(ks[1], (B, S, D), jnp.float32), 'value': jax.random.normal(ks[2], (B, S, D), jnp.float32), 'tau': jax.random.uniform(ks[3], (B, 1), jnp.float32, 0.5, 1.5), 'delta': jax.random.normal(ks[4], (B, S), jnp.float32)}
        sc = 1.0 / np.sqrt(D)
        for i, name in enumerate(['q', 'k', 'v', 'o']):
            inp[f'W{name}'] = jax.random.normal(ks[5 + 2 * i], (D, D), jnp.float32) * sc
            inp[f'b{name}'] = jax.random.normal(ks[6 + 2 * i], (D,), jnp.float32) * 0.01
        return inp
    _L0_xcond_all = _L0_xcond_setup()
    _L0_xcond_in = {k: v for k, v in _L0_xcond_all.items() if k in ('Wq', 'bq', 'Wk', 'bk', 'Wv', 'bv', 'Wo', 'bo')}
    del _L0_xcond_all

    def _L0_ffn_setup():
        import jax, jax.numpy as jnp
        import numpy as np
        HID, FFN, NE, TOPK = (128, 512, 8, 2)
        key = jax.random.key(seed)
        ks = jax.random.split(key, 4)
        x = jax.random.normal(ks[0], (2, 256, HID), dtype=jnp.float32)
        Wr = jax.random.normal(ks[1], (HID, NE), dtype=jnp.float32) * 0.02
        W1 = jax.random.normal(ks[2], (NE, HID, FFN), dtype=jnp.float32) * (1.0 / np.sqrt(HID))
        b1 = jnp.zeros((NE, FFN), dtype=jnp.float32)
        W2 = jax.random.normal(ks[3], (NE, FFN, HID), dtype=jnp.float32) * (1.0 / np.sqrt(FFN))
        b2 = jnp.zeros((NE, HID), dtype=jnp.float32)
        return {'x': x, 'Wr': Wr, 'W1': W1, 'b1': b1, 'W2': W2, 'b2': b2}
    _L0_ffn_all = _L0_ffn_setup()
    _L0_ffn_in = {k: v for k, v in _L0_ffn_all.items() if k in ('Wr', 'W1', 'b1', 'W2', 'b2')}
    del _L0_ffn_all

    def _L1_xcond_setup():
        import jax, jax.numpy as jnp
        import numpy as np
        D_MODEL = 128
        N_HEADS = 16
        key = jax.random.key(seed)
        ks = jax.random.split(key, 16)
        B, L, S, D = (4, 256, 256, D_MODEL)
        inp = {'q': jax.random.normal(ks[0], (B, L, D), jnp.float32), 'k': jax.random.normal(ks[1], (B, S, D), jnp.float32), 'v': jax.random.normal(ks[2], (B, S, D), jnp.float32), 'tau': jax.random.uniform(ks[3], (B, 1), jnp.float32, 0.5, 1.5), 'delta': jax.random.normal(ks[4], (B, S), jnp.float32)}
        s = 1.0 / np.sqrt(D)
        inp['Wq'] = jax.random.normal(ks[5], (D, D), jnp.float32) * s
        inp['bq'] = jnp.zeros((D,), jnp.float32)
        inp['Wk'] = jax.random.normal(ks[6], (D, D), jnp.float32) * s
        inp['bk'] = jnp.zeros((D,), jnp.float32)
        inp['Wv'] = jax.random.normal(ks[7], (D, D), jnp.float32) * s
        inp['bv'] = jnp.zeros((D,), jnp.float32)
        inp['Wo'] = jax.random.normal(ks[8], (D, D), jnp.float32) * s
        inp['bo'] = jnp.zeros((D,), jnp.float32)
        return inp
    _L1_xcond_all = _L1_xcond_setup()
    _L1_xcond_in = {k: v for k, v in _L1_xcond_all.items() if k in ('Wq', 'bq', 'Wk', 'bk', 'Wv', 'bv', 'Wo', 'bo')}
    del _L1_xcond_all

    def _L1_ffn_setup():
        import jax, jax.numpy as jnp
        import numpy as np
        B, S, H = (2, 256, 128)
        N, F, SF, K = (16, 128, 512, 1)
        key = jax.random.key(seed)
        ks = jax.random.split(key, 7)
        std = 0.02
        return {'hidden_states': jax.random.normal(ks[0], (B, S, H), dtype=jnp.float32), 'router_w': jax.random.normal(ks[1], (N, H), dtype=jnp.float32) * std, 'gate_up_proj': jax.random.normal(ks[2], (N, H, 2 * F), dtype=jnp.float32) * std, 'down_proj': jax.random.normal(ks[3], (N, F, H), dtype=jnp.float32) * std, 'shared_gate_w': jax.random.normal(ks[4], (SF, H), dtype=jnp.float32) * std, 'shared_up_w': jax.random.normal(ks[5], (SF, H), dtype=jnp.float32) * std, 'shared_down_w': jax.random.normal(ks[6], (H, SF), dtype=jnp.float32) * std}
    _L1_ffn_all = _L1_ffn_setup()
    _L1_ffn_in = {k: v for k, v in _L1_ffn_all.items() if k in ('router_w', 'gate_up_proj', 'down_proj', 'shared_gate_w', 'shared_up_w', 'shared_down_w')}
    del _L1_ffn_all

    def _L2_xcond_setup():
        import jax, jax.numpy as jnp
        import numpy as np
        N, L, H, Q = (64, 258, 128, 32)
        WINDOW = 16.0
        DEV_POW = 128.0
        key = jax.random.key(seed)
        k1, k2, k3, k4, k5, k6 = jax.random.split(key, 6)
        encoder_outputs = jax.random.normal(k1, (N, L, H), dtype=jnp.float32)
        decoder_h_t = jax.random.normal(k2, (N, Q, H), dtype=jnp.float32)
        src_len = jax.random.randint(k3, (N,), 32, L + 1).astype(jnp.int32)
        p_t = jax.random.uniform(k4, (N,), dtype=jnp.float32) * (src_len.astype(jnp.float32) - 1.0)
        W_a = jax.random.normal(k5, (H, H), dtype=jnp.float32) * (1.0 / np.sqrt(H))
        W_c = jax.random.normal(k6, (H, 2 * H), dtype=jnp.float32) * (1.0 / np.sqrt(2 * H))
        return {'encoder_outputs': encoder_outputs, 'decoder_h_t': decoder_h_t, 'src_len': src_len, 'p_t': p_t, 'W_a': W_a, 'W_c': W_c}
    _L2_xcond_all = _L2_xcond_setup()
    _L2_xcond_in = {k: v for k, v in _L2_xcond_all.items() if k in ('W_a', 'W_c')}
    del _L2_xcond_all

    def _L2_ffn_setup():
        import jax, jax.numpy as jnp
        import numpy as np
        H, I, E_ROUTED, TOP_K = (128, 352, 7, 2)
        B, S = (4, 256)

        def _expert(h, g, u, d):
            return jnp.einsum('...i,hi->...h', jax.nn.silu(h @ g.T) * (h @ u.T), d)
        key = jax.random.key(seed)
        ks = jax.random.split(key, 10)
        sc = 0.02
        return {'x': jax.random.normal(ks[0], (B, S, H), dtype=jnp.float32), 'sg': jax.random.normal(ks[1], (I, H), dtype=jnp.float32) * sc, 'su': jax.random.normal(ks[2], (I, H), dtype=jnp.float32) * sc, 'sd': jax.random.normal(ks[3], (H, I), dtype=jnp.float32) * sc, 'rg': jax.random.normal(ks[4], (E_ROUTED, I, H), dtype=jnp.float32) * sc, 'ru': jax.random.normal(ks[5], (E_ROUTED, I, H), dtype=jnp.float32) * sc, 'rd': jax.random.normal(ks[6], (E_ROUTED, H, I), dtype=jnp.float32) * sc, 'wr': jax.random.normal(ks[7], (E_ROUTED, H), dtype=jnp.float32) * sc, 'rb': jnp.zeros((E_ROUTED,), dtype=jnp.float32)}
    _L2_ffn_all = _L2_ffn_setup()
    _L2_ffn_in = {k: v for k, v in _L2_ffn_all.items() if k in ('sg', 'su', 'sd', 'rg', 'ru', 'rd', 'wr', 'rb')}
    del _L2_ffn_all

    def _L3_xcond_setup():
        import jax, jax.numpy as jnp
        import numpy as np
        B, S, D, H = (2, 256, 128, 16)
        DK = D // H

        def _split_heads(x):
            b, s, _ = x.shape
            return x.reshape(b, s, H, DK).transpose(0, 2, 1, 3)
        key = jax.random.key(seed)
        ks = jax.random.split(key, 14)
        inp = {'query': jax.random.normal(ks[0], (B, S, D), jnp.float32), 'key': jax.random.normal(ks[1], (B, S, D), jnp.float32), 'value': jax.random.normal(ks[2], (B, S, D), jnp.float32), 'tau': jax.random.uniform(ks[3], (B, 1), jnp.float32, 0.5, 1.5), 'delta': jax.random.normal(ks[4], (B, S), jnp.float32)}
        sc = 1.0 / np.sqrt(D)
        for i, name in enumerate(['q', 'k', 'v', 'o']):
            inp[f'W{name}'] = jax.random.normal(ks[5 + 2 * i], (D, D), jnp.float32) * sc
            inp[f'b{name}'] = jax.random.normal(ks[6 + 2 * i], (D,), jnp.float32) * 0.01
        return inp
    _L3_xcond_all = _L3_xcond_setup()
    _L3_xcond_in = {k: v for k, v in _L3_xcond_all.items() if k in ('Wq', 'bq', 'Wk', 'bk', 'Wv', 'bv', 'Wo', 'bo')}
    del _L3_xcond_all

    def _L3_ffn_setup():
        import jax, jax.numpy as jnp
        import numpy as np
        DIM = 128
        DEPTH = 2
        HEADS = 8
        DIM_HEAD = 64
        WINDOW = 64
        INNER = HEADS * DIM_HEAD
        HID = int(DIM * 4 * 2 / 3)
        B, N = (2, 1024)
        QK_SCALE = 8.0

        def shift_token(t):
            t1, t2 = jnp.split(t, 2, axis=-1)
            t2 = jnp.pad(t2, ((0, 0), (1, 0), (0, 0)))[:, :-1]
            return jnp.concatenate([t1, t2], axis=-1)

        def l2norm(t):
            return t / jnp.clip(jnp.linalg.norm(t, axis=-1, keepdims=True), 1e-12)

        def rotate_half(x):
            x1, x2 = jnp.split(x, 2, axis=-1)
            return jnp.concatenate([-x2, x1], axis=-1)

        def rotary_xpos(q, k):
            n = q.shape[-2]
            half_idx = jnp.arange(0, DIM_HEAD, 2, dtype=jnp.float32)
            inv_freq = 1.0 / 10000.0 ** (half_idx / DIM_HEAD)
            t = jnp.arange(n, dtype=jnp.float32)
            freqs = t[:, None] * inv_freq[None, :]
            freqs = jnp.concatenate([freqs, freqs], axis=-1)
            base = (half_idx + 0.4 * DIM_HEAD) / (1.4 * DIM_HEAD)
            power = (t - n // 2) / float(WINDOW // 2)
            scale = base[None, :] ** power[:, None]
            scale = jnp.concatenate([scale, scale], axis=-1)
            cos, sin = (jnp.cos(freqs), jnp.sin(freqs))
            q = q * cos * scale + rotate_half(q) * sin * scale
            k = k * cos / scale + rotate_half(k) * sin / scale
            return (q, k)

        def local_attention(q, k, v):
            b, h, n, d = q.shape
            w = n // WINDOW
            bq = q.reshape(b, h, w, WINDOW, d) * QK_SCALE
            bk = k.reshape(b, h, w, WINDOW, d)
            bv = v.reshape(b, h, w, WINDOW, d)

            def look_around(t):
                p = jnp.pad(t, ((0, 0), (0, 0), (1, 0), (0, 0), (0, 0)))
                return jnp.concatenate([p[:, :, :w], p[:, :, 1:]], axis=3)
            bk, bv = (look_around(bk), look_around(bv))
            bt = jnp.arange(n).reshape(w, WINDOW)
            btp = jnp.pad(bt, ((1, 0), (0, 0)), constant_values=-1)
            btk = jnp.concatenate([btp[:w], btp[1:]], axis=1)
            sim = jnp.einsum('bhwid,bhwjd->bhwij', bq, bk)
            i = bt[:, :, None]
            j = btk[:, None, :]
            mask = (i < j) | (i > j + WINDOW) | (j == -1)
            sim = jnp.where(mask, -jnp.finfo(sim.dtype).max, sim)
            attn = jax.nn.softmax(sim, axis=-1)
            out = jnp.einsum('bhwij,bhwjd->bhwid', attn, bv)
            return out.reshape(b, h, n, d)

        def _layer(x, wqkv, qs, ksc, wo, lg, lb, w1, b1, w2, b2):
            b, n, _ = x.shape
            h = shift_token(x)
            qkv = h @ wqkv
            q, k, v = jnp.split(qkv, 3, axis=-1)
            to_heads = lambda t: t.reshape(b, n, HEADS, DIM_HEAD).transpose(0, 2, 1, 3)
            q, k, v = (to_heads(q), to_heads(k), to_heads(v))
            q = l2norm(q) * qs
            k = l2norm(k) * ksc
            q, k = rotary_xpos(q, k)
            o = local_attention(q, k, v)
            o = o.transpose(0, 2, 1, 3).reshape(b, n, INNER)
            x = x + o @ wo
            h = shift_token(x)
            mu = h.mean(-1, keepdims=True)
            var = h.var(-1, keepdims=True)
            h = (h - mu) / jnp.sqrt(var + 1e-05) * lg + lb
            h = h @ w1 + b1
            a, g = jnp.split(h, 2, axis=-1)
            h = a * jax.nn.gelu(g, approximate=False)
            x = x + h @ w2 + b2
            return x
        key = jax.random.key(seed)
        ks = jax.random.split(key, 6)
        return {'x': jax.random.normal(ks[0], (B, N, DIM), jnp.float32), 'wqkv': jax.random.normal(ks[1], (DEPTH, DIM, 3 * INNER), jnp.float32) * 0.02, 'q_scale': jnp.ones((DEPTH, DIM_HEAD), jnp.float32), 'k_scale': jnp.ones((DEPTH, DIM_HEAD), jnp.float32), 'wo': jax.random.normal(ks[2], (DEPTH, INNER, DIM), jnp.float32) * 0.02, 'ln_g': jnp.ones((DEPTH, DIM), jnp.float32), 'ln_b': jnp.zeros((DEPTH, DIM), jnp.float32), 'w1': jax.random.normal(ks[3], (DEPTH, DIM, 2 * HID), jnp.float32) * 0.02, 'b1': jnp.zeros((DEPTH, 2 * HID), jnp.float32), 'w2': jax.random.normal(ks[4], (DEPTH, HID, DIM), jnp.float32) * 0.02, 'b2': jnp.zeros((DEPTH, DIM), jnp.float32)}
    _L3_ffn_all = _L3_ffn_setup()
    _L3_ffn_in = {k: v for k, v in _L3_ffn_all.items() if k in ('wqkv', 'q_scale', 'k_scale', 'wo', 'ln_g', 'ln_b', 'w1', 'b1', 'w2', 'b2')}
    del _L3_ffn_all
    return {'x': x, 'ctx_1024': ctx_1024, 'condB_tau': condB_tau, 'fside_BxS2_0': fside_BxS2_0, 'condB_pt': condB_pt, '_lenS2': _lenS2, 'L0_xcond_Wq': _L0_xcond_in['Wq'], 'L0_xcond_bq': _L0_xcond_in['bq'], 'L0_xcond_Wk': _L0_xcond_in['Wk'], 'L0_xcond_bk': _L0_xcond_in['bk'], 'L0_xcond_Wv': _L0_xcond_in['Wv'], 'L0_xcond_bv': _L0_xcond_in['bv'], 'L0_xcond_Wo': _L0_xcond_in['Wo'], 'L0_xcond_bo': _L0_xcond_in['bo'], 'L0_ffn_Wr': _L0_ffn_in['Wr'], 'L0_ffn_W1': _L0_ffn_in['W1'], 'L0_ffn_b1': _L0_ffn_in['b1'], 'L0_ffn_W2': _L0_ffn_in['W2'], 'L0_ffn_b2': _L0_ffn_in['b2'], 'L1_xcond_Wq': _L1_xcond_in['Wq'], 'L1_xcond_bq': _L1_xcond_in['bq'], 'L1_xcond_Wk': _L1_xcond_in['Wk'], 'L1_xcond_bk': _L1_xcond_in['bk'], 'L1_xcond_Wv': _L1_xcond_in['Wv'], 'L1_xcond_bv': _L1_xcond_in['bv'], 'L1_xcond_Wo': _L1_xcond_in['Wo'], 'L1_xcond_bo': _L1_xcond_in['bo'], 'L1_ffn_router_w': _L1_ffn_in['router_w'], 'L1_ffn_gate_up_proj': _L1_ffn_in['gate_up_proj'], 'L1_ffn_down_proj': _L1_ffn_in['down_proj'], 'L1_ffn_shared_gate_w': _L1_ffn_in['shared_gate_w'], 'L1_ffn_shared_up_w': _L1_ffn_in['shared_up_w'], 'L1_ffn_shared_down_w': _L1_ffn_in['shared_down_w'], 'L2_xcond_W_a': _L2_xcond_in['W_a'], 'L2_xcond_W_c': _L2_xcond_in['W_c'], 'L2_ffn_sg': _L2_ffn_in['sg'], 'L2_ffn_su': _L2_ffn_in['su'], 'L2_ffn_sd': _L2_ffn_in['sd'], 'L2_ffn_rg': _L2_ffn_in['rg'], 'L2_ffn_ru': _L2_ffn_in['ru'], 'L2_ffn_rd': _L2_ffn_in['rd'], 'L2_ffn_wr': _L2_ffn_in['wr'], 'L2_ffn_rb': _L2_ffn_in['rb'], 'L3_xcond_Wq': _L3_xcond_in['Wq'], 'L3_xcond_bq': _L3_xcond_in['bq'], 'L3_xcond_Wk': _L3_xcond_in['Wk'], 'L3_xcond_bk': _L3_xcond_in['bk'], 'L3_xcond_Wv': _L3_xcond_in['Wv'], 'L3_xcond_bv': _L3_xcond_in['bv'], 'L3_xcond_Wo': _L3_xcond_in['Wo'], 'L3_xcond_bo': _L3_xcond_in['bo'], 'L3_ffn_wqkv': _L3_ffn_in['wqkv'], 'L3_ffn_q_scale': _L3_ffn_in['q_scale'], 'L3_ffn_k_scale': _L3_ffn_in['k_scale'], 'L3_ffn_wo': _L3_ffn_in['wo'], 'L3_ffn_ln_g': _L3_ffn_in['ln_g'], 'L3_ffn_ln_b': _L3_ffn_in['ln_b'], 'L3_ffn_w1': _L3_ffn_in['w1'], 'L3_ffn_b1': _L3_ffn_in['b1'], 'L3_ffn_w2': _L3_ffn_in['w2'], 'L3_ffn_b2': _L3_ffn_in['b2']}

def reference(x, ctx_1024, condB_tau, fside_BxS2_0, condB_pt, _lenS2, L0_xcond_Wq, L0_xcond_bq, L0_xcond_Wk, L0_xcond_bk, L0_xcond_Wv, L0_xcond_bv, L0_xcond_Wo, L0_xcond_bo, L0_ffn_Wr, L0_ffn_W1, L0_ffn_b1, L0_ffn_W2, L0_ffn_b2, L1_xcond_Wq, L1_xcond_bq, L1_xcond_Wk, L1_xcond_bk, L1_xcond_Wv, L1_xcond_bv, L1_xcond_Wo, L1_xcond_bo, L1_ffn_router_w, L1_ffn_gate_up_proj, L1_ffn_down_proj, L1_ffn_shared_gate_w, L1_ffn_shared_up_w, L1_ffn_shared_down_w, L2_xcond_W_a, L2_xcond_W_c, L2_ffn_sg, L2_ffn_su, L2_ffn_sd, L2_ffn_rg, L2_ffn_ru, L2_ffn_rd, L2_ffn_wr, L2_ffn_rb, L3_xcond_Wq, L3_xcond_bq, L3_xcond_Wk, L3_xcond_bk, L3_xcond_Wv, L3_xcond_bv, L3_xcond_Wo, L3_xcond_bo, L3_ffn_wqkv, L3_ffn_q_scale, L3_ffn_k_scale, L3_ffn_wo, L3_ffn_ln_g, L3_ffn_ln_b, L3_ffn_w1, L3_ffn_b1, L3_ffn_w2, L3_ffn_b2):
    import jax
    import jax.numpy as jnp

    def _L0_xcond_ref(query, key, value, tau, delta, Wq, bq, Wk, bk, Wv, bv, Wo, bo):
        import jax, jax.numpy as jnp
        import numpy as np
        B, S, D, H = (2, 256, 128, 16)
        DK = D // H

        def _split_heads(x):
            b, s, _ = x.shape
            return x.reshape(b, s, H, DK).transpose(0, 2, 1, 3)
        q = _split_heads(query @ Wq.T + bq)
        k = _split_heads(key @ Wk.T + bk)
        v = _split_heads(value @ Wv.T + bv)
        scores = jnp.einsum('bhqd,bhkd->bhqk', q, k)
        scores = scores * tau[:, :, None, None] + delta[:, None, None, :]
        scores = scores / jnp.sqrt(jnp.asarray(DK, scores.dtype))
        p_attn = jax.nn.softmax(scores, axis=-1)
        x = jnp.einsum('bhqk,bhkd->bhqd', p_attn, v)
        x = x.transpose(0, 2, 1, 3).reshape(query.shape[0], -1, H * DK)
        return x @ Wo.T + bo

    def _L0_ffn_ref(x, Wr, W1, b1, W2, b2):
        import jax, jax.numpy as jnp
        import numpy as np
        HID, FFN, NE, TOPK = (128, 512, 8, 2)
        B, S, H = x.shape
        E = Wr.shape[1]
        T = B * S
        xf = x.reshape(T, H)
        logits = xf @ Wr
        probs = jax.nn.softmax(logits, axis=-1)
        topk_p, topk_i = jax.lax.top_k(probs, TOPK)
        topk_p = topk_p / jnp.sum(topk_p, axis=-1, keepdims=True)
        c = jnp.zeros((T, E), dtype=xf.dtype).at[jnp.arange(T)[:, None], topk_i].add(topk_p)

        def expert_step(acc, ew):
            w1, bb1, w2, bb2, ce = ew
            h = jax.nn.gelu(xf @ w1 + bb1, approximate=False)
            y = h @ w2 + bb2
            return (acc + ce[:, None] * y, None)
        out, _ = jax.lax.scan(expert_step, jnp.zeros_like(xf), (W1, b1, W2, b2, c.T))
        return out.reshape(B, S, H)

    def _L1_xcond_ref(q, k, v, tau, delta, Wq, bq, Wk, bk, Wv, bv, Wo, bo):
        import jax, jax.numpy as jnp
        import numpy as np
        D_MODEL = 128
        N_HEADS = 16
        B, L, D = q.shape
        S = k.shape[1]
        H = N_HEADS
        E = D // H
        qh = (q @ Wq.T + bq).reshape(B, L, H, E)
        kh = (k @ Wk.T + bk).reshape(B, S, H, E)
        vh = (v @ Wv.T + bv).reshape(B, S, H, E)
        scale = 1.0 / np.sqrt(E).astype(np.float32)
        scores = jnp.einsum('blhe,bshe->bhls', qh, kh)
        scores = scores * tau[:, None, None, :] + delta[:, None, None, :]
        a = jax.nn.softmax(scale * scores, axis=-1)
        out = jnp.einsum('bhls,bshd->blhd', a, vh).reshape(B, L, D)
        return out @ Wo.T + bo

    def _L1_ffn_ref(hidden_states, router_w, gate_up_proj, down_proj, shared_gate_w, shared_up_w, shared_down_w):
        import jax, jax.numpy as jnp
        import numpy as np
        B, S, H = (2, 256, 128)
        N, F, SF, K = (16, 128, 512, 1)
        b, s, h = hidden_states.shape
        hidden = hidden_states.reshape(-1, h)
        t = hidden.shape[0]
        logits = hidden @ router_w.T
        top_vals, top_idx = jax.lax.top_k(logits, K)
        scores = jnp.full_like(logits, -jnp.inf)
        scores = scores.at[jnp.arange(t)[:, None], top_idx].set(top_vals)
        scores = jax.nn.sigmoid(scores.astype(jnp.float32)).astype(hidden.dtype)
        routed_in = hidden[None, :, :] * scores.T[:, :, None]
        gate_up = jnp.einsum('nth,nhf->ntf', routed_in, gate_up_proj)
        gate, up = jnp.split(gate_up, 2, axis=-1)
        routed_out = jnp.einsum('ntf,nfh->nth', up * jax.nn.silu(gate), down_proj)
        expert_sum = routed_out.sum(axis=0)
        shared = jax.nn.silu(hidden @ shared_gate_w.T) * (hidden @ shared_up_w.T) @ shared_down_w.T
        return (shared + expert_sum).reshape(b, s, h)

    def _L2_xcond_ref(encoder_outputs, decoder_h_t, src_len, p_t, W_a, W_c):
        import jax, jax.numpy as jnp
        import numpy as np
        N, L, H, Q = (64, 258, 128, 32)
        WINDOW = 16.0
        DEV_POW = 128.0
        n, l, h = encoder_outputs.shape
        idx = jnp.arange(l, dtype=jnp.float32)
        src_end = src_len.astype(jnp.float32)
        attn_start = jnp.maximum(p_t - WINDOW, 0.0)
        attn_end = jnp.minimum(p_t + WINDOW, src_end)
        mask = (idx[None, :] < attn_start[:, None]) | (idx[None, :] > attn_end[:, None])
        score = jnp.einsum('nqh,hk,nlk->nql', decoder_h_t, W_a, encoder_outputs)
        score = jnp.where(mask[:, None, :], -1000000000.0, score)
        align = jax.nn.softmax(score, axis=2)
        gauss = jnp.exp(-(idx[None, :] - p_t[:, None]) ** 2 / DEV_POW)
        align = align * gauss[:, None, :]
        context = jnp.einsum('nql,nlh->nqh', align, encoder_outputs)
        cat = jnp.concatenate([context, decoder_h_t], axis=2)
        return jnp.tanh(cat @ W_c.T)

    def _L2_ffn_ref(x, sg, su, sd, rg, ru, rd, wr, rb):
        import jax, jax.numpy as jnp
        import numpy as np
        H, I, E_ROUTED, TOP_K = (128, 352, 7, 2)
        B, S = (4, 256)

        def _expert(h, g, u, d):
            return jnp.einsum('...i,hi->...h', jax.nn.silu(h @ g.T) * (h @ u.T), d)
        shared_out = _expert(x, sg, su, sd)
        logits = x @ wr.T + rb
        probs = jax.nn.softmax(logits, axis=-1)
        scores, idx = jax.lax.top_k(probs, TOP_K)
        scores = scores / scores.sum(axis=-1, keepdims=True)
        w = jnp.sum(scores[..., None] * jax.nn.one_hot(idx, E_ROUTED, dtype=x.dtype), axis=-2)
        out = shared_out
        for e in range(E_ROUTED):
            out = out + w[..., e:e + 1] * _expert(x, rg[e], ru[e], rd[e])
        return out

    def _L3_xcond_ref(query, key, value, tau, delta, Wq, bq, Wk, bk, Wv, bv, Wo, bo):
        import jax, jax.numpy as jnp
        import numpy as np
        B, S, D, H = (2, 256, 128, 16)
        DK = D // H

        def _split_heads(x):
            b, s, _ = x.shape
            return x.reshape(b, s, H, DK).transpose(0, 2, 1, 3)
        q = _split_heads(query @ Wq.T + bq)
        k = _split_heads(key @ Wk.T + bk)
        v = _split_heads(value @ Wv.T + bv)
        scores = jnp.einsum('bhqd,bhkd->bhqk', q, k)
        scores = scores * tau[:, :, None, None] + delta[:, None, None, :]
        scores = scores / jnp.sqrt(jnp.asarray(DK, scores.dtype))
        p_attn = jax.nn.softmax(scores, axis=-1)
        x = jnp.einsum('bhqk,bhkd->bhqd', p_attn, v)
        x = x.transpose(0, 2, 1, 3).reshape(query.shape[0], -1, H * DK)
        return x @ Wo.T + bo

    def _L3_ffn_ref(x, wqkv, q_scale, k_scale, wo, ln_g, ln_b, w1, b1, w2, b2):
        import jax, jax.numpy as jnp
        import numpy as np
        DIM = 128
        DEPTH = 2
        HEADS = 8
        DIM_HEAD = 64
        WINDOW = 64
        INNER = HEADS * DIM_HEAD
        HID = int(DIM * 4 * 2 / 3)
        B, N = (2, 1024)
        QK_SCALE = 8.0

        def shift_token(t):
            t1, t2 = jnp.split(t, 2, axis=-1)
            t2 = jnp.pad(t2, ((0, 0), (1, 0), (0, 0)))[:, :-1]
            return jnp.concatenate([t1, t2], axis=-1)

        def l2norm(t):
            return t / jnp.clip(jnp.linalg.norm(t, axis=-1, keepdims=True), 1e-12)

        def rotate_half(x):
            x1, x2 = jnp.split(x, 2, axis=-1)
            return jnp.concatenate([-x2, x1], axis=-1)

        def rotary_xpos(q, k):
            n = q.shape[-2]
            half_idx = jnp.arange(0, DIM_HEAD, 2, dtype=jnp.float32)
            inv_freq = 1.0 / 10000.0 ** (half_idx / DIM_HEAD)
            t = jnp.arange(n, dtype=jnp.float32)
            freqs = t[:, None] * inv_freq[None, :]
            freqs = jnp.concatenate([freqs, freqs], axis=-1)
            base = (half_idx + 0.4 * DIM_HEAD) / (1.4 * DIM_HEAD)
            power = (t - n // 2) / float(WINDOW // 2)
            scale = base[None, :] ** power[:, None]
            scale = jnp.concatenate([scale, scale], axis=-1)
            cos, sin = (jnp.cos(freqs), jnp.sin(freqs))
            q = q * cos * scale + rotate_half(q) * sin * scale
            k = k * cos / scale + rotate_half(k) * sin / scale
            return (q, k)

        def local_attention(q, k, v):
            b, h, n, d = q.shape
            w = n // WINDOW
            bq = q.reshape(b, h, w, WINDOW, d) * QK_SCALE
            bk = k.reshape(b, h, w, WINDOW, d)
            bv = v.reshape(b, h, w, WINDOW, d)

            def look_around(t):
                p = jnp.pad(t, ((0, 0), (0, 0), (1, 0), (0, 0), (0, 0)))
                return jnp.concatenate([p[:, :, :w], p[:, :, 1:]], axis=3)
            bk, bv = (look_around(bk), look_around(bv))
            bt = jnp.arange(n).reshape(w, WINDOW)
            btp = jnp.pad(bt, ((1, 0), (0, 0)), constant_values=-1)
            btk = jnp.concatenate([btp[:w], btp[1:]], axis=1)
            sim = jnp.einsum('bhwid,bhwjd->bhwij', bq, bk)
            i = bt[:, :, None]
            j = btk[:, None, :]
            mask = (i < j) | (i > j + WINDOW) | (j == -1)
            sim = jnp.where(mask, -jnp.finfo(sim.dtype).max, sim)
            attn = jax.nn.softmax(sim, axis=-1)
            out = jnp.einsum('bhwij,bhwjd->bhwid', attn, bv)
            return out.reshape(b, h, n, d)

        def _layer(x, wqkv, qs, ksc, wo, lg, lb, w1, b1, w2, b2):
            b, n, _ = x.shape
            h = shift_token(x)
            qkv = h @ wqkv
            q, k, v = jnp.split(qkv, 3, axis=-1)
            to_heads = lambda t: t.reshape(b, n, HEADS, DIM_HEAD).transpose(0, 2, 1, 3)
            q, k, v = (to_heads(q), to_heads(k), to_heads(v))
            q = l2norm(q) * qs
            k = l2norm(k) * ksc
            q, k = rotary_xpos(q, k)
            o = local_attention(q, k, v)
            o = o.transpose(0, 2, 1, 3).reshape(b, n, INNER)
            x = x + o @ wo
            h = shift_token(x)
            mu = h.mean(-1, keepdims=True)
            var = h.var(-1, keepdims=True)
            h = (h - mu) / jnp.sqrt(var + 1e-05) * lg + lb
            h = h @ w1 + b1
            a, g = jnp.split(h, 2, axis=-1)
            h = a * jax.nn.gelu(g, approximate=False)
            x = x + h @ w2 + b2
            return x
        for l in range(DEPTH):
            x = _layer(x, wqkv[l], q_scale[l], k_scale[l], wo[l], ln_g[l], ln_b[l], w1[l], b1[l], w2[l], b2[l])
        return x
    x = x + _L0_xcond_ref(_layernorm(x, axis=-1), ctx_1024, ctx_1024, condB_tau[:, None], fside_BxS2_0, L0_xcond_Wq, L0_xcond_bq, L0_xcond_Wk, L0_xcond_bk, L0_xcond_Wv, L0_xcond_bv, L0_xcond_Wo, L0_xcond_bo)
    x = x + _L0_ffn_ref(_layernorm(x, axis=-1), L0_ffn_Wr, L0_ffn_W1, L0_ffn_b1, L0_ffn_W2, L0_ffn_b2)
    x = x + _L1_xcond_ref(_layernorm(x, axis=-1), ctx_1024, ctx_1024, condB_tau[:, None], fside_BxS2_0, L1_xcond_Wq, L1_xcond_bq, L1_xcond_Wk, L1_xcond_bk, L1_xcond_Wv, L1_xcond_bv, L1_xcond_Wo, L1_xcond_bo)
    x = x + _L1_ffn_ref(_layernorm(x, axis=-1), L1_ffn_router_w, L1_ffn_gate_up_proj, L1_ffn_down_proj, L1_ffn_shared_gate_w, L1_ffn_shared_up_w, L1_ffn_shared_down_w)
    x = x + _L2_xcond_ref(ctx_1024, _layernorm(x, axis=-1), _lenS2, condB_pt, L2_xcond_W_a, L2_xcond_W_c)
    x = x + _L2_ffn_ref(_layernorm(x, axis=-1), L2_ffn_sg, L2_ffn_su, L2_ffn_sd, L2_ffn_rg, L2_ffn_ru, L2_ffn_rd, L2_ffn_wr, L2_ffn_rb)
    x = x + _L3_xcond_ref(_layernorm(x, axis=-1), ctx_1024, ctx_1024, condB_tau[:, None], fside_BxS2_0, L3_xcond_Wq, L3_xcond_bq, L3_xcond_Wk, L3_xcond_bk, L3_xcond_Wv, L3_xcond_bv, L3_xcond_Wo, L3_xcond_bo)
    x = x + _L3_ffn_ref(_layernorm(x, axis=-1), L3_ffn_wqkv, L3_ffn_q_scale, L3_ffn_k_scale, L3_ffn_wo, L3_ffn_ln_g, L3_ffn_ln_b, L3_ffn_w1, L3_ffn_b1, L3_ffn_w2, L3_ffn_b2)
    return x

_drawn_inputs = setup_inputs


def setup_inputs(seed=0):
    import zlib

    import numpy as np

    out = dict(_drawn_inputs(seed))
    spreads = {'L0_ffn_b1': (0.0, 0.1),
     'L0_ffn_b2': (0.0, 0.1),
     'L1_xcond_bq': (0.0, 0.8),
     'L1_xcond_bk': (0.0, 2.0),
     'L1_xcond_bv': (0.0, 0.1),
     'L1_xcond_bo': (0.0, 0.1),
     'L2_ffn_rb': (0.0, 0.8),
     'L3_ffn_q_scale': (1.0, 0.6),
     'L3_ffn_k_scale': (1.0, 0.6),
     'L3_ffn_ln_g': (1.0, 0.6),
     'L3_ffn_ln_b': (0.0, 0.8),
     'L3_ffn_b1': (0.0, 0.8),
     'L3_ffn_b2': (0.0, 0.8)}
    factors = {'condB_pt': 8.0,
     'L0_xcond_bq': 7.747,
     'L0_xcond_bk': 64.0,
     'L0_xcond_bo': 2.76,
     'L1_ffn_router_w': 8.0,
     'L1_ffn_gate_up_proj': 8.0,
     'L1_ffn_down_proj': 8.0,
     'L1_ffn_shared_gate_w': 7.174,
     'L1_ffn_shared_up_w': 7.165,
     'L1_ffn_shared_down_w': 7.144,
     'L2_ffn_sg': 8.0,
     'L2_ffn_su': 8.0,
     'L2_ffn_sd': 8.0,
     'L2_ffn_rg': 8.0,
     'L2_ffn_ru': 8.0,
     'L2_ffn_rd': 8.0,
     'L2_ffn_wr': 8.0,
     'L3_xcond_bq': 64.0,
     'L3_xcond_bk': 64.0,
     'L3_xcond_bv': 40.821,
     'L3_xcond_bo': 56.076,
     'L3_ffn_w1': 8.0,
     'L3_ffn_w2': 8.0,
     'L3_xcond_Wq': 4.25,
     'L3_xcond_Wk': 4.401}
    for name, (base, spread) in spreads.items():
        noise = np.random.default_rng([zlib.crc32(name.encode()), seed]).standard_normal(out[name].shape)
        drawn = base * np.exp(spread * noise) if base else spread * noise
        out[name] = jnp.asarray(drawn.astype(out[name].dtype))
    for name, factor in factors.items():
        out[name] = (out[name] * factor).astype(out[name].dtype)
    return out
```

```python
from contextlib import ExitStack

import numpy as np
import concourse.bass as bass
from concourse import mybir

F32 = mybir.dt.float32
F32R = mybir.dt.float32r
BF16 = mybir.dt.bfloat16
U32 = mybir.dt.uint32
I32 = mybir.dt.int32
ACT = mybir.ActivationFunctionType
ALU = mybir.AluOpType
AX = mybir.AxisListType

P = 128
B = 2
S = 512
T = B * S
NT = T // P
HT = NT // B
L = 77
EPS = 1e-5

H = 16
DK = P // H
G = 4
HG = H // G
GW = HG * L
NC = -(-H * L // P)
VW = H * (DK + 1)
VG = B * NC // 4

RING = 3
WMAX = 1088
UB = 4

LH = 8
LD = 64
INNER = LH * LD
WIN = 64
QK_SCALE = 8.0
DEPTH = 2
CH3 = 3
L3W = 3 * INNER + 4 * P + 2 * CH3 * P + CH3 * P

C_ID = 0
C_KM = C_ID + P
C_DM = C_KM + HG
C_VM = C_DM + 2
C_IO = C_VM + B * NC * H
C_SH = C_IO + L + 1
C_SE = C_SH + P
C_MS = C_SE + P
NCONST = C_MS + P + WIN

V_BQ = 0
V_BK = V_BQ + 3 * G
V_BV = V_BK + 3 * G
V_B1 = V_BV + 3
V_B2 = V_B1 + 32
V_LG = V_B2 + 8
V_LB = V_LG + DEPTH
V_B1A = V_LB + DEPTH
V_B1G = V_B1A + DEPTH * CH3
V_B23 = V_B1G + DEPTH * CH3
V_TAU = V_B23 + DEPTH
V_DEL = V_TAU + B * L
V_PT = V_DEL + B * L
V_RB = V_PT + B
V_QS = V_RB + 8
NVEC = V_QS + DEPTH * 4 * LD
NROW = 3 * P

MOE = ("gelu", "top1", "top2")


def moe_plan():
    plans = []
    first = 0
    for kind, experts, chunks in (("gelu", 8, 4), ("top1", 4 + 16, 1), ("top2", 8, 3)):
        units = [(e, b, c) for e in range(experts) for b in range(B) for c in range(chunks)]
        plans.append(dict(kind=kind, experts=experts, chunks=chunks, first=first, units=units))
        first += experts
    return plans, first


class Count:

    def __init__(self, engine, semaphore):
        self.engine, self.semaphore, self.value = engine, semaphore, 0

    def done(self, instruction):
        self.value += 1
        instruction.then_inc(self.semaphore, 1)

    def wait(self):
        self.engine.wait_ge(self.semaphore, self.value)


def build(nc, d, out, stages):
    plans, n_ring = moe_plan()
    ctx = ExitStack()
    with ctx:
        def sb(name, shape, dt=F32, where=None):
            return (where or ctx).enter_context(nc.sbuf_tensor(name, shape, dt))

        def sem(name):
            return ctx.enter_context(nc.semaphore(name))

        ps = ctx.enter_context(nc.psum_tensor("ps", [P, 8, S], F32))
        bank = [ps[:, i, :] for i in range(8)]

        x = sb("x", [P, NT, P])
        xn = sb("xn", [P, NT, P])
        x_hi = sb("x_hi", [P, T], F32R)
        x_lo = sb("x_lo", [P, T], F32R)
        cst = sb("cst", [P, NCONST])
        vec = sb("vec", [P, NVEC])
        ident = cst[:, C_ID:C_ID + P]
        stats = sb("stats", [P, NT, 12])
        mv = sb("mv", [P, NT, 2])
        ve = sb("ve", [P, NT])
        rstd = sb("rstd", [P, NT])
        mhalf = sb("mhalf", [P, 16])
        gate = sb("gate", [P, 3, S])
        prod = sb("prod", [P, 3, S])
        a_hi = sb("a_hi", [P, UB, S], F32R)
        a_lo = sb("a_lo", [P, UB, S], F32R)
        acc = sb("acc", [P, T])
        ytmp = sb("ytmp", [P, 2, S])

        early = ExitStack()
        rows = sb("rows", [1, NROW], F32, early)
        ones = sb("ones", [1, P], F32, early)
        aw = sb("aw", [P, 3, 1024], F32, early)
        ctxT = sb("ctxT", [P, B * L], F32, early)
        ctx_rep = sb("ctx_rep", [P, B, NC * P], F32, early)
        wq_hi = sb("wq_hi", [P, G * 96], F32R, early)
        wq_lo = sb("wq_lo", [P, G * 96], F32R, early)
        wo_hi = sb("wo_hi", [P, P], F32R, early)
        wo_lo = sb("wo_lo", [P, P], F32R, early)
        tau_s = sb("tau_s", [P, B * L], F32, early)
        del_f = sb("del_f", [P, B * L], F32, early)
        del_h = sb("del_h", [P, B * L], F32R, early)
        del_l = sb("del_l", [P, B * L], F32, early)
        del_x = sb("del_x", [P, B * L], F32, early)
        k_f = sb("k_f", [96, G, B * L], F32, early)
        k_x = sb("k_x", [96, G, B * L], F32R, early)
        k_st = sb("k_st", [P, B, G, GW], F32R, early)
        v_bd = sb("v_bd", [P, B * NC, H, DK + 1], F32, early)
        brow = sb("brow", [1, P], F32, early)
        rw_hi = sb("rw_hi", [P, 32], F32R, early)
        rw_lo = sb("rw_lo", [P, 32], F32R, early)
        rw = sb("rw", [P, 32], F32, early)
        w_raw = sb("w_raw", [P, RING, WMAX], F32, early)
        w_hi = sb("w_hi", [P, RING, WMAX], F32R, early)
        w_lo = sb("w_lo", [P, RING, WMAX], F32R, early)
        l2w = sb("l2w", [P, 3 * P], F32, early)
        ctx_n = sb("ctx_n", [L, B, P], F32, early)
        slen = sb("slen", [P, B], I32, early)
        l2s = sb("l2s", [P, 8], F32, early)
        valid = sb("valid", [P, B, L], F32, early)
        gauss = sb("gauss", [P, B, L], F32, early)
        neg = sb("neg", [P, B, L], F32, early)

        att = ExitStack()
        qs = sb("qs", [P, G, T], F32R, att)
        e_sb = sb("e_sb", [P, 2, NC * P], F32, att)
        pT = sb("pT", [P, 2, NC * P], F32, att)
        mx = sb("mx", [P, 2, H], F32, att)
        rsum = sb("rsum", [P, 2, H], F32, att)
        on = sb("on", [P, NT, P], F32, att)
        oT_hi = sb("oT_hi", [P, S], F32R, att)
        oT_lo = sb("oT_lo", [P, S], F32R, att)
        att.close()
        l2x = ExitStack()
        wc_hi = sb("wc_hi", [P, 2 * P], F32R, l2x)
        wc_lo = sb("wc_lo", [P, 2 * P], F32R, l2x)
        m_hi = sb("m_hi", [P, B, 78], F32R, l2x)
        m_lo = sb("m_lo", [P, B, 78], F32R, l2x)
        sc = sb("sc", [P, NT, L], F32, l2x)
        sc2 = sb("sc2", [P, NT, L], F32, l2x)
        l2m = sb("l2m", [P, 3, NT], F32, l2x)
        alT = sb("alT", [L, B, S], F32, l2x)
        c_hi = sb("c_hi", [P, B, S], F32R, l2x)
        c_lo = sb("c_lo", [P, B, S], F32R, l2x)
        th = sb("th", [P, B, S], F32, l2x)
        l2x.close()
        moe = ExitStack()
        lg = sb("lg", [P, NT, 16], F32, moe)
        pr = sb("pr", [P, NT, 16], F32, moe)
        m8 = sb("m8", [P, NT, 8], F32, moe)
        i8 = sb("i8", [P, NT, 8], U32, moe)
        i8f = sb("i8f", [P, NT, 8], F32, moe)
        sel = sb("sel", [P, 2, NT, 16], F32, moe)
        cw = sb("cw", [P, NT, 16], F32, moe)
        sm = sb("sm", [P, 4, NT], F32, moe)
        cT = sb("cT", [16, T], F32, moe)
        crow = sb("crow", [P, 4, T], F32, moe)
        cB = sb("cB", [P, 2, T], F32, moe)
        moe.close()
        early.close()

        late = ExitStack()
        w3_raw = sb("w3_raw", [P, L3W], F32, late)
        w3_hi = sb("w3_hi", [P, L3W], F32R, late)
        w3_lo = sb("w3_lo", [P, L3W], F32R, late)
        ident_b = sb("ident_b", [P, P], BF16, late)
        mask = sb("mask", [P, P + WIN], BF16, late)
        kept = sb("kept", [P, NT, P], F32, late)
        rope_raw = sb("rope_raw", [P, 4, HT, LD], F32, late)
        rope = sb("rope", [P, 4, HT, LD], F32, late)
        kT = sb("kT", [P, 4, T], F32, late)
        qT = sb("qT", [P, 2, LH, P], F32, late)
        v_all = sb("v_all", [P, NT, INNER], F32, late)
        sq = sb("sq", [P, 2, INNER], F32, late)
        r1 = sb("r1", [P, 2, INNER], F32, late)
        r2 = sb("r2", [P, 2, INNER], F32, late)
        qk = sb("qk", [P, 2, 2, INNER], F32, late)
        ssq = sb("ssq", [P, 2, 2 * LH], F32, late)
        rn = sb("rn", [P, 2, 2 * LH], F32, late)
        rq = sb("rq", [P, 2, 2, LH], F32, late)
        mx3 = sb("mx3", [P, 2, LH], F32, late)
        nb3 = sb("nb3", [P, 2, LH], F32, late)
        sum3 = sb("sum3", [P, 2, LH], F32, late)
        rs3 = sb("rs3", [P, 2, LH], F32, late)
        p3 = sb("p3", [P, 2, 2, 2 * P], F32, late)
        pT3 = sb("pT3", [P, 2, 4, P], F32, late)
        on3 = sb("on3", [P, NT, INNER], F32, late)
        o_hi = sb("o_hi", [P, 2, INNER], F32R, late)
        o_lo = sb("o_lo", [P, 2, INNER], F32R, late)
        late.close()

        s = {n: sem(n) for n in (
            "ld_cst", "ld_x", "ld_ctx", "ld_aw", "ld_aw_more", "ld_rw", "ld_l2", "ld_w0", "ld_w1", "ld_w2", "ld_row", "ld_w3", "ld_rope",
            "stored",
            "dve_step", "act_step", "pool_step",
            "pool_set", "gauss_d2", "gauss_ready", "rw_ready",
            "ve_ready", "rstd_ready", "xn_ready", "xT_ps", "xhi_ready", "xlo_ready",
            "k_ps", "k_ready", "v_ps", "v_ready", "brow_ps", "brow_ready", "wsplit",
            "q_ps", "q_hi", "q_lo", "score_ps", "sub_done", "exp_done", "pt_ps", "pt_ready", "pv_ps", "on_ready",
            "oT_ps", "oT_hi_ready", "oT_lo_ready", "ao_ps", "x_added",
            "m_ps", "m_ready", "s_ps", "s_sub", "s_exp", "al_ready", "al_ps", "alT_ready", "c_ps", "chi_ready",
            "clo_ready", "t_ps", "tanh_ready",
            "lg_ps", "rt_sub", "rt_exp", "cw_ready", "cT_ps", "cT_ready", "cb_ready",
            "whi_ready", "wlo_ready", "hid_ps", "scaled", "gate_ready", "prod_ready", "ahi_ready", "alo_ready",
            "out_ps", "y_taken", "acc_added", "yT_ps",
            "w3hi_ready", "w3lo_ready", "rope_ready", "q3_ps", "k3_ps", "v3_ps", "sq_ready", "v3_ready", "rot_ready", "kr_ready",
            "ssq_ready", "qk_ready", "qkT_ps", "qkT_ready", "sim_ps", "nb_ready", "p3_ready",
            "pT3_ps", "pT3_even", "pT3_odd", "pv3_ps", "on3_ready", "o3_ps", "ohi_ready", "olo_ready", "o3_out", "x3_added",
            "shift_ps", "hF_ready", "kept", "kept_added",
        )}
        s_w = [s["ld_w0"], s["ld_w1"], s["ld_w2"]]


        ATT_HEAD = (0, 2, 6)
        MOE_HEAD = (1, 3, 5)
        L2_HEAD = 4
        order = [("att", 0), ("moe", 0), ("att", 1), ("moe", 1), ("l2x", 0), ("moe", 2), ("att", 2),
                 ("loc", 0), ("loc", 1)][:stages]
        n_ring = sum(p["experts"] for m, p in enumerate(plans) if ("moe", m) in order)
        WIDTH = (1024, 384, 1088)
        before = {st: 2 * n for n, st in enumerate(order)}
        n_units = [len(p["units"]) for p in plans]
        unit_base = [sum(n_units[:m]) for m in range(3)] + [sum(n_units), sum(n_units) + B * CH3]
        prod_base = [0, 0, n_units[1], n_units[1] + n_units[2], n_units[1] + n_units[2] + B * CH3]
        group_base = [0, 16, 20, 36, 38]
        cb_base = [0, 8, 24]
        units_through = {}
        for m, p in enumerate(plans):
            for e in range(p["experts"]):
                units_through[p["first"] + e] = unit_base[m] + (e + 1) * B * p["chunks"]
        LAG = {"gelu": 2, "top1": 3, "top2": 2, "geglu": 2}

        def half(t, b):
            return t[:, b * S:(b + 1) * S]

        def tiles(b):
            return range(HT * b, HT * (b + 1))

        def first_of_group(kind, e, c):
            return c == 0 and (kind != "top1" or e in (0, 4))

        def last_of_group(kind, chunks, e, c):
            return c == chunks - 1 and (kind != "top1" or e in (3, 19))

        def group_of(kind, e, b):
            if kind == "top1":
                return (0 if e < 4 else 2) + b
            return 2 * e + b

        def rows_of(kind, c):
            return 96 if kind == "top2" and c == 2 else P

        def hid_cols(kind, c, up):
            if kind == "gelu":
                return c * P
            if kind == "top1":
                return up * P
            return up * 352 + c * P

        def out_cols(kind, c):
            return {"gelu": 512, "top1": 256, "top2": 704}[kind] + c * P

        block = ctx.enter_context(nc.Block())

        @block.sync
        def _(sp):
            sp.dma_start(cst[:, :], d["consts"]).then_inc(s["ld_cst"], 16)
            sp.dma_start(x[:, :, :], d["x"]).then_inc(s["ld_x"], 16)
            sp.dma_start(vec[:, :], d["vec"]).then_inc(s["ld_cst"], 16)
            sp.dma_start(ctxT[:, :], d["ctxT"]).then_inc(s["ld_ctx"], 16)
            sp.dma_start(aw[:, 0, :], d["aw"][:, 0, :]).then_inc(s["ld_aw"], 16)
            sp.dma_start(ctx_rep[:, :, :], d["ctx_rep"]).then_inc(s["ld_ctx"], 16)
            sp.dma_start(rows[:, :], d["rows"]).then_inc(s["ld_ctx"], 16)
            sp.dma_start(rw[:, :], d["rw"]).then_inc(s["ld_rw"], 16)
            sp.dma_start(aw[:, 1:3, :], d["aw"][:, 1:3, :]).then_inc(s["ld_aw_more"], 16)
            sp.dma_start(l2w[:, :], d["l2w"]).then_inc(s["ld_l2"], 16)
            sp.dma_start(ctx_n[:, :, :], d["ctx_n"]).then_inc(s["ld_l2"], 16)
            sp.dma_start(slen[:, :], d["slen"]).then_inc(s["ld_l2"], 16)
            for n in range(n_ring):
                if n >= RING:
                    sp.wait_ge(s["wlo_ready"], n - RING + 1)
                m = 0 if n < 8 else 1 if n < 28 else 2
                width = WIDTH[m]
                src = d["w" + str(m)][n - plans[m]["first"]]
                sp.dma_start(w_raw[:, n % RING, 0:width], src).then_inc(s_w[n % RING], 16)
            for layer in range(DEPTH):
                if ("loc", layer) not in order:
                    continue
                if layer == 0:
                    sp.wait_ge(s["x_added"], before[("loc", 0)])
                    sp.dma_start(rope_raw[:, :, :, :], d["rope"]).then_inc(s["ld_rope"], 16)
                else:
                    sp.wait_ge(s["w3lo_ready"], 2)
                sp.dma_start(w3_raw[:, 0:3 * INNER], d["w3"][layer, :, 0:3 * INNER]).then_inc(s["ld_w3"], 16)
                sp.dma_start(w3_raw[:, 3 * INNER:L3W], d["w3"][layer, :, 3 * INNER:L3W]).then_inc(s["ld_w3"], 16)
            for b in range(B):
                sp.wait_ge(s["x_added"], 2 * len(order) - B + b + 1)
                sp.dma_start(out[:, 4 * b:4 * b + 4, :], x[:, 4 * b:4 * b + 4, :]).then_inc(s["stored"], 16)
            sp.wait_ge(s["stored"], 16 * B)

        @block.tensor
        def _(pe):
            def three(dst, a_h, a_l, b_h, b_l, start=True, stop=True):
                pe.matmul(dst, a_h, b_h, start=start, stop=False)
                pe.matmul(dst, a_l, b_h, start=False, stop=False)
                return pe.matmul(dst, a_h, b_l, start=False, stop=stop)

            def head(ln, jx):
                for b in range(B):
                    pe.wait_ge(s["xn_ready"], 2 * ln + b + 1)
                    for k, t in enumerate(tiles(b)):
                        last = pe.transpose(bank[6 + b][:, k * P:(k + 1) * P], xn[:, t, :], ident)
                    last.then_inc(s["xT_ps"], 1)

            def attention(i):
                j = ATT_HEAD[i]
                if i == 0:
                    pe.wait_ge(s["ld_cst"], 32)
                    pe.wait_ge(s["ld_ctx"], 48)
                    pe.wait_ge(s["pool_set"], 2)
                else:
                    pe.wait_ge(s["x_added"], before[("att", i)])
                pe.wait_ge(s["ld_aw" if i == 0 else "ld_aw_more"], 16)
                for g in range(G):
                    last = pe.matmul(bank[4 + g // 3][0:96, (g % 3) * B * L:(g % 3 + 1) * B * L],
                                     aw[:, i, 384 + 96 * g:480 + 96 * g], ctxT[:, :], start=True, stop=True)
                last.then_inc(s["k_ps"], 1)
                for vg in range(VG):
                    bk = (6, 7, 4, 5, 6)[vg]
                    if vg in (2, 3):
                        pe.wait_ge(s["k_ready"], i + 1)
                    if vg == 4:
                        pe.wait_ge(s["v_ready"], VG * i + 1)
                    for q in range(4):
                        c = 4 * vg + q
                        last = pe.matmul(bank[bk][:, q * P:(q + 1) * P],
                                         ctx_rep[:, c // NC, (c % NC) * P:(c % NC + 1) * P],
                                         aw[:, i, 768:896], start=True, stop=True)
                    last.then_inc(s["v_ps"], 1)
                pe.wait_ge(s["v_ready"], VG * i + 2)
                pe.matmul(bank[7][0:1, 0:P], vec[:, V_BV + i:V_BV + i + 1], aw[:, i, 896:1024],
                          start=True, stop=True).then_inc(s["brow_ps"], 1)
                head(j, j)
                pe.wait_ge(s["wsplit"], i + 1)
                for b in range(B):
                    pe.wait_ge(s["xlo_ready"], 2 * j + b + 1)
                    for g in range(G):
                        if b == 1:
                            pe.wait_ge(s["q_lo"], 8 * i + g + 1)
                        w = slice(96 * g, 96 * g + 96)
                        three(bank[g][0:96, :], wq_hi[:, w], wq_lo[:, w], half(x_hi, b), half(x_lo, b))\
                            .then_inc(s["q_ps"], 1)

                def scores(t):
                    pe.wait_ge(s["q_lo"], 8 * i + (8 if t >= HT or t == 0 else 4))
                    if t == 0:
                        pe.wait_ge(s["k_ready"], i + 1)
                        pe.wait_ge(s["pool_set"], 3 + i)
                    else:
                        pe.wait_ge(s["sub_done"], NT * i + t)
                    for g in range(G):
                        last = pe.matmul(bank[g][:, 0:GW], qs[:, g, t * P:(t + 1) * P], k_st[:, t // HT, g, :],
                                         start=True, stop=True)
                    last.then_inc(s["score_ps"], 1)

                def turn(t):
                    pe.wait_ge(s["exp_done"], NT * i + t + 1)
                    for k in range(3):
                        n = 3 * (NT * i + t) + k
                        if 3 * t + k >= 2:
                            pe.wait_ge(s["pt_ready"], n - 1)
                        for c in range(4 * k, min(4 * k + 4, NC)):
                            last = pe.transpose(bank[4 + n % 2][:, (c % 4) * P:(c % 4 + 1) * P],
                                                e_sb[:, t % 2, c * P:(c + 1) * P], ident)
                        last.then_inc(s["pt_ps"], 1)

                def values(t):
                    pe.wait_ge(s["pt_ready"], 3 * (NT * i + t) + 3)
                    if t == 0:
                        pe.wait_ge(s["v_ready"], VG * (i + 1))
                    if t > 0:
                        pe.wait_ge(s["on_ready"], NT * i + t)
                    for c in range(NC):
                        last = pe.matmul(bank[7][:, 0:VW], pT[:, t % 2, c * P:(c + 1) * P],
                                         v_bd[:, (t // HT) * NC + c, :, :].rearrange("p h d -> p (h d)"),
                                         start=(c == 0), stop=(c == NC - 1))
                    last.then_inc(s["pv_ps"], 1)

                def turn_out(b):
                    pe.wait_ge(s["on_ready"], NT * i + HT * b + HT)
                    if b == 1:
                        pe.wait_ge(s["x_added"], before[("att", i)] + 1)
                    for k, t in enumerate(tiles(b)):
                        last = pe.transpose(bank[6][:, k * P:(k + 1) * P], on[:, t, :], ident)
                    last.then_inc(s["oT_ps"], 1)

                def project(b):
                    pe.wait_ge(s["oT_lo_ready"], 2 * i + b + 1)
                    pe.wait_ge(s["brow_ready"], i + 1)
                    for k in range(HT):
                        c = slice(k * P, (k + 1) * P)
                        pe.matmul(bank[6][:, c], ones[:, :], brow[:, :], start=True, stop=False)
                        last = three(bank[6][:, c], oT_hi[:, c], oT_lo[:, c], wo_hi[:, :], wo_lo[:, :], start=False)
                    last.then_inc(s["ao_ps"], 1)

                scores(0)
                for t in range(NT):
                    if t + 1 < NT:
                        scores(t + 1)
                    turn(t)
                    values(t)
                    if t == 4:
                        turn_out(0)
                    if t == 5:
                        project(0)
                turn_out(1)
                project(1)

            def feed_forward(kind, m, jx, units, chunks, hid_w, out_w):
                lag, ub, gb = LAG[kind], unit_base[m], group_base[m]
                for n in range(len(units) + lag):
                    if n < len(units):
                        e, b, c = units[n]
                        r = rows_of(kind, c)
                        if kind == "geglu":
                            pe.wait_ge(s["xlo_ready"], 2 * jx + b + 1)
                            pe.wait_ge(s["w3lo_ready"], 2 * (m - 3) + 2)
                            if n == 2:
                                pe.wait_ge(s["hF_ready"], 2 * (m - 3) + 2)
                        else:
                            pe.wait_ge(s["wlo_ready"], plans[m]["first"] + e + 1)
                        if n >= 3 and kind == "gelu":
                            pe.wait_ge(s["gate_ready"], ub + n - 2)
                        elif n >= 3:
                            pe.wait_ge(s["prod_ready"], prod_base[m] + n - 2)
                        for up in range(1 if kind == "gelu" else 2):
                            h, lo = hid_w(e, c, up)
                            last = three(bank[2 + 2 * (n % 3) + up][0:r, :], h, lo, half(x_hi, b), half(x_lo, b))
                        last.then_inc(s["hid_ps"], 1)
                    if n == 2 and kind != "geglu":
                        pe.wait_ge(s["cw_ready"], m + 1)
                        ne = 16 if kind == "top1" else 8
                        for hb in range(B):
                            for k, t in enumerate(tiles(hb)):
                                last = pe.transpose(bank[hb][0:ne, k * P:(k + 1) * P], cw[:, t, 0:ne], ident)
                            last.then_inc(s["cT_ps"], 1)
                    if n >= lag:
                        u = n - lag
                        e, b, c = units[u]
                        r = rows_of(kind, c)
                        pe.wait_ge(s["alo_ready"], ub + u + 1)
                        first = first_of_group(kind, e, c)
                        if first:
                            before_it = group_of(kind, e, b) - 2
                            if before_it >= 0 and kind != "geglu":
                                pe.wait_ge(s["y_taken"], gb + before_it + 1)
                            elif kind != "geglu":
                                pe.wait_ge(s["cT_ready"], 2 * m + 2)
                        h, lo = out_w(e, c, r)
                        k = (ub + u) % UB
                        three(bank[b], h, lo, a_hi[0:r, k, :], a_lo[0:r, k, :], start=first,
                              stop=last_of_group(kind, chunks, e, c)).then_inc(s["out_ps"], 1)

            def routed(m):
                p = plans[m]
                kind, jx = p["kind"], MOE_HEAD[m]
                head(jx, jx)
                ne, r0 = ((8, 0), (16, 8), (8, 24))[m]
                pe.wait_ge(s["xlo_ready"], 2 * jx + 2)
                pe.wait_ge(s["rw_ready"], 1)
                for t in range(NT):
                    c = slice(t * P, (t + 1) * P)
                    last = three(bank[0][:, t * ne:(t + 1) * ne], x_hi[:, c], x_lo[:, c],
                                 rw_hi[:, r0:r0 + ne], rw_lo[:, r0:r0 + ne])
                last.then_inc(s["lg_ps"], 1)

                def hid_w(e, c, up):
                    slot, c0 = (p["first"] + e) % RING, hid_cols(kind, c, up)
                    w = slice(c0, c0 + rows_of(kind, c))
                    return w_hi[:, slot, w], w_lo[:, slot, w]

                def out_w(e, c, r):
                    slot, c0 = (p["first"] + e) % RING, out_cols(kind, c)
                    return w_hi[0:r, slot, c0:c0 + P], w_lo[0:r, slot, c0:c0 + P]

                feed_forward(kind, m, jx, p["units"], p["chunks"], hid_w, out_w)
                for b in range(B):
                    if kind == "top1":
                        pe.wait_ge(s["y_taken"], group_base[m] + 3 + b)
                        pe.wait_ge(s["prod_ready"], prod_base[m] + n_units[m])
                    else:
                        pe.wait_ge(s["acc_added"], 14 * (m // 2) + 13 + b)
                    for k in range(HT):
                        last = pe.transpose(bank[2 + b][:, k * P:(k + 1) * P], acc[:, (HT * b + k) * P:(HT * b + k + 1) * P], ident)
                    if kind == "top1":
                        for k in range(HT):
                            last = pe.transpose(bank[4 + b][:, k * P:(k + 1) * P], ytmp[:, b, k * P:(k + 1) * P], ident)
                    last.then_inc(s["yT_ps"], 1)

            def l2_attention():
                j = L2_HEAD
                pe.wait_ge(s["ld_l2"], 48)
                pe.wait_ge(s["x_added"], before[("l2x", 0)])
                pe.matmul(bank[4][:, 0:B * L], l2w[:, 0:P], ctxT[:, :], start=True, stop=True).then_inc(s["m_ps"], 1)
                head(j, j)
                pe.wait_ge(s["m_ready"], 1)
                for b in range(B):
                    pe.wait_ge(s["xlo_ready"], 2 * j + b + 1)
                    for k, t in enumerate(tiles(b)):
                        c = slice(t * P, (t + 1) * P)
                        last = three(bank[b][:, k * 78:(k + 1) * 78], x_hi[:, c], x_lo[:, c], m_hi[:, b, :], m_lo[:, b, :])
                    last.then_inc(s["s_ps"], 1)
                for b in range(B):
                    pe.wait_ge(s["al_ready"], b + 1)
                    for k, t in enumerate(tiles(b)):
                        last = pe.transpose(bank[2 + b][0:L, k * P:(k + 1) * P], sc2[:, t, :], ident)
                    last.then_inc(s["al_ps"], 1)
                    pe.wait_ge(s["alT_ready"], b + 1)
                    pe.matmul(bank[4 + b], ctx_n[:, b, :], alT[:, b, :], start=True, stop=True).then_inc(s["c_ps"], 1)
                for b in range(B):
                    pe.wait_ge(s["clo_ready"], b + 1)
                    for k, t in enumerate(tiles(b)):
                        c, c0 = slice(t * P, (t + 1) * P), slice(k * P, (k + 1) * P)
                        three(bank[6 + b][:, c0], c_hi[:, b, c0], c_lo[:, b, c0], wc_hi[:, 0:P], wc_lo[:, 0:P], stop=False)
                        last = three(bank[6 + b][:, c0], x_hi[:, c], x_lo[:, c], wc_hi[:, P:2 * P], wc_lo[:, P:2 * P],
                                     start=False)
                    last.then_inc(s["t_ps"], 1)

            def local(layer):
                m = 3 + layer
                ja, jf = 7 + 2 * layer, 8 + 2 * layer
                pe.wait_ge(s["x_added"], before[("loc", layer)])
                for b in range(B):
                    if layer == 0:
                        pe.wait_ge(s["xn_ready"], 2 * 7 + b + 1)
                    for k, t in enumerate(tiles(b)):
                        last = pe.transpose(bank[6 + b][:, k * P:(k + 1) * P], x[:, t, :], ident)
                    last.then_inc(s["xT_ps"], 1)
                n0 = NT * layer

                def proj(t, what):
                    c = slice(t * P, (t + 1) * P)
                    w = slice(what * INNER, (what + 1) * INNER)
                    if what == 0:
                        pe.wait_ge(s["xlo_ready"], 2 * ja + (2 if t >= HT or t == 0 else 1))
                        pe.wait_ge(s["w3lo_ready"], 2 * layer + 1)
                        if t > 0:
                            pe.wait_ge(s["v3_ready"], n0 + t)
                    if what == 1 and t > 0:
                        pe.wait_ge(s["kr_ready"], n0 + t)
                    if what == 2:
                        pe.wait_ge(s["rot_ready"], n0 + t + 1)
                    three(bank[7 if what == 1 else 6], x_hi[:, c], x_lo[:, c], w3_hi[:, w], w3_lo[:, w])\
                        .then_inc(s[("q3_ps", "k3_ps", "v3_ps")[what]], 1)

                def turn_qk(t, what):
                    if what == 0:
                        pe.wait_ge(s["qk_ready"], n0 + t + 1)
                    if 2 * t + what > 0:
                        pe.wait_ge(s["qkT_ready"], 2 * (n0 + t) + what)
                    for c in range(4):
                        last = pe.transpose(bank[5][:, c * P:(c + 1) * P], qk[:, t % 2, what, c * P:(c + 1) * P], ident)
                    last.then_inc(s["qkT_ps"], 1)

                def sim(q):
                    t, pair = divmod(q, 4)
                    w = P + (WIN if t % HT else 0)
                    g = 4 * n0 + q
                    if pair == 0:
                        pe.wait_ge(s["qkT_ready"], 2 * (n0 + t) + 2)
                    if q >= 2:
                        pe.wait_ge(s["p3_ready"], g - 1)
                    for hh in range(2):
                        dst = bank[q % 2][:, hh * 192:hh * 192 + w]
                        pe.matmul(dst, ident_b[:, :], mask[:, P + WIN - w:P + WIN], start=True, stop=False)
                        last = pe.matmul(dst, qT[:, t % 2, 2 * pair + hh, :], kT[:, pair, (t + 1) * P - w:(t + 1) * P],
                                         start=False, stop=True)
                    last.then_inc(s["sim_ps"], 1)

                def turn_p(q):
                    t, pair = divmod(q, 4)
                    g = 4 * n0 + q
                    pe.wait_ge(s["p3_ready"], g + 1)
                    if q >= 2:
                        pe.wait_ge(s["pT3_odd" if q % 2 else "pT3_even"], g // 2)
                    for hh in range(2):
                        for blk in range(0 if t % HT else 1, 2):
                            k = 2 * hh + blk
                            last = pe.transpose(bank[2 + q % 2][:, k * P:(k + 1) * P],
                                                p3[:, q % 2, hh, blk * P:(blk + 1) * P], ident)
                    last.then_inc(s["pT3_ps"], 1)

                def pv(q):
                    t, pair = divmod(q, 4)
                    g = 4 * n0 + q
                    pe.wait_ge(s["pT3_odd" if q % 2 else "pT3_even"], g // 2 + 1)
                    pe.wait_ge(s["v3_ready"], n0 + t + 1)
                    if pair == 0 and t > 0:
                        pe.wait_ge(s["on3_ready"], n0 + t)
                    for hh in range(2):
                        h = 2 * pair + hh
                        blks = range(0 if t % HT else 1, 2)
                        for blk in blks:
                            last = pe.matmul(bank[4][:, h * LD:(h + 1) * LD], pT3[:, q % 2, 2 * hh + blk, :],
                                             v_all[:, t - 1 + blk, h * LD:(h + 1) * LD],
                                             start=(blk == blks[0]), stop=(blk == 1))
                    last.then_inc(s["pv3_ps"], 1)

                pe.wait_ge(s["pool_set"], 6)
                for t in range(2):
                    for what in range(3):
                        proj(t, what)
                turn_qk(0, 0)
                turn_qk(0, 1)
                sim(0)
                for q in range(4 * NT):
                    t, pair = divmod(q, 4)
                    if pair == 0 and t + 2 < NT:
                        proj(t + 2, 0)
                        proj(t + 2, 1)
                    if pair == 1 and t + 1 < NT:
                        turn_qk(t + 1, 0)
                    if pair == 2 and t + 1 < NT:
                        turn_qk(t + 1, 1)
                    if pair == 2 and t + 2 < NT:
                        proj(t + 2, 2)
                    if q + 1 < 4 * NT:
                        sim(q + 1)
                    turn_p(q)
                    pv(q)
                pe.wait_ge(s["on3_ready"], n0 + NT)
                pe.wait_ge(s["w3lo_ready"], 2 * layer + 2)

                def out3(t):
                    pe.wait_ge(s["olo_ready"], n0 + t + 1)
                    if t >= 4:
                        pe.wait_ge(s["x3_added"], n0 + t - 3)
                    for c in range(4):
                        w = slice(3 * INNER + c * P, 3 * INNER + (c + 1) * P)
                        cc = slice(c * P, (c + 1) * P)
                        last = three(bank[4 + t % 4][:, 0:P], o_hi[:, t % 2, cc], o_lo[:, t % 2, cc],
                                     w3_hi[:, w], w3_lo[:, w], start=(c == 0), stop=(c == 3))
                    last.then_inc(s["o3_out"], 1)

                for t in range(NT):
                    if t >= 4:
                        pe.wait_ge(s["olo_ready"], n0 + t - 3)
                    for c in range(4):
                        last = pe.transpose(bank[t % 4][:, c * P:(c + 1) * P], on3[:, t, c * P:(c + 1) * P], ident)
                    last.then_inc(s["o3_ps"], 1)
                    if t >= 1:
                        out3(t - 1)
                out3(NT - 1)
                for b in range(B):
                    pe.wait_ge(s["x3_added"], n0 + HT * (b + 1))
                    pe.matmul(bank[b][:, 0:HT * 64], cst[:, C_SH:C_SH + P], x[:, HT * b:HT * b + HT, 64:P],
                              start=True, stop=False)
                    pe.matmul(bank[b][:, 64:HT * 64], cst[:, C_SE:C_SE + P], x[:, HT * b:HT * b + HT - 1, 64:P],
                              start=False, stop=True).then_inc(s["shift_ps"], 1)
                head(8 + layer, jf)

                def hid_w(e, c, up):
                    w0 = 4 * INNER + ((1 - up) * CH3 + c) * P
                    return w3_hi[:, w0:w0 + P], w3_lo[:, w0:w0 + P]

                def out_w(e, c, r):
                    w0 = 4 * INNER + (2 * CH3 + c) * P
                    return w3_hi[:, w0:w0 + P], w3_lo[:, w0:w0 + P]

                feed_forward("geglu", m, jf, [(0, b, c) for b in range(B) for c in range(CH3)], CH3, hid_w, out_w)
                for b in range(B):
                    pe.wait_ge(s["y_taken"], group_base[m] + b + 1)
                    for k in range(HT):
                        last = pe.transpose(bank[2 + b][:, k * P:(k + 1) * P], acc[:, (HT * b + k) * P:(HT * b + k + 1) * P], ident)
                    last.then_inc(s["yT_ps"], 1)

            for what, i in order:
                {"att": attention, "moe": routed, "l2x": lambda i: l2_attention(), "loc": local}[what](i)

        @block.scalar
        def _(act):
            step = Count(act, s["act_step"])

            def split_w(n):
                m = 0 if n < 8 else 1 if n < 28 else 2
                act.wait_ge(s_w[n % RING], 16 * (n // RING + 1))
                if n >= RING:
                    act.wait_ge(s["out_ps"], units_through[n - RING])
                act.activation(w_hi[:, n % RING, 0:WIDTH[m]], w_raw[:, n % RING, 0:WIDTH[m]], ACT.Copy)\
                    .then_inc(s["whi_ready"], 1)

            def head(jx):
                for b in range(B):
                    act.wait_ge(s["xT_ps"], 2 * jx + b + 1)
                    act.activation(half(x_hi, b), bank[6 + b], ACT.Copy).then_inc(s["xhi_ready"], 1)

            def attention(i):
                head(ATT_HEAD[i])
                for n in range(2 * G):
                    b, g = divmod(n, G)
                    act.wait_ge(s["q_ps"], 8 * i + n + 1)
                    if n == 0:
                        act.wait_ge(s["pool_set"], 3 + i)
                    act.activation(half(qs[0:96, g, :], b), bank[g][0:96, :], ACT.Identity,
                                   bias=vec[0:96, V_BQ + G * i + g:V_BQ + G * i + g + 1]).then_inc(s["q_hi"], 1)

                def out_hi(b):
                    act.wait_ge(s["oT_ps"], 2 * i + b + 1)
                    if b == 1:
                        act.wait_ge(s["ao_ps"], 2 * i + 1)
                    act.activation(oT_hi[:, :], bank[6], ACT.Copy).then_inc(s["oT_hi_ready"], 1)

                for t in range(NT):
                    act.wait_ge(s["sub_done"], NT * i + t + 1)
                    act.activation(e_sb[:, t % 2, 0:H * L], e_sb[:, t % 2, 0:H * L], ACT.Exp).then_inc(s["exp_done"], 1)
                    if t == 5:
                        out_hi(0)
                    if t >= 2:
                        act.wait_ge(s["pv_ps"], NT * i + t - 1)
                    for k in range(3):
                        n = 3 * (NT * i + t) + k
                        w = min(4, NC - 4 * k) * P
                        act.wait_ge(s["pt_ps"], n + 1)
                        act.activation(pT[:, t % 2, 4 * k * P:4 * k * P + w], bank[4 + n % 2][:, 0:w], ACT.Copy)\
                            .then_inc(s["pt_ready"], 1)
                out_hi(1)

            def feed_forward(kind, m, units):
                ub, pb = unit_base[m], prod_base[m]
                for n in range(len(units) + 1):
                    if n < len(units):
                        e, b, c = units[n]
                        r = rows_of(kind, c)
                        g = ub + n
                        if kind != "geglu" and b == 0 and c == 0 and plans[m]["first"] + e + 1 < n_ring:
                            split_w(plans[m]["first"] + e + 1)
                        routed_top1 = kind == "top1" and e >= 4
                        if routed_top1:
                            act.wait_ge(s["scaled"], n - 8 + 1)
                        else:
                            act.wait_ge(s["hid_ps"], g + 1)
                        if n >= 3 and not routed_top1:
                            if kind == "gelu":
                                act.wait_ge(s["alo_ready"], g - 2)
                            else:
                                act.wait_ge(s["prod_ready"], pb + n - 2)
                        src = gate[0:r, g % 3, :] if routed_top1 else bank[2 + 2 * (n % 3)][0:r, :]
                        if kind == "gelu":
                            act.activation(gate[:, g % 3, :], src, ACT.Gelu,
                                           bias=vec[:, V_B1 + 4 * e + c:V_B1 + 4 * e + c + 1]).then_inc(s["gate_ready"], 1)
                        elif kind == "geglu":
                            v = V_B1G + (m - 3) * CH3 + c
                            act.activation(gate[:, g % 3, :], src, ACT.Gelu, bias=vec[:, v:v + 1]).then_inc(s["gate_ready"], 1)
                        else:
                            act.activation(gate[0:r, g % 3, :], src, ACT.Silu).then_inc(s["gate_ready"], 1)
                    if kind != "gelu" and n >= 1:
                        u = n - 1
                        r = rows_of(kind, units[u][2])
                        act.wait_ge(s["prod_ready"], pb + u + 1)
                        if u >= UB:
                            act.wait_ge(s["out_ps"], ub + u - UB + 1)
                        act.activation(a_hi[0:r, (ub + u) % UB, :], prod[0:r, (ub + u) % 3, :], ACT.Copy)\
                            .then_inc(s["ahi_ready"], 1)
                    if n == 2 and kind != "geglu":
                        ne = 16 if kind == "top1" else 8
                        for hb in range(B):
                            act.wait_ge(s["cT_ps"], 2 * m + hb + 1)
                            act.activation(half(cT[0:ne, :], hb), bank[hb][0:ne, :], ACT.Copy).then_inc(s["cT_ready"], 1)
                        act.wait_ge(s["cT_ready"], 2 * m + 2)
                        for r in range(4):
                            act.dma_start(crow[32 * r:32 * r + 1, 0:ne // 4, :], cT[r:ne:4, :]).then_inc(s["ld_row"], 16)

            def routed(m):
                head(MOE_HEAD[m])
                act.wait_ge(s["rt_sub"], m + 1)
                if m == 1:
                    act.activation(sm[:, 0, :], m8[:, :, 0], ACT.Exp, scale=-1.0).then_inc(s["rt_exp"], 1)
                else:
                    ne = 8 if m == 0 else 7
                    act.activation(lg[:, :, 0:ne], lg[:, :, 0:ne], ACT.Exp).then_inc(s["rt_exp"], 1)
                feed_forward(plans[m]["kind"], m, plans[m]["units"])

            def l2_attention():
                head(L2_HEAD)
                for b in range(B):
                    act.wait_ge(s["s_sub"], b + 1)
                    ts = slice(HT * b, HT * b + HT)
                    act.activation(sc[:, ts, :], sc[:, ts, :], ACT.Exp).then_inc(s["s_exp"], 1)
                for b in range(B):
                    act.wait_ge(s["al_ps"], b + 1)
                    act.activation(alT[:, b, :], bank[2 + b][0:L, :], ACT.Copy).then_inc(s["alT_ready"], 1)
                    act.wait_ge(s["c_ps"], b + 1)
                    act.activation(c_hi[:, b, :], bank[4 + b], ACT.Copy).then_inc(s["chi_ready"], 1)
                for b in range(B):
                    act.wait_ge(s["t_ps"], b + 1)
                    act.activation(th[:, b, :], bank[6 + b], ACT.Tanh).then_inc(s["tanh_ready"], 1)

            def split_w3(layer, part):
                w = (slice(0, 3 * INNER), slice(3 * INNER, L3W))[part]
                act.wait_ge(s["ld_w3"], 32 * (layer + 1))
                if layer == 1 and part == 1:
                    act.wait_ge(s["out_ps"], unit_base[4])
                act.activation(w3_hi[:, w], w3_raw[:, w], ACT.Copy).then_inc(s["w3hi_ready"], 1)

            def local(layer):
                m, ja, jf = 3 + layer, 7 + 2 * layer, 8 + 2 * layer
                if layer == 0:
                    act.wait_ge(s["x_added"], before[("loc", 0)])
                    act.activation(kept[:, :, :], x[:, :, :], ACT.Copy).then_inc(s["kept"], 1)
                    split_w3(0, 0)
                split_w3(layer, 1)
                for b in range(B):
                    act.wait_ge(s["xT_ps"], 2 * ja + b + 1)
                    act.activation(x_hi[0:64, b * S:(b + 1) * S], bank[6 + b][0:64, :], ACT.Copy)
                    act.activation(x_hi[64:P, b * S + 1:(b + 1) * S], bank[6 + b][64:P, 0:S - 1], ACT.Copy)\
                        .then_inc(s["xhi_ready"], 1)
                n0 = NT * layer

                def square(t, what):
                    act.wait_ge(s[("q3_ps", "k3_ps")[what]], n0 + t + 1)
                    if t > 0 and what == 0:
                        act.wait_ge(s["ssq_ready"], n0 + t)
                    act.activation(sq[:, what, :], bank[6 + what], ACT.Square).then_inc(s["sq_ready"], 1)

                def take_v(t):
                    act.wait_ge(s["v3_ps"], n0 + t + 1)
                    act.activation(v_all[:, t, :], bank[6], ACT.Copy).then_inc(s["v3_ready"], 1)

                def take_qk(t, what):
                    act.wait_ge(s["qkT_ps"], 2 * (n0 + t) + what + 1)
                    src = bank[5].rearrange("p (c n) -> p c n", c=4)
                    if what:
                        act.activation(kT[:, :, t * P:(t + 1) * P], src, ACT.Copy).then_inc(s["qkT_ready"], 1)
                        return
                    if t == 0:
                        act.wait_ge(s["pool_set"], 6)
                    act.activation(qT[0:LD, t % 2, 0:LH:2, :], src[0:LD], ACT.Copy)
                    act.activation(qT[LD:P, t % 2, 1:LH:2, :], src[LD:P], ACT.Copy).then_inc(s["qkT_ready"], 1)

                def exps(q):
                    t, pair = divmod(q, 4)
                    w = P + (WIN if t % HT else 0)
                    g = 4 * n0 + q
                    act.wait_ge(s["nb_ready"], g + 1)
                    if q >= 2:
                        act.wait_ge(s["pT3_ps"], g - 1)
                    for hh in range(2):
                        h = 2 * pair + hh
                        last = act.activation(p3[:, q % 2, hh, 2 * P - w:2 * P], bank[q % 2][:, hh * 192:hh * 192 + w],
                                              ACT.Exp, bias=nb3[:, t % 2, h:h + 1], scale=rq[:, t % 2, 0, h:h + 1],
                                              accum_out=sum3[:, t % 2, h:h + 1])
                    last.then_inc(s["p3_ready"], 1)

                for t in range(2):
                    square(t, 0)
                    square(t, 1)
                    take_v(t)
                take_qk(0, 0)
                take_qk(0, 1)
                for q in range(4 * NT):
                    t, pair = divmod(q, 4)
                    exps(q)
                    if pair == 0 and t + 2 < NT:
                        square(t + 2, 0)
                        square(t + 2, 1)
                    if pair == 1 and t + 1 < NT:
                        take_qk(t + 1, 0)
                    if pair == 2 and t + 1 < NT:
                        take_qk(t + 1, 1)
                    if pair == 2 and t + 2 < NT:
                        take_v(t + 2)
                    if q % 2:
                        act.wait_ge(s["pT3_ps"], 4 * n0 + q + 1)
                        if q >= 2:
                            act.wait_ge(s["pv3_ps"], 4 * n0 + q - 1)
                        blk = slice(0 if t % HT else 1, 2)
                        src = bank[3].rearrange("p (h k n) -> p h k n", h=2, k=2)[:, :, blk, :]
                        act.activation(pT3[:, 1, :, :].rearrange("p (h k) n -> p h k n", h=2)[:, :, blk, :], src, ACT.Copy)\
                            .then_inc(s["pT3_odd"], 1)
                if layer == 0 and ("loc", 1) in order:
                    split_w3(1, 0)
                for t in range(NT):
                    act.wait_ge(s["o3_ps"], n0 + t + 1)
                    if t >= 2:
                        act.wait_ge(s["o3_out"], n0 + t - 1)
                    act.activation(o_hi[:, t % 2, :], bank[t % 4], ACT.Copy).then_inc(s["ohi_ready"], 1)
                for b in range(B):
                    act.wait_ge(s["xT_ps"], 2 * jf + b + 1)
                    act.activation(ytmp[:, b, :], bank[6 + b], ACT.Identity, bias=vec[:, V_LB + layer:V_LB + layer + 1],
                                   scale=vec[:, V_LG + layer:V_LG + layer + 1]).then_inc(s["hF_ready"], 1)
                    act.wait_ge(s["hF_ready"], 2 * layer + b + 1)
                    act.activation(half(x_hi, b), ytmp[:, b, :], ACT.Copy).then_inc(s["xhi_ready"], 1)
                feed_forward("geglu", m, [(0, b, c) for b in range(B) for c in range(CH3)])

            if n_ring:
                split_w(0)
            for what, i in order:
                {"att": attention, "moe": routed, "l2x": lambda i: l2_attention(), "loc": local}[what](i)
                if (what, i) == ("att", 0):
                    act.wait_ge(s["gauss_d2"], 1)
                    act.activation(gauss[:, :, :], gauss[:, :, :], ACT.Exp, scale=-1.0 / 128.0)\
                        .then_inc(s["gauss_ready"], 1)

        @block.gpsimd
        def _(pool):
            step = Count(pool, s["pool_step"])

            def split_w(n):
                m = 0 if n < 8 else 1 if n < 28 else 2
                pool.wait_ge(s["whi_ready"], n + 1)
                w = slice(0, WIDTH[m])
                pool.tensor_tensor(w_lo[:, n % RING, w], w_raw[:, n % RING, w], w_hi[:, n % RING, w].bitcast(F32),
                                   ALU.subtract).then_inc(s["wlo_ready"], 1)

            def norm(ln):
                for b in range(B):
                    pool.wait_ge(s["ve_ready"], 2 * ln + b + 1)
                    pool.tensor_tensor(rstd[:, HT * b:HT * b + HT], ve[:, HT * b:HT * b + HT], mhalf[:, 0:HT], ALU.pow)\
                        .then_inc(s["rstd_ready"], 1)

            def attention(i):
                if i > 0:
                    pool.wait_ge(s["x_added"], before[("att", i)])
                step.done(pool.memset(e_sb[:, :, H * L:NC * P], 0.0))
                step.wait()
                pool.memset(qs[96:P, :, :].bitcast(F32), 1.0).then_inc(s["pool_set"], 1)
                pool.wait_ge(s["pool_set"], 3 + i)
                norm(ATT_HEAD[i])

            def routed(m):
                p = plans[m]
                kind, gb, cb = p["kind"], group_base[m], cb_base[m]
                norm(MOE_HEAD[m])
                skip = {"gelu": 0, "top1": 4, "top2": 1}[kind]

                def weights_of(e):
                    w = e - skip
                    if w == 0:
                        pool.wait_ge(s["ld_row"], 64 * (m + 1))
                    if w >= 2:
                        if kind == "top1":
                            pool.wait_ge(s["scaled"], 2 * (w - 1))
                        else:
                            pool.wait_ge(s["y_taken"], gb + 2 * (e - 1))
                    pool.wait_ge(s["wlo_ready"], min(p["first"] + max(e - 1, 0) + 2, n_ring))
                    if kind != "top1" and e >= 3:
                        pool.wait_ge(s["acc_added"], 14 * (m // 2) + 2 * (e - 2))
                    pool.partition_broadcast(cB[:, w % 2, :], crow[32 * (w % 4):32 * (w % 4) + 1, w // 4, :], P)\
                        .then_inc(s["cb_ready"], 1)
                    pool.wait_ge(s["cb_ready"], cb + w + 1)

                def add(e, b):
                    pool.wait_ge(s["y_taken"], gb + 2 * e + b + 1)
                    pool.tensor_tensor(half(acc, b), half(acc, b), ytmp[:, b, :], ALU.add).then_inc(s["acc_added"], 1)

                for e in range(p["experts"]):
                    if p["first"] + e + 1 < n_ring:
                        split_w(p["first"] + e + 1)
                    if e == 0 and skip == 0:
                        weights_of(0)
                    if kind != "top1" and e - 1 >= 1:
                        add(e - 1, 0)
                        add(e - 1, 1)
                    if e + 1 >= skip and e + 1 < p["experts"]:
                        weights_of(e + 1)
                if kind != "top1":
                    add(p["experts"] - 1, 0)
                    add(p["experts"] - 1, 1)

            def split_w3(layer, part):
                w = (slice(0, 3 * INNER), slice(3 * INNER, L3W))[part]
                pool.wait_ge(s["w3hi_ready"], 2 * layer + part + 1)
                pool.tensor_tensor(w3_lo[:, w], w3_raw[:, w], w3_hi[:, w].bitcast(F32), ALU.subtract)\
                    .then_inc(s["w3lo_ready"], 1)

            def local(layer):
                n0 = NT * layer
                if layer == 0:
                    pool.wait_ge(s["x_added"], before[("loc", 0)])
                    norm(7)
                    step.done(pool.memset(p3[:, :, :, 0:WIN], 0.0))
                    step.wait()
                    pool.memset(qT[:, :, :, :], 0.0).then_inc(s["pool_set"], 1)
                    split_w3(0, 0)
                for t in range(NT):
                    n = n0 + t
                    pool.wait_ge(s["kr_ready"], n + 1)
                    if t >= 2:
                        pool.wait_ge(s["qkT_ps"], 2 * n - 2)
                    pool.tensor_tensor(qk[:, t % 2, :, :], r1[:, :, :], r2[:, :, :], ALU.add)
                    pool.wait_ge(s["ssq_ready"], n + 1)
                    step.done(pool.tensor_tensor(rn[:, t % 2, :], ssq[:, t % 2, :], mhalf[:, 0:2 * LH], ALU.pow))
                    step.wait()
                    k = qk[:, t % 2, 1, :].rearrange("p (h d) -> p h d", h=LH)
                    pool.tensor_tensor(k, k, rn[:, t % 2, LH:2 * LH].unsqueeze(2).to_broadcast([P, LH, LD]), ALU.mult)\
                        .then_inc(s["qk_ready"], 1)
                    if t == 1:
                        split_w3(layer, 1)
                if layer == 0 and ("loc", 1) in order:
                    split_w3(1, 0)
                norm(8 + layer)
                if layer == 1:
                    pool.wait_ge(s["xn_ready"], 2 * 9 + 2)
                    pool.wait_ge(s["kept"], 1)
                    pool.tensor_tensor(x[:, :, :], x[:, :, :], kept[:, :, :], ALU.add).then_inc(s["kept_added"], 1)

            pool.memset(mhalf[:, :], -0.5).then_inc(s["pool_set"], 1)
            pool.memset(ones[:, :], 1.0).then_inc(s["pool_set"], 1)
            if n_ring:
                split_w(0)
            for what, i in order:
                {"att": attention, "moe": routed, "l2x": lambda i: norm(L2_HEAD), "loc": local}[what](i)

        @block.vector
        def _(dve):
            step = Count(dve, s["dve_step"])

            def then(instruction):
                step.done(instruction)
                step.wait()

            def split_low(dst, full, upper):
                return dve.tensor_tensor(dst, full, upper.bitcast(F32), ALU.subtract)

            def statistics(b):
                for t in tiles(b):
                    last = dve.bn_stats(stats[:, t, 0:6], x[:, t, :])
                then(last)

            def head(ln, jx, shifted=False):
                for b in range(B):
                    ts = slice(HT * b, HT * b + HT)
                    if shifted:
                        dve.wait_ge(s["shift_ps"], 2 * (ln - 8) + b + 1)
                        for k, t in enumerate(tiles(b)):
                            dve.bn_stats(stats[:, t, 0:6], x[:, t, 0:64])
                            last = dve.bn_stats(stats[:, t, 6:12], bank[b][:, 64 * k:64 * k + 64])
                        then(last)
                    else:
                        statistics(b)
                    for t in tiles(b):
                        last = dve.bn_aggr(mv[:, t, :], stats[:, t, 0:12 if shifted else 6])
                    then(last)
                    dve.tensor_scalar(ve[:, ts], mv[:, ts, 1], EPS, None, ALU.add).then_inc(s["ve_ready"], 1)
                for b in range(B):
                    dve.wait_ge(s["rstd_ready"], 2 * ln + b + 1)
                    for k, t in enumerate(tiles(b)):
                        if shifted:
                            dve.tensor_scalar(xn[:, t, 0:64], x[:, t, 0:64], mv[:, t, 0:1], rstd[:, t:t + 1],
                                              ALU.subtract, ALU.mult)
                            last = dve.tensor_scalar(xn[:, t, 64:P], bank[b][:, 64 * k:64 * k + 64], mv[:, t, 0:1],
                                                     rstd[:, t:t + 1], ALU.subtract, ALU.mult)
                        else:
                            last = dve.tensor_scalar(xn[:, t, :], x[:, t, :], mv[:, t, 0:1], rstd[:, t:t + 1],
                                                     ALU.subtract, ALU.mult)
                    last.then_inc(s["xn_ready"], 1)
                for b in range(B):
                    dve.wait_ge(s["xhi_ready"], 2 * jx + b + 1)
                    full = ytmp[:, b, :] if shifted else bank[6 + b]
                    split_low(half(x_lo, b), full, half(x_hi, b)).then_inc(s["xlo_ready"], 1)

            def x_tiles(b):
                return x[:, HT * b:HT * b + HT, :].rearrange("p t d -> p (t d)")

            def attention(i):
                w = aw[:, i, :]
                dve.wait_ge(s["ld_aw" if i == 0 else "ld_aw_more"], 16)
                dve.tensor_copy(wq_hi[:, :], w[:, 0:384])
                then(dve.tensor_copy(wo_hi[:, :], w[:, 896:1024]))
                split_low(wq_lo[:, :], w[:, 0:384], wq_hi[:, :])
                split_low(wo_lo[:, :], w[:, 896:1024], wo_hi[:, :]).then_inc(s["wsplit"], 1)
                dve.wait_ge(s["k_ps"], i + 1)
                for g in range(G):
                    last = dve.scalar_tensor_tensor(
                        out=k_f[:, g, :], in0=bank[4 + g // 3][0:96, (g % 3) * B * L:(g % 3 + 1) * B * L],
                        scalar=vec[0:96, V_BK + G * i + g:V_BK + G * i + g + 1], in1=tau_s[0:96, :],
                        op0=ALU.add, op1=ALU.mult)
                then(last)
                then(dve.tensor_copy(k_x[:, :, :], k_f[:, :, :]))
                then(split_low(k_x[32:64, :, :], k_f[32:64, :, :], k_x[32:64, :, :]))
                for g in range(G):
                    src = k_x[:, g, :].bitcast(F32).rearrange("p (b k) -> p b k", b=B)
                    last = dve.tensor_tensor(
                        k_st[0:96, :, g, :].rearrange("p b (j k) -> p b j k", j=HG),
                        src.unsqueeze(2).to_broadcast([96, B, HG, L]),
                        cst[0:96, C_KM:C_KM + HG].unsqueeze(1).unsqueeze(3).to_broadcast([96, B, HG, L]), ALU.mult)
                last.then_inc(s["k_ready"], 1)
                for vg in range(VG):
                    dve.wait_ge(s["v_ps"], VG * i + vg + 1)
                    src = bank[(6, 7, 4, 5, 6)[vg]].rearrange("p (c h d) -> p c h d", c=4, h=H)
                    m = cst[:, C_VM + 4 * vg * H:C_VM + 4 * (vg + 1) * H].rearrange("p (c h) -> p c h", c=4)
                    for q in range(4):
                        last = dve.tensor_tensor(v_bd[:, 4 * vg + q, :, 0:DK], src[:, q, :, :],
                                                 m[:, q, :].unsqueeze(2).to_broadcast([P, H, DK]), ALU.mult)
                    last.then_inc(s["v_ready"], 1)
                dve.wait_ge(s["brow_ps"], i + 1)
                dve.tensor_tensor(brow[:, :], bank[7][0:1, 0:P], rows[0:1, i * P:(i + 1) * P], ALU.add)\
                    .then_inc(s["brow_ready"], 1)
                head(ATT_HEAD[i], ATT_HEAD[i])
                for n in range(2 * G):
                    b, g = divmod(n, G)
                    dve.wait_ge(s["q_hi"], 8 * i + n + 1)
                    q = half(qs[64:96, g, :], b)
                    dve.scalar_tensor_tensor(out=q, in0=bank[g][64:96, :], scalar=vec[64:96, V_BQ + G * i + g:V_BQ + G * i + g + 1],
                                             in1=q.bitcast(F32), op0=ALU.add, op1=ALU.subtract).then_inc(s["q_lo"], 1)

                def maximum(t):
                    n = NT * i + t
                    sp_ = ps[:, 0:4, 0:GW].rearrange("p g (j k) -> p g j k", j=HG)
                    m = mx[:, t % 2, :].rearrange("p (g j) -> p g j", g=G)
                    dve.wait_ge(s["score_ps"], n + 1)
                    then(dve.tensor_reduce(m, sp_, AX.X, ALU.max))
                    if t >= 2:
                        dve.wait_ge(s["pt_ps"], 3 * (n - 1))
                    dve.tensor_tensor(e_sb[:, t % 2, 0:H * L].rearrange("p (g j k) -> p g j k", g=G, j=HG), sp_,
                                      m.unsqueeze(3).to_broadcast([P, G, HG, L]), ALU.subtract).then_inc(s["sub_done"], 1)

                def normalise(t):
                    dve.wait_ge(s["pv_ps"], NT * i + t + 1)
                    o = bank[7][:, 0:VW].rearrange("p (h d) -> p h d", h=H)
                    then(dve.reciprocal(rsum[:, t % 2, :], o[:, :, DK]))
                    dve.tensor_tensor(on[:, t, :].rearrange("p (h d) -> p h d", h=H), o[:, :, 0:DK],
                                      rsum[:, t % 2, :].unsqueeze(2).to_broadcast([P, H, DK]), ALU.mult)\
                        .then_inc(s["on_ready"], 1)

                def out_lo(b):
                    dve.wait_ge(s["oT_hi_ready"], 2 * i + b + 1)
                    split_low(oT_lo[:, :], bank[6], oT_hi[:, :]).then_inc(s["oT_lo_ready"], 1)

                def add(b):
                    dve.wait_ge(s["ao_ps"], 2 * i + b + 1)
                    dve.tensor_tensor(x_tiles(b), x_tiles(b), bank[6], ALU.add).then_inc(s["x_added"], 1)

                for t in range(NT):
                    maximum(t)
                    if t >= 1:
                        normalise(t - 1)
                    if t == 5:
                        out_lo(0)
                    if t == 6:
                        add(0)
                normalise(NT - 1)
                out_lo(1)
                add(1)
                dve.wait_ge(s["x_added"], before[("att", i)] + 2)

            def feed_forward(kind, m, units, chunks):
                ub, pb, gb = unit_base[m], prod_base[m], group_base[m]
                lag = LAG[kind]

                def lower(u, full):
                    r = rows_of(kind, units[u][2])
                    k = (ub + u) % UB
                    split_low(a_lo[0:r, k, :], full[0:r, (ub + u) % 3, :], a_hi[0:r, k, :]).then_inc(s["alo_ready"], 1)

                def take_y(e, b):
                    g = group_of(kind, e, b)
                    u = max(n for n, (ee, bb, c) in enumerate(units) if (ee, bb) == (e, b))
                    dve.wait_ge(s["out_ps"], ub + u + 1)
                    w = e - {"gelu": 0, "top1": 4, "top2": 1, "geglu": 0}[kind]
                    if kind == "geglu":
                        v = V_B23 + m - 3
                        i_ = dve.tensor_scalar(half(acc, b), bank[b], vec[:, v:v + 1], None, ALU.add)
                    elif kind == "top1":
                        i_ = dve.tensor_copy(half(acc, b) if e < 4 else ytmp[:, b, :], bank[b])
                    elif w < 0:
                        i_ = dve.tensor_copy(half(acc, b), bank[b])
                    else:
                        dve.wait_ge(s["cb_ready"], cb_base[m] + w + 1)
                        if e >= 2:
                            dve.wait_ge(s["acc_added"], 14 * (m // 2) + 2 * (e - 2) + b + 1)
                        dst = half(acc, b) if e == 0 else ytmp[:, b, :]
                        if kind == "gelu":
                            i_ = dve.scalar_tensor_tensor(out=dst, in0=bank[b], scalar=vec[:, V_B2 + e:V_B2 + e + 1],
                                                          in1=half(cB[:, w % 2, :], b), op0=ALU.add, op1=ALU.mult)
                        else:
                            i_ = dve.tensor_tensor(dst, bank[b], half(cB[:, w % 2, :], b), ALU.mult)
                    i_.then_inc(s["y_taken"], 1)

                for n in range(len(units) + lag + 1):
                    v = n - lag - 1
                    if v >= 0:
                        e, b, c = units[v]
                        if last_of_group(kind, chunks, e, c):
                            take_y(e, b)
                    if kind == "gelu":
                        if n < len(units):
                            g = ub + n
                            dve.wait_ge(s["gate_ready"], g + 1)
                            if n >= UB:
                                dve.wait_ge(s["out_ps"], g - UB + 1)
                            then(dve.tensor_copy(a_hi[:, g % UB, :], gate[:, g % 3, :]))
                            lower(n, gate)
                        continue
                    if kind == "top1" and n < len(units) and units[n][0] >= 4:
                        e, b, c = units[n]
                        w = e - 4
                        dve.wait_ge(s["hid_ps"], ub + n + 1)
                        dve.wait_ge(s["cb_ready"], cb_base[m] + w + 1)
                        dve.wait_ge(s["prod_ready"], pb + n - 2)
                        dve.tensor_tensor(gate[:, (ub + n) % 3, :], bank[2 + 2 * (n % 3)], half(cB[:, w % 2, :], b), ALU.mult)\
                            .then_inc(s["scaled"], 1)
                    u = n - 1 if kind == "top1" else n
                    if 0 <= u < len(units):
                        e, b, c = units[u]
                        g, r = ub + u, rows_of(kind, c)
                        dve.wait_ge(s["gate_ready"], g + 1)
                        if u >= 3:
                            dve.wait_ge(s["alo_ready"], g - 2)
                        up = bank[3 + 2 * (u % 3)][0:r, :]
                        dst, gt = prod[0:r, g % 3, :], gate[0:r, g % 3, :]
                        if kind == "geglu":
                            v = V_B1A + (m - 3) * CH3 + c
                            i_ = dve.scalar_tensor_tensor(out=dst, in0=up, scalar=vec[:, v:v + 1], in1=gt,
                                                          op0=ALU.add, op1=ALU.mult)
                        else:
                            i_ = dve.tensor_tensor(dst, gt, up, ALU.mult)
                        i_.then_inc(s["prod_ready"], 1)
                    u -= 1
                    if 0 <= u < len(units):
                        dve.wait_ge(s["ahi_ready"], pb + u + 1)
                        lower(u, prod)

            def route(m):
                ne = (8, 16, 7)[m]
                cols = (8, 16, 8)[m]
                dve.wait_ge(s["lg_ps"], m + 1)
                logits = bank[0][:, 0:NT * cols].rearrange("p (t e) -> p t e", e=cols)
                every = lambda v, n: v.unsqueeze(2).to_broadcast([P, NT, n])
                index = cst[:, C_IO:C_IO + cols].unsqueeze(1).to_broadcast([P, NT, cols])
                top = 1 if m == 1 else 2
                if m == 1:
                    then(dve.tensor_copy(lg[:, :, 0:cols], logits))
                    ranked = lg
                else:
                    if m == 2:
                        rb = vec[:, V_RB:V_RB + 8].unsqueeze(1).to_broadcast([P, NT, 8])
                        then(dve.tensor_tensor(lg[:, :, 0:8], logits, rb, ALU.add))
                        logits = lg[:, :, 0:8]
                        dve.memset(pr[:, :, 7:8], -1.0)
                    then(dve.tensor_reduce(sm[:, 0, :], logits[:, :, 0:ne], AX.X, ALU.max))
                    dve.tensor_tensor(lg[:, :, 0:ne], logits[:, :, 0:ne], every(sm[:, 0, :], ne), ALU.subtract)\
                        .then_inc(s["rt_sub"], 1)
                    dve.wait_ge(s["rt_exp"], m + 1)
                    then(dve.tensor_reduce(sm[:, 1, :], lg[:, :, 0:ne], AX.X, ALU.add))
                    then(dve.reciprocal(sm[:, 2, :], sm[:, 1, :]))
                    then(dve.tensor_tensor(pr[:, :, 0:ne], lg[:, :, 0:ne], every(sm[:, 2, :], ne), ALU.mult))
                    ranked = pr
                for t in range(NT):
                    last = dve.max(m8[:, t, :], ranked[:, t, 0:cols])
                if m == 1:
                    last.then_inc(s["rt_sub"], 1)
                    dve.wait_ge(s["rt_sub"], 2)
                else:
                    then(last)
                for t in range(NT):
                    last = dve.max_index(i8[:, t, :], m8[:, t, :], ranked[:, t, 0:cols])
                then(last)
                then(dve.tensor_copy(i8f[:, :, 0:top], i8[:, :, 0:top]))
                for k in range(top):
                    last = dve.tensor_tensor(sel[:, k, :, 0:cols], index, every(i8f[:, :, k], cols), ALU.is_equal)
                then(last)
                if m == 1:
                    dve.wait_ge(s["rt_exp"], 2)
                    then(dve.tensor_scalar(sm[:, 1, :], sm[:, 0, :], 1.0, None, ALU.add))
                    then(dve.reciprocal(sm[:, 2, :], sm[:, 1, :]))
                    dve.tensor_tensor(cw[:, :, 0:cols], sel[:, 0, :, 0:cols], every(sm[:, 2, :], cols), ALU.mult)\
                        .then_inc(s["cw_ready"], 1)
                else:
                    then(dve.tensor_tensor(sel[:, 0, :, 0:cols], sel[:, 0, :, 0:cols], sel[:, 1, :, 0:cols], ALU.add))
                    then(dve.tensor_tensor(cw[:, :, 0:cols], sel[:, 0, :, 0:cols], pr[:, :, 0:cols], ALU.mult))
                    then(dve.tensor_reduce(sm[:, 0, :], cw[:, :, 0:cols], AX.X, ALU.add))
                    then(dve.reciprocal(sm[:, 1, :], sm[:, 0, :]))
                    dve.tensor_tensor(cw[:, :, 0:cols], cw[:, :, 0:cols], every(sm[:, 1, :], cols), ALU.mult)\
                        .then_inc(s["cw_ready"], 1)

            def routed(m):
                p = plans[m]
                head(MOE_HEAD[m], MOE_HEAD[m])
                route(m)
                feed_forward(p["kind"], m, p["units"], p["chunks"])
                for b in range(B):
                    dve.wait_ge(s["yT_ps"], 2 * m + b + 1)
                    i_ = dve.tensor_tensor(x_tiles(b), x_tiles(b), bank[2 + b], ALU.add)
                    if m == 1:
                        then(i_)
                        for k, t in enumerate(tiles(b)):
                            i_ = dve.scalar_tensor_tensor(out=x[:, t, :], in0=bank[4 + b][:, k * P:(k + 1) * P],
                                                          scalar=sm[:, 2, t:t + 1], in1=x[:, t, :], op0=ALU.mult, op1=ALU.add)
                    i_.then_inc(s["x_added"], 1)
                dve.wait_ge(s["x_added"], before[("moe", m)] + 2)

            def l2_attention():
                dve.wait_ge(s["ld_l2"], 48)
                dve.memset(m_hi[:, :, L:78].bitcast(F32), 0.0)
                dve.memset(m_lo[:, :, L:78].bitcast(F32), 0.0)
                dve.wait_ge(s["m_ps"], 1)
                m_ps = bank[4][:, 0:B * L].rearrange("p (b k) -> p b k", b=B)
                dve.tensor_copy(m_hi[:, :, 0:L], m_ps)
                then(dve.tensor_copy(wc_hi[:, :], l2w[:, P:3 * P]))
                split_low(wc_lo[:, :], l2w[:, P:3 * P], wc_hi[:, :])
                split_low(m_lo[:, :, 0:L], m_ps, m_hi[:, :, 0:L]).then_inc(s["m_ready"], 1)
                head(L2_HEAD, L2_HEAD)
                every = lambda v: v.unsqueeze(2).to_broadcast([P, HT, L])
                row = lambda v: v.unsqueeze(1).to_broadcast([P, HT, L])
                for b in range(B):
                    ts = slice(HT * b, HT * b + HT)
                    z = sc[:, ts, :]
                    dve.wait_ge(s["s_ps"], b + 1)
                    src = bank[b][:, 0:HT * 78].rearrange("p (t k) -> p t k", t=HT)[:, :, 0:L]
                    then(dve.tensor_tensor(z, src, row(valid[:, b, :]), ALU.mult))
                    then(dve.tensor_tensor(z, z, row(neg[:, b, :]), ALU.add))
                    then(dve.tensor_reduce(l2m[:, 0, ts], z, AX.X, ALU.max))
                    dve.tensor_tensor(z, z, every(l2m[:, 0, ts]), ALU.subtract).then_inc(s["s_sub"], 1)
                dve.wait_ge(s["gauss_ready"], 1)
                for b in range(B):
                    ts = slice(HT * b, HT * b + HT)
                    z, z2 = sc[:, ts, :], sc2[:, ts, :]
                    dve.wait_ge(s["s_exp"], b + 1)
                    then(dve.tensor_reduce(l2m[:, 1, ts], z, AX.X, ALU.add))
                    then(dve.reciprocal(l2m[:, 2, ts], l2m[:, 1, ts]))
                    then(dve.tensor_tensor(z2, z, every(l2m[:, 2, ts]), ALU.mult))
                    dve.tensor_tensor(z2, z2, row(gauss[:, b, :]), ALU.mult).then_inc(s["al_ready"], 1)
                for b in range(B):
                    dve.wait_ge(s["chi_ready"], b + 1)
                    split_low(c_lo[:, b, :], bank[4 + b], c_hi[:, b, :]).then_inc(s["clo_ready"], 1)
                for b in range(B):
                    dve.wait_ge(s["tanh_ready"], b + 1)
                    dve.tensor_tensor(x_tiles(b), x_tiles(b), th[:, b, :], ALU.add).then_inc(s["x_added"], 1)
                dve.wait_ge(s["x_added"], before[("l2x", 0)] + 2)

            def local(layer):
                m, ja, jf = 3 + layer, 7 + 2 * layer, 8 + 2 * layer
                n0 = NT * layer
                if layer == 0:
                    for b in range(B):
                        statistics(b)
                        for t in tiles(b):
                            last = dve.bn_aggr(mv[:, t, :], stats[:, t, 0:6])
                        then(last)
                        dve.tensor_scalar(ve[:, HT * b:HT * b + HT], mv[:, HT * b:HT * b + HT, 1], EPS, None, ALU.add)\
                            .then_inc(s["ve_ready"], 1)
                    dve.tensor_copy(ident_b[:, :], ident)
                    dve.tensor_copy(mask[:, :], cst[:, C_MS:C_MS + P + WIN])
                    dve.wait_ge(s["ld_rope"], 16)
                if layer == 0:
                    dve.wait_ge(s["kept"], 1)
                    for b in range(B):
                        dve.wait_ge(s["rstd_ready"], 2 * 7 + b + 1)
                        for t in tiles(b):
                            last = dve.tensor_scalar(x[:, t, :], x[:, t, :], mv[:, t, 0:1], rstd[:, t:t + 1],
                                                     ALU.subtract, ALU.mult)
                        last.then_inc(s["xn_ready"], 1)
                for k in range(4):
                    v = V_QS + (4 * layer + k) * LD
                    last = dve.tensor_tensor(rope[:, k, :, :], rope_raw[:, k, :, :],
                                             vec[:, v:v + LD].unsqueeze(1).to_broadcast([P, HT, LD]), ALU.mult)
                then(last)
                for b in range(B):
                    c0 = b * S
                    dve.memset(x_hi[64:P, c0:c0 + 1].bitcast(F32), 0.0)
                    dve.memset(x_lo[64:P, c0:c0 + 1].bitcast(F32), 0.0)
                    dve.wait_ge(s["xhi_ready"], 2 * ja + b + 1)
                    split_low(x_lo[0:64, c0:c0 + S], bank[6 + b][0:64, :], x_hi[0:64, c0:c0 + S])
                    split_low(x_lo[64:P, c0 + 1:c0 + S], bank[6 + b][64:P, 0:S - 1], x_hi[64:P, c0 + 1:c0 + S])\
                        .then_inc(s["xlo_ready"], 1)

                def rotate(t, what):
                    dve.wait_ge(s["sq_ready"], 2 * (n0 + t) + what + 1)
                    if what == 0 and t > 0:
                        dve.wait_ge(s["qk_ready"], n0 + t)
                    src = bank[6 + what].rearrange("p (h d) -> p h d", h=LH)
                    swapped = bank[6 + what].rearrange("p (h a d) -> p h a d", h=LH, a=2)[:, :, ::-1, :]
                    c, sn = rope[:, 2 * what, t % HT, :], rope[:, 2 * what + 1, t % HT, :]
                    dve.tensor_tensor(r1[:, what, :].rearrange("p (h d) -> p h d", h=LH), src,
                                      c.unsqueeze(1).to_broadcast([P, LH, LD]), ALU.mult)
                    dve.tensor_tensor(r2[:, what, :].rearrange("p (h a d) -> p h a d", h=LH, a=2), swapped,
                                      sn.rearrange("p (a d) -> p a d", a=2).unsqueeze(1).to_broadcast([P, LH, 2, LD // 2]),
                                      ALU.mult).then_inc(s[("rot_ready", "kr_ready")[what]], 1)

                def norms(t):
                    n = n0 + t
                    if t >= 1:
                        dve.wait_ge(s["qk_ready"], n)
                    then(dve.tensor_reduce(ssq[:, t % 2, :], sq[:, :, :].rearrange("p w (h d) -> p (w h) d", h=LH),
                                           AX.X, ALU.add))
                    dve.tensor_scalar(ssq[:, t % 2, :], ssq[:, t % 2, :], 1e-24, None, ALU.max).then_inc(s["ssq_ready"], 1)

                def query_scale(t):
                    dve.wait_ge(s["qk_ready"], n0 + t + 1)
                    if t >= 2:
                        dve.wait_ge(s["p3_ready"], 4 * (n0 + t) - 4)
                    dve.tensor_scalar(rq[:, t % 2, 0, :], rn[:, t % 2, 0:LH], QK_SCALE, None, ALU.mult)
                    then(dve.tensor_scalar(rq[:, t % 2, 1, :], rn[:, t % 2, 0:LH], -QK_SCALE, None, ALU.mult))

                def maximum(q):
                    t, pair = divmod(q, 4)
                    w = P + (WIN if t % HT else 0)
                    dve.wait_ge(s["sim_ps"], 4 * n0 + q + 1)
                    h = slice(2 * pair, 2 * pair + 2)
                    then(dve.tensor_reduce(mx3[:, t % 2, h],
                                           bank[q % 2][:, 0:384].rearrange("p (h k) -> p h k", h=2)[:, :, 0:w], AX.X, ALU.max))
                    dve.tensor_tensor(nb3[:, t % 2, h], mx3[:, t % 2, h], rq[:, t % 2, 1, h], ALU.mult)\
                        .then_inc(s["nb_ready"], 1)

                def normalise(t):
                    dve.wait_ge(s["pv3_ps"], 4 * (n0 + t) + 4)
                    then(dve.reciprocal(rs3[:, t % 2, :], sum3[:, t % 2, :]))
                    dve.tensor_tensor(on3[:, t, :].rearrange("p (h d) -> p h d", h=LH),
                                      bank[4].rearrange("p (h d) -> p h d", h=LH),
                                      rs3[:, t % 2, :].unsqueeze(2).to_broadcast([P, LH, LD]), ALU.mult)\
                        .then_inc(s["on3_ready"], 1)

                for t in range(2):
                    rotate(t, 0)
                    rotate(t, 1)
                    norms(t)
                query_scale(0)
                maximum(0)
                for q in range(4 * NT):
                    t, pair = divmod(q, 4)
                    if pair == 3 and t + 1 < NT:
                        query_scale(t + 1)
                    if q + 1 < 4 * NT:
                        maximum(q + 1)
                    if q % 2 == 0:
                        dve.wait_ge(s["pT3_ps"], 4 * n0 + q + 1)
                        if q >= 2:
                            dve.wait_ge(s["pv3_ps"], 4 * n0 + q - 1)
                        blk = slice(0 if t % HT else 1, 2)
                        src = bank[2].rearrange("p (h k n) -> p h k n", h=2, k=2)[:, :, blk, :]
                        dve.tensor_copy(pT3[:, 0, :, :].rearrange("p (h k) n -> p h k n", h=2)[:, :, blk, :], src)\
                            .then_inc(s["pT3_even"], 1)
                    if pair == 0 and t > 0:
                        pass
                    if pair == 3:
                        normalise(t)
                    if pair == 0 and t + 2 < NT:
                        rotate(t + 2, 0)
                    if pair == 1 and t + 2 < NT:
                        rotate(t + 2, 1)
                    if pair == 2 and t + 2 < NT:
                        norms(t + 2)
                for t in range(NT + 1):
                    n = n0 + t
                    if t < NT:
                        dve.wait_ge(s["ohi_ready"], n + 1)
                        split_low(o_lo[:, t % 2, :], bank[t % 4], o_hi[:, t % 2, :]).then_inc(s["olo_ready"], 1)
                    if t >= 1:
                        dve.wait_ge(s["o3_out"], n)
                        dve.tensor_tensor(x[:, t - 1, :], x[:, t - 1, :], bank[4 + (t - 1) % 4][:, 0:P], ALU.add)\
                            .then_inc(s["x3_added"], 1)
                dve.wait_ge(s["x3_added"], n0 + NT)
                head(8 + layer, jf, shifted=True)
                feed_forward("geglu", m, [(0, b, c) for b in range(B) for c in range(CH3)], CH3)
                if layer == 1:
                    dve.wait_ge(s["kept_added"], 1)
                for b in range(B):
                    dve.wait_ge(s["yT_ps"], 2 * m + b + 1)
                    dve.tensor_tensor(x_tiles(b), x_tiles(b), bank[2 + b], ALU.add).then_inc(s["x_added"], 1)
                dve.wait_ge(s["x_added"], before[("loc", layer)] + 2)

            dve.wait_ge(s["ld_cst"], 32)
            isq = 1.0 / float(np.sqrt(DK))
            dve.tensor_scalar(tau_s[:, :], vec[:, V_TAU:V_TAU + B * L], isq, None, ALU.mult)
            then(dve.tensor_scalar(del_f[:, :], vec[:, V_DEL:V_DEL + B * L], isq, None, ALU.mult))
            then(dve.tensor_copy(del_h[:, :], del_f[:, :]))
            then(split_low(del_l[:, :], del_f[:, :], del_h[:, :]))
            then(dve.tensor_scalar(del_l[:, :], del_l[:, :], cst[:, C_DM + 1:C_DM + 2], None, ALU.mult))
            then(dve.scalar_tensor_tensor(out=del_x[:, :], in0=del_h[:, :].bitcast(F32), scalar=cst[:, C_DM:C_DM + 1],
                                          in1=del_l[:, :], op0=ALU.mult, op1=ALU.add))
            for b in range(B):
                dve.tensor_copy(k_st[96:P, b, :, :].rearrange("p g (j k) -> p (g j) k", j=HG),
                                del_x[96:P, b * L:(b + 1) * L].unsqueeze(1).to_broadcast([32, H, L]))
            dve.tensor_copy(v_bd[:, :, :, DK], cst[:, C_VM:C_VM + B * NC * H].rearrange("p (c h) -> p c h", h=H))
            dve.wait_ge(s["ld_x"], 16)
            for what, i in order:
                if (what, i) == ("moe", 0):
                    dve.wait_ge(s["ld_rw"], 16)
                    then(dve.tensor_copy(rw_hi[:, :], rw[:, :]))
                    split_low(rw_lo[:, :], rw[:, :], rw_hi[:, :]).then_inc(s["rw_ready"], 1)
                {"att": attention, "moe": routed, "l2x": lambda i: l2_attention(), "loc": local}[what](i)
                if what == "att" and i == 0:
                    dve.wait_ge(s["ld_l2"], 48)
                    pt, index = vec[:, V_PT:V_PT + B], cst[:, C_IO:C_IO + L]
                    dve.tensor_copy(l2s[:, 0:2], slen[:, :])
                    dve.tensor_scalar(l2s[:, 2:4], pt, 16.0, 0.0, ALU.subtract, ALU.max)
                    then(dve.tensor_scalar(l2s[:, 4:6], pt, 16.0, None, ALU.add))
                    then(dve.tensor_tensor(l2s[:, 4:6], l2s[:, 4:6], l2s[:, 0:2], ALU.min))
                    for b in range(B):
                        dve.tensor_scalar(valid[:, b, :], index, l2s[:, 2 + b:3 + b], None, ALU.is_ge)
                        dve.tensor_scalar(neg[:, b, :], index, l2s[:, 4 + b:5 + b], None, ALU.is_le)
                        last = dve.tensor_scalar(gauss[:, b, :], index, pt[:, b:b + 1], None, ALU.subtract)
                    then(last)
                    then(dve.tensor_tensor(valid[:, :, :], valid[:, :, :], neg[:, :, :], ALU.mult))
                    dve.tensor_scalar(neg[:, :, :], valid[:, :, :], 1.0, 1e9, ALU.subtract, ALU.mult)
                    dve.tensor_tensor(gauss[:, :, :], gauss[:, :, :], gauss[:, :, :], ALU.mult).then_inc(s["gauss_d2"], 1)



def constants():
    c = np.zeros((P, NCONST), np.float32)
    r = np.arange(P)
    c[r, C_ID + r] = 1.0
    for j in range(HG):
        c[:96, C_KM + j] = (r[:96] % 32) // DK == j
    c[96, C_DM] = 1.0
    c[97, C_DM + 1] = 1.0
    for k in range(B * NC):
        flat = (k % NC) * P + r
        for h in range(H):
            c[:, C_VM + k * H + h] = flat // L == h
    c[:, C_IO:C_IO + L + 1] = np.arange(L + 1)
    c[r[:-1], C_SH + r[1:]] = 1.0
    c[P - 1, C_SE] = 1.0
    i, j = r[:, None], np.arange(P + WIN)[None, :]
    c[:, C_MS:C_MS + P + WIN] = np.where((j >= i) & (j <= i + WIN), 0.0, -1e30)
    return c


def rotary():
    f = np.float32
    half_idx = np.arange(0, LD, 2, dtype=f)
    inv = (f(1.0) / f(10000.0) ** (half_idx / f(LD))).astype(f)
    t = np.arange(S, dtype=f)
    freqs = t[:, None] * inv[None, :]
    freqs = np.concatenate([freqs, freqs], -1)
    base = (half_idx + f(0.4 * LD)) / f(1.4 * LD)
    power = (t - f(S // 2)) / f(WIN // 2)
    scale = np.power(base[None, :].astype(f), power[:, None]).astype(f)
    scale = np.concatenate([scale, scale], -1)
    sign = np.concatenate([-np.ones(LD // 2, f), np.ones(LD // 2, f)])
    cos, sin = np.cos(freqs), np.sin(freqs) * sign
    tabs = np.stack([cos * scale, sin * scale, cos / scale, sin / scale]).astype(f)
    return np.ascontiguousarray(tabs.reshape(4, HT, P, LD).transpose(2, 0, 1, 3))


def lay_out(a):
    f = np.float32
    d = {"consts": constants(), "rope": rotary()}
    d["x"] = a["x"].reshape(NT, P, P).transpose(1, 0, 2)
    c = a["ctx_1024"]
    cT = c.transpose(2, 0, 1)
    d["ctxT"] = cT.reshape(P, B * L)
    rep = np.zeros((P, B, NC * P), f)
    rep[:, :, :H * L] = np.tile(cT, (1, 1, H))
    d["ctx_rep"] = rep
    d["ctx_n"] = c.transpose(1, 0, 2)
    att = ("L0", "L1", "L3")
    aw = np.zeros((P, 3, 1024), f)
    vec = np.zeros((P, NVEC), f)
    rows = np.zeros((1, NROW), f)

    def stack(w):
        return np.repeat(w.reshape(-1, G, 1, 32), 3, axis=2).reshape(-1, G * 96)

    for i, n in enumerate(att):
        g = lambda k: a[f"{n}_xcond_{k}"]
        aw[:, i, 0:384] = stack(g("Wq").T)
        aw[:, i, 384:768] = stack(g("Wk").T)
        aw[:, i, 768:896] = g("Wv").T
        aw[:, i, 896:1024] = g("Wo").T
        vec[0:96, V_BQ + G * i:V_BQ + G * i + G] = stack(g("bq")[None, :]).reshape(G, 96).T
        vec[0:96, V_BK + G * i:V_BK + G * i + G] = stack(g("bk")[None, :]).reshape(G, 96).T
        vec[:, V_BV + i] = g("bv")
        rows[0, i * P:(i + 1) * P] = g("bo")
    d["aw"], d["rows"] = aw, rows
    vec[:, V_B1:V_B1 + 32] = a["L0_ffn_b1"].reshape(32, P).T
    vec[:, V_B2:V_B2 + 8] = a["L0_ffn_b2"].T
    vec[:, V_LG:V_LG + DEPTH] = a["L3_ffn_ln_g"].T
    vec[:, V_LB:V_LB + DEPTH] = a["L3_ffn_ln_b"].T
    hid = a["L3_ffn_b1"].shape[1] // 2
    pad = np.zeros((DEPTH, 2, CH3 * P), f)
    pad[:, :, :hid] = a["L3_ffn_b1"].reshape(DEPTH, 2, hid)
    vec[:, V_B1A:V_B1A + DEPTH * CH3] = pad[:, 0].reshape(DEPTH * CH3, P).T
    vec[:, V_B1G:V_B1G + DEPTH * CH3] = pad[:, 1].reshape(DEPTH * CH3, P).T
    vec[:, V_B23:V_B23 + DEPTH] = a["L3_ffn_b2"].T
    vec[:, V_TAU:V_TAU + B * L] = np.repeat(a["condB_tau"], L)[None, :]
    vec[:, V_DEL:V_DEL + B * L] = a["fside_BxS2_0"].reshape(1, B * L)
    vec[:, V_PT:V_PT + B] = a["condB_pt"][None, :]
    vec[:, V_RB:V_RB + 7] = a["L2_ffn_rb"][None, :]
    for layer in range(DEPTH):
        for k, name in enumerate(("q_scale", "k_scale")):
            v = a[f"L3_ffn_{name}"][layer]
            o = V_QS + (4 * layer + 2 * k) * LD
            vec[:, o:o + LD] = v[None, :]
            vec[:, o + LD:o + 2 * LD] = np.concatenate([v[LD // 2:], v[:LD // 2]])[None, :]
    d["vec"] = vec
    rw = np.zeros((P, 32), f)
    rw[:, 0:8] = a["L0_ffn_Wr"]
    rw[:, 8:24] = a["L1_ffn_router_w"].T
    rw[:, 24:31] = a["L2_ffn_wr"].T
    d["rw"] = rw
    wc = a["L2_xcond_W_c"].T
    d["l2w"] = np.concatenate([a["L2_xcond_W_a"].T, wc[:P], wc[P:]], axis=1)
    d["slen"] = np.repeat(a["_lenS2"][None, :], P, axis=0)
    w2 = a["L0_ffn_W2"].reshape(8, 4, P, P).transpose(0, 2, 1, 3).reshape(8, P, 4 * P)
    d["w0"] = np.concatenate([a["L0_ffn_W1"], w2], axis=2)
    w = np.zeros((20, P, 384), f)
    w[4:, :, 0:256] = a["L1_ffn_gate_up_proj"]
    w[4:, :, 256:384] = a["L1_ffn_down_proj"]
    for e in range(4):
        r = slice(e * P, (e + 1) * P)
        w[e, :, 0:128] = a["L1_ffn_shared_gate_w"][r].T
        w[e, :, 128:256] = a["L1_ffn_shared_up_w"][r].T
        w[e, :, 256:384] = a["L1_ffn_shared_down_w"][:, r].T
    d["w1"] = w
    w = np.zeros((8, P, 1088), f)
    for e in range(8):
        gw, uw, dw = ((a["L2_ffn_sg"], a["L2_ffn_su"], a["L2_ffn_sd"]) if e == 0 else
                      (a["L2_ffn_rg"][e - 1], a["L2_ffn_ru"][e - 1], a["L2_ffn_rd"][e - 1]))
        w[e, :, 0:352] = gw.T
        w[e, :, 352:704] = uw.T
        for k in range(3):
            part = dw[:, k * P:(k + 1) * P].T
            w[e, :part.shape[0], 704 + k * P:704 + (k + 1) * P] = part
    d["w2"] = w
    w = np.zeros((DEPTH, P, L3W), f)
    w[:, :, 0:3 * INNER] = a["L3_ffn_wqkv"]
    w[:, :, 3 * INNER:4 * INNER] = a["L3_ffn_wo"].reshape(DEPTH, 4, P, P).transpose(0, 2, 1, 3).reshape(DEPTH, P, INNER)
    w[:, :, 4 * INNER:4 * INNER + hid] = a["L3_ffn_w1"][:, :, :hid]
    w[:, :, 4 * INNER + CH3 * P:4 * INNER + CH3 * P + hid] = a["L3_ffn_w1"][:, :, hid:]
    w2 = np.zeros((DEPTH, CH3 * P, P), f)
    w2[:, :hid] = a["L3_ffn_w2"]
    w[:, :, 4 * INNER + 2 * CH3 * P:] = w2.reshape(DEPTH, CH3, P, P).transpose(0, 2, 1, 3).reshape(DEPTH, P, CH3 * P)
    d["w3"] = w
    return {k: np.ascontiguousarray(v) for k, v in d.items()}


STAGES = 9


def kernel(**inputs):
    import concourse.bacc as bacc
    from concourse.bass_utils import run_bass_kernel_spmd

    nc = bacc.Bacc("TRN2", target_bir_lowering=False, num_devices=1)
    arrays = {f"in_{k}": v for k, v in lay_out({k: np.asarray(v) for k, v in inputs.items()}).items()}
    d = {k[3:]: nc.dram_tensor(k, v.shape, mybir.dt.from_np(v.dtype), kind="ExternalInput").ap() for k, v in arrays.items()}
    out = nc.dram_tensor("out", (P, NT, P), F32, kind="ExternalOutput").ap()
    build(nc, d, out, STAGES)
    r = run_bass_kernel_spmd(nc, [arrays], core_ids=[0])
    return np.asarray(r.results[0]["out"]).transpose(1, 0, 2).reshape(B, S, P)
```

```python
from contextlib import ExitStack

import numpy as np
import concourse.bass as bass
from concourse import mybir

F32 = mybir.dt.float32
F32R = mybir.dt.float32r
BF16 = mybir.dt.bfloat16
U32 = mybir.dt.uint32
I32 = mybir.dt.int32
ACT = mybir.ActivationFunctionType
ALU = mybir.AluOpType
AX = mybir.AxisListType

P = 128
B = 2
S = 512
T = B * S
NT = T // P
HT = NT // B
L = 77
EPS = 1e-5

H = 16
DK = P // H
G = 4
HG = H // G
GW = HG * L
NC = -(-H * L // P)
VW = H * (DK + 1)
VG = B * NC // 4

RING = 3
WMAX = 1088
UB = 4

LH = 8
LD = 64
INNER = LH * LD
WIN = 64
QK_SCALE = 8.0
DEPTH = 2
CH3 = 3
L3W = 3 * INNER + 4 * P + 2 * CH3 * P + CH3 * P

C_ID = 0
C_KM = C_ID + P
C_DM = C_KM + HG
C_VM = C_DM + 2
C_IO = C_VM + B * NC * H
C_SH = C_IO + L + 1
C_SE = C_SH + P
C_MS = C_SE + P
NCONST = C_MS + P + WIN

V_BQ = 0
V_BK = V_BQ + 3 * G
V_BV = V_BK + 3 * G
V_B1 = V_BV + 3
V_B2 = V_B1 + 32
V_LG = V_B2 + 8
V_LB = V_LG + DEPTH
V_B1A = V_LB + DEPTH
V_B1G = V_B1A + DEPTH * CH3
V_B23 = V_B1G + DEPTH * CH3
V_TAU = V_B23 + DEPTH
V_DEL = V_TAU + B * L
V_PT = V_DEL + B * L
V_RB = V_PT + B
V_QS = V_RB + 8
NVEC = V_QS + DEPTH * 4 * LD
NROW = 3 * P

MOE = ("gelu", "top1", "top2")


def moe_plan():
    plans = []
    first = 0
    for kind, experts, chunks in (("gelu", 8, 4), ("top1", 4 + 16, 1), ("top2", 8, 3)):
        units = [(e, b, c) for e in range(experts) for b in range(B) for c in range(chunks)]
        plans.append(dict(kind=kind, experts=experts, chunks=chunks, first=first, units=units))
        first += experts
    return plans, first


class Count:

    def __init__(self, engine, semaphore):
        self.engine, self.semaphore, self.value = engine, semaphore, 0

    def done(self, instruction):
        self.value += 1
        instruction.then_inc(self.semaphore, 1)

    def wait(self):
        self.engine.wait_ge(self.semaphore, self.value)


def build(nc, d, out, stages):
    plans, n_ring = moe_plan()
    ctx = ExitStack()
    with ctx:
        def sb(name, shape, dt=F32, where=None):
            return (where or ctx).enter_context(nc.sbuf_tensor(name, shape, dt))

        def sem(name):
            return ctx.enter_context(nc.semaphore(name))

        ps = ctx.enter_context(nc.psum_tensor("ps", [P, 8, S], F32))
        bank = [ps[:, i, :] for i in range(8)]

        x = sb("x", [P, NT, P])
        xn = sb("xn", [P, NT, P])
        x_hi = sb("x_hi", [P, T], F32R)
        x_lo = sb("x_lo", [P, T], F32R)
        cst = sb("cst", [P, NCONST])
        vec = sb("vec", [P, NVEC])
        ident = cst[:, C_ID:C_ID + P]
        stats = sb("stats", [P, NT, 12])
        mv = sb("mv", [P, NT, 2])
        ve = sb("ve", [P, NT])
        rstd = sb("rstd", [P, NT])
        mhalf = sb("mhalf", [P, 16])
        gate = sb("gate", [P, 3, S])
        prod = sb("prod", [P, 3, S])
        a_hi = sb("a_hi", [P, UB, S], F32R)
        a_lo = sb("a_lo", [P, UB, S], F32R)
        acc = sb("acc", [P, T])
        ytmp = sb("ytmp", [P, 2, S])

        early = ExitStack()
        w_raw = sb("w_raw", [P, RING, WMAX], F32, early)
        w_hi = sb("w_hi", [P, RING, WMAX], F32R, early)
        w_lo = sb("w_lo", [P, RING, WMAX], F32R, early)
        rows = sb("rows", [1, NROW], F32, early)
        ones = sb("ones", [1, P], F32, early)
        aw = sb("aw", [P, 3, 1024], F32, early)
        ctxT = sb("ctxT", [P, B * L], F32, early)
        ctx_rep = sb("ctx_rep", [P, B, NC * P], F32, early)
        wq_hi = sb("wq_hi", [P, G * 96], F32R, early)
        wq_lo = sb("wq_lo", [P, G * 96], F32R, early)
        wo_hi = sb("wo_hi", [P, P], F32R, early)
        wo_lo = sb("wo_lo", [P, P], F32R, early)
        tau_s = sb("tau_s", [P, B * L], F32, early)
        del_f = sb("del_f", [P, B * L], F32, early)
        del_h = sb("del_h", [P, B * L], F32R, early)
        del_l = sb("del_l", [P, B * L], F32, early)
        del_x = sb("del_x", [P, B * L], F32, early)
        k_f = sb("k_f", [96, G, B * L], F32, early)
        k_x = sb("k_x", [96, G, B * L], F32R, early)
        k_st = sb("k_st", [P, B, G, GW], F32R, early)
        v_bd = sb("v_bd", [P, B * NC, H, DK + 1], F32, early)
        brow = sb("brow", [1, P], F32, early)
        rw_hi = sb("rw_hi", [P, 32], F32R, early)
        rw_lo = sb("rw_lo", [P, 32], F32R, early)
        rw = sb("rw", [P, 32], F32, early)
        l2w = sb("l2w", [P, 3 * P], F32, early)
        ctx_n = sb("ctx_n", [L, B, P], F32, early)
        slen = sb("slen", [P, B], I32, early)
        l2s = sb("l2s", [P, 8], F32, early)
        valid = sb("valid", [P, B, L], F32, early)
        gauss = sb("gauss", [P, B, L], F32, early)
        neg = sb("neg", [P, B, L], F32, early)

        att = ExitStack()
        qs = sb("qs", [P, G, T], F32R, att)
        e_sb = sb("e_sb", [P, 2, NC * P], F32, att)
        pT = sb("pT", [P, 2, NC * P], F32, att)
        mx = sb("mx", [P, 2, H], F32, att)
        rsum = sb("rsum", [P, 2, H], F32, att)
        on = sb("on", [P, NT, P], F32, att)
        oT_hi = sb("oT_hi", [P, S], F32R, att)
        oT_lo = sb("oT_lo", [P, S], F32R, att)
        att.close()
        l2x = ExitStack()
        wc_hi = sb("wc_hi", [P, 2 * P], F32R, l2x)
        wc_lo = sb("wc_lo", [P, 2 * P], F32R, l2x)
        m_hi = sb("m_hi", [P, B, 78], F32R, l2x)
        m_lo = sb("m_lo", [P, B, 78], F32R, l2x)
        sc = sb("sc", [P, NT, L], F32, l2x)
        sc2 = sb("sc2", [P, NT, L], F32, l2x)
        l2m = sb("l2m", [P, 3, NT], F32, l2x)
        alT = sb("alT", [L, B, S], F32, l2x)
        c_hi = sb("c_hi", [P, B, S], F32R, l2x)
        c_lo = sb("c_lo", [P, B, S], F32R, l2x)
        th = sb("th", [P, B, S], F32, l2x)
        l2x.close()
        moe = ExitStack()
        lg = sb("lg", [P, NT, 16], F32, moe)
        pr = sb("pr", [P, NT, 16], F32, moe)
        m8 = sb("m8", [P, NT, 8], F32, moe)
        i8 = sb("i8", [P, NT, 8], U32, moe)
        i8f = sb("i8f", [P, NT, 8], F32, moe)
        sel = sb("sel", [P, 2, NT, 16], F32, moe)
        cw = sb("cw", [P, NT, 16], F32, moe)
        sm = sb("sm", [P, 4, NT], F32, moe)
        cT = sb("cT", [16, T], F32, moe)
        crow = sb("crow", [P, 4, T], F32, moe)
        cB = sb("cB", [P, 2, T], F32, moe)
        moe.close()
        early.close()

        late = ExitStack()
        w3_raw = sb("w3_raw", [P, RING * WMAX], F32, late)
        w3_hi = sb("w3_hi", [P, RING * WMAX], F32R, late)
        w3_lo = sb("w3_lo", [P, RING * WMAX], F32R, late)
        w3b_hi = sb("w3b_hi", [P, L3W - 3 * INNER], F32R, late)
        w3b_lo = sb("w3b_lo", [P, L3W - 3 * INNER], F32R, late)
        ident_b = sb("ident_b", [P, P], BF16, late)
        mask = sb("mask", [P, P + WIN], BF16, late)
        kept = sb("kept", [P, NT, P], F32, late)
        rope_raw = sb("rope_raw", [P, 4, HT, LD], F32, late)
        rope = sb("rope", [P, 4, HT, LD], F32, late)
        kT = sb("kT", [P, 4, T], F32, late)
        qT = sb("qT", [P, 2, LH, P], F32, late)
        v_all = sb("v_all", [P, NT, INNER], F32, late)
        sq = sb("sq", [P, 2, INNER], F32, late)
        r1 = sb("r1", [P, 2, INNER], F32, late)
        r2 = sb("r2", [P, 2, INNER], F32, late)
        qk = sb("qk", [P, 2, 2, INNER], F32, late)
        ssq = sb("ssq", [P, 2, 2 * LH], F32, late)
        rn = sb("rn", [P, 2, 2 * LH], F32, late)
        rq = sb("rq", [P, 2, 2, LH], F32, late)
        mx3 = sb("mx3", [P, 2, LH], F32, late)
        nb3 = sb("nb3", [P, 2, LH], F32, late)
        sum3 = sb("sum3", [P, 2, LH], F32, late)
        rs3 = sb("rs3", [P, 2, LH], F32, late)
        p3 = sb("p3", [P, 2, 2, 2 * P], F32, late)
        pT3 = sb("pT3", [P, 2, 4, P], F32, late)
        on3 = sb("on3", [P, 2, INNER], F32, late)
        o_hi = sb("o_hi", [P, 2, INNER], F32R, late)
        o_lo = sb("o_lo", [P, 2, INNER], F32R, late)
        late.close()

        s = {n: sem(n) for n in (
            "ld_cst", "ld_x", "ld_ctx", "ld_aw", "ld_aw_more", "ld_rw", "ld_l2", "ld_w0", "ld_w1", "ld_w2", "ld_row", "ld_w3", "ld_rope",
            "stored",
            "dve_step", "act_step", "pool_step",
            "pool_set", "gauss_d2", "gauss_ready", "rw_ready",
            "ve_ready", "rstd_ready", "xn_ready", "xT_ps", "xhi_ready", "xlo_ready",
            "k_ps", "k_ready", "v_ps", "v_taken", "v_ready", "brow_ready", "wsplit",
            "q_ps", "q_hi", "q_lo", "score_ps", "sub_done", "exp_done", "pt_ps", "pt_ready", "pv_ps", "on_ready",
            "oT_ps", "oT_hi_ready", "oT_lo_ready", "ao_ps", "x_added",
            "m_ps", "m_ready", "s_ps", "s_sub", "s_exp", "al_ready", "al_ps", "alT_ready", "c_ps", "chi_ready",
            "clo_ready", "t_ps", "tanh_ready",
            "lg_ps", "rt_sub", "rt_exp", "cw_ready", "cT_ps", "cT_ready", "cb_ready",
            "whi_ready", "wlo_ready", "hid_ps", "scaled", "gate_ready", "prod_ready", "ahi_ready", "alo_ready",
            "out_ps", "y_taken", "acc_added", "yT_ps",
            "w3hi_ready", "w3lo_ready", "rope_ready", "q3_ps", "k3_ps", "v3_ps", "sq_ready", "v3_ready", "rot_ready", "kr_ready",
            "ssq_ready", "qk_ready", "qkT_ps", "qkT_ready", "sim_ps", "nb_ready", "p3_ready",
            "pT3_ps", "pT3_even", "pT3_odd", "pv3_ps", "on3_ready", "o3_ps", "ohi_ready", "olo_ready", "o3_out", "x3_added",
            "shift_ps", "hF_ready", "kept", "kept_added",
        )}
        s_w = [s["ld_w0"], s["ld_w1"], s["ld_w2"]]


        ATT_HEAD = (0, 2, 6)
        MOE_HEAD = (1, 3, 5)
        L2_HEAD = 4
        order = [("att", 0), ("moe", 0), ("att", 1), ("moe", 1), ("l2x", 0), ("moe", 2), ("att", 2),
                 ("loc", 0), ("loc", 1)][:stages]
        n_ring = sum(p["experts"] for m, p in enumerate(plans) if ("moe", m) in order)
        WIDTH = (1024, 384, 1088)
        before = {st: 2 * n for n, st in enumerate(order)}
        n_units = [len(p["units"]) for p in plans]
        unit_base = [sum(n_units[:m]) for m in range(3)] + [sum(n_units), sum(n_units) + B * CH3]
        prod_base = [0, 0, n_units[1], n_units[1] + n_units[2], n_units[1] + n_units[2] + B * CH3]
        group_base = [0, 16, 20, 36, 38]
        cb_base = [0, 8, 24]
        units_through = {}
        for m, p in enumerate(plans):
            for e in range(p["experts"]):
                units_through[p["first"] + e] = unit_base[m] + (e + 1) * B * p["chunks"]
        V_BANK = (0, 1, 2, 3, 7)
        OT_BANK, AO_BANK = (6, 0), (6, 1)
        v_stage = [ytmp[:, 0, :], ytmp[:, 1, :], gate[:, 0, :], gate[:, 1, :], gate[:, 2, :]]
        ahead = {i: MOE_HEAD[m] for i, m in ((0, 0), (1, 1)) if ("moe", m) in order}
        LAG = {"gelu": 2, "top1": 3, "top2": 2, "geglu": 2}

        def half(t, b):
            return t[:, b * S:(b + 1) * S]

        def tiles(b):
            return range(HT * b, HT * (b + 1))

        def first_of_group(kind, e, c):
            return c == 0 and (kind != "top1" or e in (0, 4))

        def last_of_group(kind, chunks, e, c):
            return c == chunks - 1 and (kind != "top1" or e in (3, 19))

        def group_of(kind, e, b):
            if kind == "top1":
                return (0 if e < 4 else 2) + b
            return 2 * e + b

        def rows_of(kind, c):
            return 96 if kind == "top2" and c == 2 else P

        def hid_cols(kind, c, up):
            if kind == "gelu":
                return c * P
            if kind == "top1":
                return up * P
            return up * 352 + c * P

        def out_cols(kind, c):
            return {"gelu": 512, "top1": 256, "top2": 704}[kind] + c * P

        def w3_parts(layer, c0, width):
            if layer == 1 and c0 >= 3 * INNER:
                w = slice(c0 - 3 * INNER, c0 - 3 * INNER + width)
                return w3b_hi[:, w], w3b_lo[:, w]
            return w3_hi[:, c0:c0 + width], w3_lo[:, c0:c0 + width]

        block = ctx.enter_context(nc.Block())

        @block.sync
        def _(sp):
            sp.dma_start(cst[:, :], d["consts"]).then_inc(s["ld_cst"], 16)
            sp.dma_start(x[:, :, :], d["x"]).then_inc(s["ld_x"], 16)
            sp.dma_start(vec[:, :], d["vec"]).then_inc(s["ld_cst"], 16)
            sp.dma_start(ctxT[:, :], d["ctxT"]).then_inc(s["ld_ctx"], 16)
            sp.dma_start(aw[:, 0, :], d["aw"][:, 0, :]).then_inc(s["ld_aw"], 16)
            sp.dma_start(ctx_rep[:, :, :], d["ctx_rep"]).then_inc(s["ld_ctx"], 16)
            sp.dma_start(rows[:, :], d["rows"]).then_inc(s["ld_ctx"], 16)
            sp.dma_start(rw[:, :], d["rw"]).then_inc(s["ld_rw"], 16)
            sp.dma_start(aw[:, 1:3, :], d["aw"][:, 1:3, :]).then_inc(s["ld_aw_more"], 16)
            sp.dma_start(l2w[:, :], d["l2w"]).then_inc(s["ld_l2"], 16)
            sp.dma_start(ctx_n[:, :, :], d["ctx_n"]).then_inc(s["ld_l2"], 16)
            sp.dma_start(slen[:, :], d["slen"]).then_inc(s["ld_l2"], 16)
            for n in range(n_ring):
                if n >= RING:
                    sp.wait_ge(s["wlo_ready"], n - RING + 1)
                m = 0 if n < 8 else 1 if n < 28 else 2
                width = WIDTH[m]
                src = d["w" + str(m)][n - plans[m]["first"]]
                sp.dma_start(w_raw[:, n % RING, 0:width], src).then_inc(s_w[n % RING], 16)
            for layer in range(DEPTH):
                if ("loc", layer) not in order:
                    continue
                if layer == 0:
                    sp.wait_ge(s["wlo_ready"], n_ring)
                    sp.wait_ge(s["out_ps"], sum(n_units))
                else:
                    sp.wait_ge(s["w3lo_ready"], 2)
                sp.dma_start(w3_raw[:, 0:3 * INNER], d["w3"][layer, :, 0:3 * INNER]).then_inc(s["ld_w3"], 16)
                sp.dma_start(w3_raw[:, 3 * INNER:L3W], d["w3"][layer, :, 3 * INNER:L3W]).then_inc(s["ld_w3"], 16)
                if layer == 0:
                    sp.wait_ge(s["x_added"], before[("loc", 0)])
                    sp.dma_start(rope_raw[:, :, :, :], d["rope"]).then_inc(s["ld_rope"], 16)
            for b in range(B):
                sp.wait_ge(s["x_added"], 2 * len(order) - B + b + 1)
                sp.dma_start(out[:, 4 * b:4 * b + 4, :], x[:, 4 * b:4 * b + 4, :]).then_inc(s["stored"], 16)
            sp.wait_ge(s["stored"], 16 * B)

        @block.tensor
        def _(pe):
            def three(dst, a_h, a_l, b_h, b_l, start=True, stop=True):
                pe.matmul(dst, a_h, b_h, start=start, stop=False)
                pe.matmul(dst, a_l, b_h, start=False, stop=False)
                return pe.matmul(dst, a_h, b_l, start=False, stop=stop)

            def turn_x(ln, jx, b):
                pe.wait_ge(s["xn_ready"], 2 * ln + b + 1)
                for k, t in enumerate(tiles(b)):
                    last = pe.transpose(bank[6 + b][:, k * P:(k + 1) * P], xn[:, t, :], ident)
                last.then_inc(s["xT_ps"], 1)

            def head(ln, jx, halves=range(B)):
                for b in halves:
                    turn_x(ln, jx, b)

            def attention(i):
                j = ATT_HEAD[i]
                if i == 0:
                    pe.wait_ge(s["ld_cst"], 32)
                    pe.wait_ge(s["ld_ctx"], 48)
                    pe.wait_ge(s["pool_set"], 2)
                else:
                    pe.wait_ge(s["x_added"], before[("att", i)])
                pe.wait_ge(s["ld_aw" if i == 0 else "ld_aw_more"], 16)
                for g in range(G):
                    pe.matmul(bank[4 + g // 3][0:96, (g % 3) * B * L:(g % 3 + 1) * B * L],
                              aw[:, i, 384 + 96 * g:480 + 96 * g], ctxT[:, :], start=True, stop=True)
                pe.matmul(bank[5][0:1, 2 * P:3 * P], vec[:, V_BV + i:V_BV + i + 1], aw[:, i, 896:1024],
                          start=True, stop=True).then_inc(s["k_ps"], 1)
                for vg in range(VG):
                    for q in range(4):
                        c = 4 * vg + q
                        last = pe.matmul(bank[V_BANK[vg]][:, q * P:(q + 1) * P],
                                         ctx_rep[:, c // NC, (c % NC) * P:(c % NC + 1) * P],
                                         aw[:, i, 768:896], start=True, stop=True)
                    last.then_inc(s["v_ps"], 1)
                pe.wait_ge(s["v_taken"], VG * (i + 1))
                head(j, j)
                def queries(b):
                    pe.wait_ge(s["wsplit"], i + 1)
                    pe.wait_ge(s["xlo_ready"], 2 * j + b + 1)
                    if b == 1:
                        pe.wait_ge(s["k_ready"], i + 1)
                    for g in range(G):
                        w = slice(96 * g, 96 * g + 96)
                        three(bank[4 * b + g][0:96, :], wq_hi[:, w], wq_lo[:, w], half(x_hi, b), half(x_lo, b))\
                            .then_inc(s["q_ps"], 1)

                def scores(t):
                    if t == 0:
                        pe.wait_ge(s["q_lo"], 8 * i + 4)
                        pe.wait_ge(s["k_ready"], i + 1)
                        pe.wait_ge(s["pool_set"], 3 + i)
                    else:
                        pe.wait_ge(s["q_lo"], 8 * i + 8)
                        pe.wait_ge(s["sub_done"], NT * i + t)
                    for g in range(G):
                        last = pe.matmul(bank[g][:, 0:GW], qs[:, g, t * P:(t + 1) * P], k_st[:, t // HT, g, :],
                                         start=True, stop=True)
                    last.then_inc(s["score_ps"], 1)

                def turn(t, parts):
                    pe.wait_ge(s["exp_done"], NT * i + t + 1)
                    for k in parts:
                        n = 3 * (NT * i + t) + k
                        if 3 * t + k >= 2:
                            pe.wait_ge(s["pt_ready"], n - 1)
                        for c in range(4 * k, min(4 * k + 4, NC)):
                            last = pe.transpose(bank[4 + n % 2][:, (c % 4) * P:(c % 4 + 1) * P],
                                                e_sb[:, t % 2, c * P:(c + 1) * P], ident)
                        last.then_inc(s["pt_ps"], 1)

                def values(t):
                    pe.wait_ge(s["pt_ready"], 3 * (NT * i + t) + 3)
                    if t == 0:
                        pe.wait_ge(s["v_ready"], VG * (i + 1))
                    if t > 0:
                        pe.wait_ge(s["on_ready"], NT * i + t)
                    for c in range(NC):
                        last = pe.matmul(bank[7][:, 0:VW], pT[:, t % 2, c * P:(c + 1) * P],
                                         v_bd[:, (t // HT) * NC + c, :, :].rearrange("p h d -> p (h d)"),
                                         start=(c == 0), stop=(c == NC - 1))
                    last.then_inc(s["pv_ps"], 1)

                def turn_out(b):
                    pe.wait_ge(s["on_ready"], NT * i + HT * b + HT)
                    for k, t in enumerate(tiles(b)):
                        last = pe.transpose(bank[OT_BANK[b]][:, k * P:(k + 1) * P], on[:, t, :], ident)
                    last.then_inc(s["oT_ps"], 1)

                def project(b):
                    pe.wait_ge(s["brow_ready"], i + 1)
                    if b == 0:
                        pe.wait_ge(s["oT_lo_ready"], 2 * i + 1)
                    for k in range(HT):
                        c = slice(k * P, (k + 1) * P)
                        pe.matmul(bank[AO_BANK[b]][:, c], ones[:, :], brow[:, :], start=True, stop=False)
                        if k == 0:
                            pe.wait_ge(s["oT_lo_ready"], 2 * i + b + 1)
                        last = three(bank[AO_BANK[b]][:, c], oT_hi[:, c], oT_lo[:, c], wo_hi[:, :], wo_lo[:, :], start=False)
                    last.then_inc(s["ao_ps"], 1)

                queries(0)
                scores(0)
                queries(1)
                for t in range(NT):
                    if t + 1 < NT:
                        scores(t + 1)
                    turn(t, (0, 1))
                    if t > 0:
                        values(t - 1)
                    turn(t, (2,))
                    if t == 5:
                        turn_out(0)
                    if t == 6:
                        project(0)
                values(NT - 1)
                if i in ahead:
                    pe.wait_ge(s["x_added"], before[("att", i)] + 1)
                    turn_x(ahead[i], ahead[i], 0)
                turn_out(1)
                project(1)

            def feed_forward(kind, m, jx, units, chunks, hid_w, out_w):
                lag, ub, gb = LAG[kind], unit_base[m], group_base[m]
                for n in range(len(units) + lag):
                    if n < len(units):
                        e, b, c = units[n]
                        r = rows_of(kind, c)
                        if kind == "geglu":
                            pe.wait_ge(s["xlo_ready"], 2 * jx + b + 1)
                            if n == 2:
                                turn_x(m + 5, jx, 1)
                                pe.wait_ge(s["hF_ready"], 2 * (m - 3) + 2)
                        else:
                            pe.wait_ge(s["wlo_ready"], plans[m]["first"] + e + 1)
                        if n >= 3 and kind == "gelu":
                            pe.wait_ge(s["gate_ready"], ub + n - 2)
                        elif n >= 3:
                            pe.wait_ge(s["prod_ready"], prod_base[m] + n - 2)
                        for up in range(1 if kind == "gelu" else 2):
                            h, lo = hid_w(e, c, up)
                            last = three(bank[2 + 2 * (n % 3) + up][0:r, :], h, lo, half(x_hi, b), half(x_lo, b))
                        last.then_inc(s["hid_ps"], 1)
                    if n == 2 and kind != "geglu":
                        pe.wait_ge(s["cw_ready"], m + 1)
                        ne = 16 if kind == "top1" else 8
                        for hb in range(B):
                            for k, t in enumerate(tiles(hb)):
                                last = pe.transpose(bank[hb][0:ne, k * P:(k + 1) * P], cw[:, t, 0:ne], ident)
                            last.then_inc(s["cT_ps"], 1)
                    if n >= lag:
                        u = n - lag
                        e, b, c = units[u]
                        r = rows_of(kind, c)
                        pe.wait_ge(s["alo_ready"], ub + u + 1)
                        first = first_of_group(kind, e, c)
                        if first:
                            before_it = group_of(kind, e, b) - 2
                            if before_it >= 0 and kind != "geglu":
                                pe.wait_ge(s["y_taken"], gb + before_it + 1)
                            elif kind != "geglu":
                                pe.wait_ge(s["cT_ready"], 2 * m + 2)
                        h, lo = out_w(e, c, r)
                        k = (ub + u) % UB
                        three(bank[b], h, lo, a_hi[0:r, k, :], a_lo[0:r, k, :], start=first,
                              stop=last_of_group(kind, chunks, e, c)).then_inc(s["out_ps"], 1)

            def routed(m):
                p = plans[m]
                kind, jx = p["kind"], MOE_HEAD[m]
                ne, r0 = ((8, 0), (16, 8), (8, 24))[m]

                def router(b):
                    pe.wait_ge(s["xlo_ready"], 2 * jx + b + 1)
                    for t in tiles(b):
                        c = slice(t * P, (t + 1) * P)
                        last = three(bank[0][:, t * ne:(t + 1) * ne], x_hi[:, c], x_lo[:, c],
                                     rw_hi[:, r0:r0 + ne], rw_lo[:, r0:r0 + ne])
                    last.then_inc(s["lg_ps"], 1)

                pe.wait_ge(s["rw_ready"], 1)
                if m in (0, 1):
                    router(0)
                    head(jx, jx, (1,))
                else:
                    head(jx, jx)
                    router(0)
                router(1)

                def hid_w(e, c, up):
                    slot, c0 = (p["first"] + e) % RING, hid_cols(kind, c, up)
                    w = slice(c0, c0 + rows_of(kind, c))
                    return w_hi[:, slot, w], w_lo[:, slot, w]

                def out_w(e, c, r):
                    slot, c0 = (p["first"] + e) % RING, out_cols(kind, c)
                    return w_hi[0:r, slot, c0:c0 + P], w_lo[0:r, slot, c0:c0 + P]

                feed_forward(kind, m, jx, p["units"], p["chunks"], hid_w, out_w)
                for b in range(B):
                    if kind == "top1":
                        pe.wait_ge(s["y_taken"], group_base[m] + 3 + b)
                        pe.wait_ge(s["prod_ready"], prod_base[m] + n_units[m])
                    else:
                        pe.wait_ge(s["acc_added"], 14 * (m // 2) + 13 + b)
                    for k in range(HT):
                        last = pe.transpose(bank[2 + b][:, k * P:(k + 1) * P], acc[:, (HT * b + k) * P:(HT * b + k + 1) * P], ident)
                    if kind == "top1":
                        for k in range(HT):
                            last = pe.transpose(bank[4 + b][:, k * P:(k + 1) * P], ytmp[:, b, k * P:(k + 1) * P], ident)
                    last.then_inc(s["yT_ps"], 1)

            def l2_attention():
                j = L2_HEAD
                pe.wait_ge(s["ld_l2"], 48)
                pe.wait_ge(s["x_added"], before[("l2x", 0)])
                pe.matmul(bank[4][:, 0:B * L], l2w[:, 0:P], ctxT[:, :], start=True, stop=True).then_inc(s["m_ps"], 1)
                head(j, j)
                pe.wait_ge(s["m_ready"], 1)
                for b in range(B):
                    pe.wait_ge(s["xlo_ready"], 2 * j + b + 1)
                    for k, t in enumerate(tiles(b)):
                        c = slice(t * P, (t + 1) * P)
                        last = three(bank[b][:, k * 78:(k + 1) * 78], x_hi[:, c], x_lo[:, c], m_hi[:, b, :], m_lo[:, b, :])
                    last.then_inc(s["s_ps"], 1)
                for b in range(B):
                    pe.wait_ge(s["al_ready"], b + 1)
                    for k, t in enumerate(tiles(b)):
                        last = pe.transpose(bank[2 + b][0:L, k * P:(k + 1) * P], sc2[:, t, :], ident)
                    last.then_inc(s["al_ps"], 1)
                    pe.wait_ge(s["alT_ready"], b + 1)
                    pe.matmul(bank[4 + b], ctx_n[:, b, :], alT[:, b, :], start=True, stop=True).then_inc(s["c_ps"], 1)
                for b in range(B):
                    pe.wait_ge(s["clo_ready"], b + 1)
                    for k, t in enumerate(tiles(b)):
                        c, c0 = slice(t * P, (t + 1) * P), slice(k * P, (k + 1) * P)
                        three(bank[6 + b][:, c0], c_hi[:, b, c0], c_lo[:, b, c0], wc_hi[:, 0:P], wc_lo[:, 0:P], stop=False)
                        last = three(bank[6 + b][:, c0], x_hi[:, c], x_lo[:, c], wc_hi[:, P:2 * P], wc_lo[:, P:2 * P],
                                     start=False)
                    last.then_inc(s["t_ps"], 1)

            def local(layer):
                m = 3 + layer
                ja, jf = 7 + 2 * layer, 8 + 2 * layer
                for b in range(B):
                    pe.wait_ge(s["x_added"], before[("loc", layer)] - (B - 1 - b if layer else 0))
                    if layer == 0:
                        pe.wait_ge(s["xn_ready"], 2 * 7 + b + 1)
                    for k, t in enumerate(tiles(b)):
                        last = pe.transpose(bank[6 + b][:, k * P:(k + 1) * P], x[:, t, :], ident)
                    last.then_inc(s["xT_ps"], 1)
                n0 = NT * layer

                def proj(t, what):
                    c = slice(t * P, (t + 1) * P)
                    if what == 0:
                        pe.wait_ge(s["xlo_ready"], 2 * ja + (2 if t >= HT or t == 0 else 1))
                        pe.wait_ge(s["w3lo_ready"], 2 * layer + 1)
                        if t > 0:
                            pe.wait_ge(s["v3_ready"], n0 + t)
                    if what == 1 and t > 0:
                        pe.wait_ge(s["kr_ready"], n0 + t)
                    if what == 1 and t > 3:
                        pe.wait_ge(s["x3_added"], n0 + t - 3)
                    if what == 2:
                        pe.wait_ge(s["rot_ready"], n0 + t + 1)
                    three(bank[7 if what == 1 else 6], x_hi[:, c], x_lo[:, c],
                          *w3_parts(layer, what * INNER, INNER))\
                        .then_inc(s[("q3_ps", "k3_ps", "v3_ps")[what]], 1)

                def turn_qk(t, what):
                    if what == 0:
                        pe.wait_ge(s["qk_ready"], n0 + t + 1)
                    if 2 * t + what > 0:
                        pe.wait_ge(s["qkT_ready"], 2 * (n0 + t) + what)
                    if what == 0 and t > 2:
                        pe.wait_ge(s["olo_ready"], n0 + t - 2)
                    for c in range(4):
                        last = pe.transpose(bank[5][:, c * P:(c + 1) * P], qk[:, t % 2, what, c * P:(c + 1) * P], ident)
                    last.then_inc(s["qkT_ps"], 1)

                def sim(q):
                    t, pair = divmod(q, 4)
                    w = P + (WIN if t % HT else 0)
                    g = 4 * n0 + q
                    if pair == 0:
                        pe.wait_ge(s["qkT_ready"], 2 * (n0 + t) + 2)
                    if q >= 2:
                        pe.wait_ge(s["p3_ready"], g - 1)
                    for hh in range(2):
                        dst = bank[q % 2][:, hh * 192:hh * 192 + w]
                        pe.matmul(dst, ident_b[:, :], mask[:, P + WIN - w:P + WIN], start=True, stop=False)
                        last = pe.matmul(dst, qT[:, t % 2, 2 * pair + hh, :], kT[:, pair, (t + 1) * P - w:(t + 1) * P],
                                         start=False, stop=True)
                    last.then_inc(s["sim_ps"], 1)

                def turn_p(q):
                    t, pair = divmod(q, 4)
                    g = 4 * n0 + q
                    pe.wait_ge(s["p3_ready"], g + 1)
                    if q >= 2:
                        pe.wait_ge(s["pT3_odd" if q % 2 else "pT3_even"], g // 2)
                    for hh in range(2):
                        for blk in range(0 if t % HT else 1, 2):
                            k = 2 * hh + blk
                            last = pe.transpose(bank[2 + q % 2][:, k * P:(k + 1) * P],
                                                p3[:, q % 2, hh, blk * P:(blk + 1) * P], ident)
                    last.then_inc(s["pT3_ps"], 1)

                def pv(q):
                    t, pair = divmod(q, 4)
                    g = 4 * n0 + q
                    pe.wait_ge(s["pT3_odd" if q % 2 else "pT3_even"], g // 2 + 1)
                    pe.wait_ge(s["v3_ready"], n0 + t + 1)
                    if pair == 0 and t > 0:
                        pe.wait_ge(s["on3_ready"], n0 + t)
                    for hh in range(2):
                        h = 2 * pair + hh
                        blks = range(0 if t % HT else 1, 2)
                        for blk in blks:
                            last = pe.matmul(bank[4][:, h * LD:(h + 1) * LD], pT3[:, q % 2, 2 * hh + blk, :],
                                             v_all[:, t - 1 + blk, h * LD:(h + 1) * LD],
                                             start=(blk == blks[0]), stop=(blk == 1))
                    last.then_inc(s["pv3_ps"], 1)

                def turn_o(t):
                    pe.wait_ge(s["on3_ready"], n0 + t + 1)
                    pe.wait_ge(s["qkT_ready"], 2 * (n0 + min(t + 2, NT - 1)) + 2)
                    if t > 0:
                        pe.wait_ge(s["olo_ready"], n0 + t)
                    for c in range(4):
                        last = pe.transpose(bank[5][:, c * P:(c + 1) * P], on3[:, t % 2, c * P:(c + 1) * P], ident)
                    last.then_inc(s["o3_ps"], 1)

                def out3(t):
                    pe.wait_ge(s["olo_ready"], n0 + t + 1)
                    pe.wait_ge(s["w3lo_ready"], 2 * layer + 2)
                    pe.wait_ge(s["kr_ready"], n0 + min(t + 4, NT))
                    if t > 0:
                        pe.wait_ge(s["x3_added"], n0 + t)
                    for c in range(4):
                        cc = slice(c * P, (c + 1) * P)
                        last = three(bank[7][:, 0:P], o_hi[:, t % 2, cc], o_lo[:, t % 2, cc],
                                     *w3_parts(layer, 3 * INNER + c * P, P), start=(c == 0), stop=(c == 3))
                    last.then_inc(s["o3_out"], 1)

                def shift(b):
                    pe.wait_ge(s["x3_added"], n0 + HT * (b + 1))
                    if b == 0:
                        pe.wait_ge(s["v3_ready"], n0 + NT)
                    pe.matmul(bank[6 + b][:, 0:HT * 64], cst[:, C_SH:C_SH + P], x[:, HT * b:HT * b + HT, 64:P],
                              start=True, stop=False)
                    pe.matmul(bank[6 + b][:, 64:HT * 64], cst[:, C_SE:C_SE + P], x[:, HT * b:HT * b + HT - 1, 64:P],
                              start=False, stop=True).then_inc(s["shift_ps"], 1)

                pe.wait_ge(s["pool_set"], 6)
                for what in range(3):
                    proj(0, what)
                proj(1, 0)
                proj(1, 1)
                turn_qk(0, 0)
                proj(1, 2)
                turn_qk(0, 1)
                sim(0)
                sim(1)
                proj(2, 0)
                for q in range(4 * NT):
                    t, pair = divmod(q, 4)
                    if q + 2 < 4 * NT and pair != 2:
                        sim(q + 2)
                    turn_p(q)
                    if q + 2 < 4 * NT and pair == 2:
                        sim(q + 2)
                    if q >= 1:
                        pv(q - 1)
                    if pair < 2 and t + 1 < NT:
                        turn_qk(t + 1, pair)
                    if pair == 2 and t > 0:
                        turn_o(t - 1)
                    if pair < 2 and t + 2 < NT:
                        proj(t + 2, 1 + pair)
                    if q == 4 * (NT - 2) + 1:
                        shift(0)
                    if q == 4 * (NT - 1) + 1:
                        turn_x(8 + layer, jf, 0)
                    if pair == 3 and t + 3 < NT:
                        proj(t + 3, 0)
                    if pair == 3 and t > 0:
                        out3(t - 1)
                pv(4 * NT - 1)
                turn_o(NT - 1)
                out3(NT - 1)
                shift(1)

                def hid_w(e, c, up):
                    return w3_parts(layer, 4 * INNER + ((1 - up) * CH3 + c) * P, P)

                def out_w(e, c, r):
                    return w3_parts(layer, 4 * INNER + (2 * CH3 + c) * P, P)

                feed_forward("geglu", m, jf, [(0, b, c) for b in range(B) for c in range(CH3)], CH3, hid_w, out_w)
                for b in range(B):
                    pe.wait_ge(s["y_taken"], group_base[m] + b + 1)
                    for k in range(HT):
                        last = pe.transpose(bank[2 + b][:, k * P:(k + 1) * P], acc[:, (HT * b + k) * P:(HT * b + k + 1) * P], ident)
                    last.then_inc(s["yT_ps"], 1)

            for what, i in order:
                {"att": attention, "moe": routed, "l2x": lambda i: l2_attention(), "loc": local}[what](i)

        @block.scalar
        def _(act):
            step = Count(act, s["act_step"])

            def split_w(n):
                m = 0 if n < 8 else 1 if n < 28 else 2
                act.wait_ge(s_w[n % RING], 16 * (n // RING + 1))
                if n >= RING:
                    act.wait_ge(s["out_ps"], units_through[n - RING])
                act.activation(w_hi[:, n % RING, 0:WIDTH[m]], w_raw[:, n % RING, 0:WIDTH[m]], ACT.Copy)\
                    .then_inc(s["whi_ready"], 1)

            def head(jx, halves=range(B)):
                for b in halves:
                    act.wait_ge(s["xT_ps"], 2 * jx + b + 1)
                    act.activation(half(x_hi, b), bank[6 + b], ACT.Copy).then_inc(s["xhi_ready"], 1)

            def split_w3(layer, part):
                w = (slice(0, 3 * INNER), slice(3 * INNER, L3W))[part]
                act.wait_ge(s["ld_w3"], 32 * (layer + 1))
                act.activation(w3_parts(layer, w.start, w.stop - w.start)[0], w3_raw[:, w], ACT.Copy)\
                    .then_inc(s["w3hi_ready"], 1)

            def attention(i):
                for vg in range(VG):
                    act.wait_ge(s["v_ps"], VG * i + vg + 1)
                    act.activation(v_stage[vg], bank[V_BANK[vg]], ACT.Copy).then_inc(s["v_taken"], 1)
                head(ATT_HEAD[i])
                for n in range(2 * G):
                    b, g = divmod(n, G)
                    act.wait_ge(s["q_ps"], 8 * i + n + 1)
                    if n == 0:
                        act.wait_ge(s["pool_set"], 3 + i)
                    act.activation(half(qs[0:96, g, :], b), bank[n][0:96, :], ACT.Identity,
                                   bias=vec[0:96, V_BQ + G * i + g:V_BQ + G * i + g + 1]).then_inc(s["q_hi"], 1)

                def out_hi(b):
                    act.wait_ge(s["oT_ps"], 2 * i + b + 1)
                    if b == 1:
                        act.wait_ge(s["ao_ps"], 2 * i + 1)
                    act.activation(oT_hi[:, :], bank[OT_BANK[b]], ACT.Copy).then_inc(s["oT_hi_ready"], 1)

                def exponentials(t):
                    act.wait_ge(s["sub_done"], NT * i + t + 1)
                    act.activation(e_sb[:, t % 2, 0:H * L], e_sb[:, t % 2, 0:H * L], ACT.Exp).then_inc(s["exp_done"], 1)

                def take_p(t, k):
                    n = 3 * (NT * i + t) + k
                    w = min(4, NC - 4 * k) * P
                    act.wait_ge(s["pt_ps"], n + 1)
                    act.activation(pT[:, t % 2, 4 * k * P:4 * k * P + w], bank[4 + n % 2][:, 0:w], ACT.Copy)\
                        .then_inc(s["pt_ready"], 1)

                exponentials(0)
                for t in range(NT):
                    if t >= 2:
                        act.wait_ge(s["pv_ps"], NT * i + t - 1)
                    take_p(t, 0)
                    take_p(t, 1)
                    if t + 1 < NT:
                        exponentials(t + 1)
                    take_p(t, 2)
                    if t == 5:
                        out_hi(0)
                    if i == 2 and t in (2, 3) and ("loc", 0) in order:
                        split_w3(0, t - 2)
                if i in ahead:
                    head(ahead[i], (0,))
                out_hi(1)

            def take_h(layer, b):
                jf = 8 + 2 * layer
                act.wait_ge(s["xT_ps"], 2 * jf + b + 1)
                act.activation(ytmp[:, b, :], bank[6 + b], ACT.Identity, bias=vec[:, V_LB + layer:V_LB + layer + 1],
                               scale=vec[:, V_LG + layer:V_LG + layer + 1]).then_inc(s["hF_ready"], 1)
                act.wait_ge(s["hF_ready"], 2 * layer + b + 1)
                act.activation(half(x_hi, b), ytmp[:, b, :], ACT.Copy).then_inc(s["xhi_ready"], 1)

            def feed_forward(kind, m, units):
                ub, pb = unit_base[m], prod_base[m]
                for n in range(len(units) + 1):
                    if kind == "geglu" and n == 2:
                        take_h(m - 3, 1)
                    if n < len(units):
                        e, b, c = units[n]
                        r = rows_of(kind, c)
                        g = ub + n
                        if kind != "geglu" and b == 0 and c == 0 and plans[m]["first"] + e + 1 < n_ring:
                            split_w(plans[m]["first"] + e + 1)
                        routed_top1 = kind == "top1" and e >= 4
                        if routed_top1:
                            act.wait_ge(s["scaled"], n - 8 + 1)
                        else:
                            act.wait_ge(s["hid_ps"], g + 1)
                        if n >= 3 and not routed_top1:
                            if kind == "gelu":
                                act.wait_ge(s["alo_ready"], g - 2)
                            else:
                                act.wait_ge(s["prod_ready"], pb + n - 2)
                        src = gate[0:r, g % 3, :] if routed_top1 else bank[2 + 2 * (n % 3)][0:r, :]
                        if kind == "gelu":
                            act.activation(gate[:, g % 3, :], src, ACT.Gelu,
                                           bias=vec[:, V_B1 + 4 * e + c:V_B1 + 4 * e + c + 1]).then_inc(s["gate_ready"], 1)
                        elif kind == "geglu":
                            v = V_B1G + (m - 3) * CH3 + c
                            act.activation(gate[:, g % 3, :], src, ACT.Gelu, bias=vec[:, v:v + 1]).then_inc(s["gate_ready"], 1)
                        else:
                            act.activation(gate[0:r, g % 3, :], src, ACT.Silu).then_inc(s["gate_ready"], 1)
                    if kind != "gelu" and n >= 1:
                        u = n - 1
                        r = rows_of(kind, units[u][2])
                        act.wait_ge(s["prod_ready"], pb + u + 1)
                        if u >= UB:
                            act.wait_ge(s["out_ps"], ub + u - UB + 1)
                        act.activation(a_hi[0:r, (ub + u) % UB, :], prod[0:r, (ub + u) % 3, :], ACT.Copy)\
                            .then_inc(s["ahi_ready"], 1)
                    if n == 2 and kind != "geglu":
                        ne = 16 if kind == "top1" else 8
                        for hb in range(B):
                            act.wait_ge(s["cT_ps"], 2 * m + hb + 1)
                            act.activation(half(cT[0:ne, :], hb), bank[hb][0:ne, :], ACT.Copy).then_inc(s["cT_ready"], 1)
                        act.wait_ge(s["cT_ready"], 2 * m + 2)
                        for r in range(4):
                            act.dma_start(crow[32 * r:32 * r + 1, 0:ne // 4, :], cT[r:ne:4, :]).then_inc(s["ld_row"], 16)

            def routed(m):
                head(MOE_HEAD[m], (1,) if m in (0, 1) else (0, 1))
                act.wait_ge(s["rt_sub"], m + 1)
                if m == 1:
                    act.activation(sm[:, 0, :], m8[:, :, 0], ACT.Exp, scale=-1.0).then_inc(s["rt_exp"], 1)
                else:
                    ne = 8 if m == 0 else 7
                    act.activation(lg[:, :, 0:ne], lg[:, :, 0:ne], ACT.Exp).then_inc(s["rt_exp"], 1)
                feed_forward(plans[m]["kind"], m, plans[m]["units"])

            def l2_attention():
                head(L2_HEAD)
                for b in range(B):
                    act.wait_ge(s["s_sub"], b + 1)
                    ts = slice(HT * b, HT * b + HT)
                    act.activation(sc[:, ts, :], sc[:, ts, :], ACT.Exp).then_inc(s["s_exp"], 1)
                for b in range(B):
                    act.wait_ge(s["al_ps"], b + 1)
                    act.activation(alT[:, b, :], bank[2 + b][0:L, :], ACT.Copy).then_inc(s["alT_ready"], 1)
                    act.wait_ge(s["c_ps"], b + 1)
                    act.activation(c_hi[:, b, :], bank[4 + b], ACT.Copy).then_inc(s["chi_ready"], 1)
                for b in range(B):
                    act.wait_ge(s["t_ps"], b + 1)
                    act.activation(th[:, b, :], bank[6 + b], ACT.Tanh).then_inc(s["tanh_ready"], 1)

            def local(layer):
                m, ja, jf = 3 + layer, 7 + 2 * layer, 8 + 2 * layer
                if layer == 0:
                    act.wait_ge(s["x_added"], before[("loc", 0)])
                    act.activation(kept[:, :, :], x[:, :, :], ACT.Copy).then_inc(s["kept"], 1)
                for b in range(B):
                    act.wait_ge(s["xT_ps"], 2 * ja + b + 1)
                    act.activation(x_hi[0:64, b * S:(b + 1) * S], bank[6 + b][0:64, :], ACT.Copy)
                    act.activation(x_hi[64:P, b * S + 1:(b + 1) * S], bank[6 + b][64:P, 0:S - 1], ACT.Copy)\
                        .then_inc(s["xhi_ready"], 1)
                n0 = NT * layer

                def square(t, what):
                    act.wait_ge(s[("q3_ps", "k3_ps")[what]], n0 + t + 1)
                    if t > 0 and what == 0:
                        act.wait_ge(s["ssq_ready"], n0 + t)
                    act.activation(sq[:, what, :], bank[6 + what], ACT.Square).then_inc(s["sq_ready"], 1)

                def take_v(t):
                    act.wait_ge(s["v3_ps"], n0 + t + 1)
                    act.activation(v_all[:, t, :], bank[6], ACT.Copy).then_inc(s["v3_ready"], 1)

                def take_qk(t, what):
                    act.wait_ge(s["qkT_ps"], 2 * (n0 + t) + what + 1)
                    src = bank[5].rearrange("p (c n) -> p c n", c=4)
                    if what:
                        act.activation(kT[:, :, t * P:(t + 1) * P], src, ACT.Copy).then_inc(s["qkT_ready"], 1)
                        return
                    if t == 0:
                        act.wait_ge(s["pool_set"], 6)
                    act.activation(qT[0:LD, t % 2, 0:LH:2, :], src[0:LD], ACT.Copy)
                    act.activation(qT[LD:P, t % 2, 1:LH:2, :], src[LD:P], ACT.Copy).then_inc(s["qkT_ready"], 1)

                def exps(q):
                    t, pair = divmod(q, 4)
                    w = P + (WIN if t % HT else 0)
                    g = 4 * n0 + q
                    act.wait_ge(s["nb_ready"], g + 1)
                    if q >= 2:
                        act.wait_ge(s["pT3_ps"], g - 1)
                    for hh in range(2):
                        h = 2 * pair + hh
                        last = act.activation(p3[:, q % 2, hh, 2 * P - w:2 * P], bank[q % 2][:, hh * 192:hh * 192 + w],
                                              ACT.Exp, bias=nb3[:, t % 2, h:h + 1], scale=rq[:, t % 2, 0, h:h + 1],
                                              accum_out=sum3[:, t % 2, h:h + 1])
                    last.then_inc(s["p3_ready"], 1)

                def take_p(q):
                    t = q // 4
                    act.wait_ge(s["pT3_ps"], 4 * n0 + q + 1)
                    if q >= 2:
                        act.wait_ge(s["pv3_ps"], 4 * n0 + q - 1)
                    blk = slice(0 if t % HT else 1, 2)
                    src = bank[3].rearrange("p (h k n) -> p h k n", h=2, k=2)[:, :, blk, :]
                    act.activation(pT3[:, 1, :, :].rearrange("p (h k) n -> p h k n", h=2)[:, :, blk, :], src, ACT.Copy)\
                        .then_inc(s["pT3_odd"], 1)

                def out_hi(t):
                    act.wait_ge(s["o3_ps"], n0 + t + 1)
                    if t >= 2:
                        act.wait_ge(s["o3_out"], n0 + t - 1)
                    act.activation(o_hi[:, t % 2, :], bank[5], ACT.Copy).then_inc(s["ohi_ready"], 1)

                square(0, 0)
                square(0, 1)
                take_v(0)
                square(1, 0)
                square(1, 1)
                take_qk(0, 0)
                take_v(1)
                take_qk(0, 1)
                for q in range(4 * NT):
                    t, pair = divmod(q, 4)
                    exps(q)
                    if pair == 0 and t >= 2:
                        out_hi(t - 2)
                    if pair == 2 and t + 1 < NT:
                        take_qk(t + 1, 0)
                    if q and q % 2 == 0:
                        take_p(q - 1)
                    if pair == 1 and t + 2 < NT:
                        square(t + 2, 0)
                    if pair == 2 and t + 2 < NT:
                        square(t + 2, 1)
                    if pair == 3 and t + 1 < NT:
                        take_qk(t + 1, 1)
                    if pair == 3 and t + 2 < NT:
                        take_v(t + 2)
                    if q in (4 * (NT - 2), 4 * (NT - 2) + 1) and layer == 0 and ("loc", 1) in order:
                        split_w3(1, q % 2)
                take_p(4 * NT - 1)
                out_hi(NT - 2)
                take_h(layer, 0)
                out_hi(NT - 1)
                feed_forward("geglu", m, [(0, b, c) for b in range(B) for c in range(CH3)])

            if n_ring:
                split_w(0)
            for what, i in order:
                {"att": attention, "moe": routed, "l2x": lambda i: l2_attention(), "loc": local}[what](i)
                if (what, i) == ("att", 0):
                    act.wait_ge(s["gauss_d2"], 1)
                    act.activation(gauss[:, :, :], gauss[:, :, :], ACT.Exp, scale=-1.0 / 128.0)\
                        .then_inc(s["gauss_ready"], 1)

        @block.gpsimd
        def _(pool):
            step = Count(pool, s["pool_step"])

            def split_w(n):
                m = 0 if n < 8 else 1 if n < 28 else 2
                pool.wait_ge(s["whi_ready"], n + 1)
                w = slice(0, WIDTH[m])
                pool.tensor_tensor(w_lo[:, n % RING, w], w_raw[:, n % RING, w], w_hi[:, n % RING, w].bitcast(F32),
                                   ALU.subtract).then_inc(s["wlo_ready"], 1)

            def norm(ln, halves=range(B)):
                for b in halves:
                    pool.wait_ge(s["ve_ready"], 2 * ln + b + 1)
                    pool.tensor_tensor(rstd[:, HT * b:HT * b + HT], ve[:, HT * b:HT * b + HT], mhalf[:, 0:HT], ALU.pow)\
                        .then_inc(s["rstd_ready"], 1)

            def split_w3(layer, part):
                w = (slice(0, 3 * INNER), slice(3 * INNER, L3W))[part]
                pool.wait_ge(s["w3hi_ready"], 2 * layer + part + 1)
                hi, lo = w3_parts(layer, w.start, w.stop - w.start)
                pool.tensor_tensor(lo, w3_raw[:, w], hi.bitcast(F32), ALU.subtract)\
                    .then_inc(s["w3lo_ready"], 1)

            def attention(i):
                norm(ATT_HEAD[i])
                if i > 0:
                    pool.wait_ge(s["x_added"], before[("att", i)])
                step.done(pool.memset(e_sb[:, :, H * L:NC * P], 0.0))
                step.wait()
                pool.memset(qs[96:P, :, :].bitcast(F32), 1.0).then_inc(s["pool_set"], 1)
                pool.wait_ge(s["pool_set"], 3 + i)
                if i == 0:
                    pool.wait_ge(s["ld_cst"], 32)
                for vg in range(VG):
                    pool.wait_ge(s["v_taken"], VG * i + vg + 1)
                    src = v_stage[vg].rearrange("p (c h d) -> p c h d", c=4, h=H)
                    m = cst[:, C_VM + 4 * vg * H:C_VM + 4 * (vg + 1) * H].rearrange("p (c h) -> p c h", c=4)
                    for q in range(4):
                        last = pool.tensor_tensor(v_bd[:, 4 * vg + q, :, 0:DK], src[:, q, :, :],
                                                  m[:, q, :].unsqueeze(2).to_broadcast([P, H, DK]), ALU.mult)
                    last.then_inc(s["v_ready"], 1)
                if i == 2 and ("loc", 0) in order:
                    split_w3(0, 0)
                    split_w3(0, 1)
                if i in ahead:
                    if i == 0:
                        split_w(0)
                    norm(ahead[i], (0,))

            def routed(m):
                p = plans[m]
                kind, gb, cb = p["kind"], group_base[m], cb_base[m]
                norm(MOE_HEAD[m], (1,) if m in (0, 1) else (0, 1))
                skip = {"gelu": 0, "top1": 4, "top2": 1}[kind]

                def weights_of(e):
                    w = e - skip
                    if w == 0:
                        pool.wait_ge(s["ld_row"], 64 * (m + 1))
                    if w >= 2:
                        if kind == "top1":
                            pool.wait_ge(s["scaled"], 2 * (w - 1))
                        else:
                            pool.wait_ge(s["y_taken"], gb + 2 * (e - 1))
                    pool.wait_ge(s["wlo_ready"], min(p["first"] + max(e - 1, 0) + 2, n_ring))
                    if kind != "top1" and e >= 3:
                        pool.wait_ge(s["acc_added"], 14 * (m // 2) + 2 * (e - 2))
                    pool.partition_broadcast(cB[:, w % 2, :], crow[32 * (w % 4):32 * (w % 4) + 1, w // 4, :], P)\
                        .then_inc(s["cb_ready"], 1)
                    pool.wait_ge(s["cb_ready"], cb + w + 1)

                def add(e, b):
                    pool.wait_ge(s["y_taken"], gb + 2 * e + b + 1)
                    pool.tensor_tensor(half(acc, b), half(acc, b), ytmp[:, b, :], ALU.add).then_inc(s["acc_added"], 1)

                for e in range(p["experts"]):
                    if p["first"] + e + 1 < n_ring:
                        split_w(p["first"] + e + 1)
                    if e == 0 and skip == 0:
                        weights_of(0)
                    if kind != "top1" and e - 1 >= 1:
                        add(e - 1, 0)
                        add(e - 1, 1)
                    if e + 1 >= skip and e + 1 < p["experts"]:
                        weights_of(e + 1)
                if kind != "top1":
                    add(p["experts"] - 1, 0)
                    add(p["experts"] - 1, 1)

            def local(layer):
                n0 = NT * layer
                if layer == 0:
                    pool.wait_ge(s["x_added"], before[("loc", 0)])
                    norm(7)
                    step.done(pool.memset(p3[:, :, :, 0:WIN], 0.0))
                    step.wait()
                    pool.memset(qT[:, :, :, :], 0.0).then_inc(s["pool_set"], 1)
                for t in range(NT):
                    n = n0 + t
                    pool.wait_ge(s["ssq_ready"], n + 1)
                    pool.tensor_tensor(rn[:, t % 2, :], ssq[:, t % 2, :], mhalf[:, 0:2 * LH], ALU.pow)
                    pool.wait_ge(s["kr_ready"], n + 1)
                    if t >= 2:
                        pool.wait_ge(s["qkT_ps"], 2 * n - 2)
                    step.done(pool.tensor_tensor(qk[:, t % 2, :, :], r1[:, :, :], r2[:, :, :], ALU.add))
                    step.wait()
                    k = qk[:, t % 2, 1, :].rearrange("p (h d) -> p h d", h=LH)
                    pool.tensor_tensor(k, k, rn[:, t % 2, LH:2 * LH].unsqueeze(2).to_broadcast([P, LH, LD]), ALU.mult)\
                        .then_inc(s["qk_ready"], 1)
                norm(8 + layer, (0,))
                if layer == 0 and ("loc", 1) in order:
                    split_w3(1, 0)
                    split_w3(1, 1)
                norm(8 + layer, (1,))
                if layer == 1:
                    pool.wait_ge(s["xn_ready"], 2 * 9 + 2)
                    pool.wait_ge(s["kept"], 1)
                    pool.tensor_tensor(x[:, :, :], x[:, :, :], kept[:, :, :], ALU.add).then_inc(s["kept_added"], 1)

            pool.memset(mhalf[:, :], -0.5).then_inc(s["pool_set"], 1)
            pool.memset(ones[:, :], 1.0).then_inc(s["pool_set"], 1)
            pool.wait_ge(s["pool_set"], 2)
            for what, i in order:
                {"att": attention, "moe": routed, "l2x": lambda i: norm(L2_HEAD), "loc": local}[what](i)

        @block.vector
        def _(dve):
            step = Count(dve, s["dve_step"])

            def then(instruction):
                step.done(instruction)
                step.wait()

            def split_low(dst, full, upper):
                return dve.tensor_tensor(dst, full, upper.bitcast(F32), ALU.subtract)

            def statistics(b):
                for t in tiles(b):
                    last = dve.bn_stats(stats[:, t, 0:6], x[:, t, :])
                then(last)

            def variance(b, width):
                for t in tiles(b):
                    last = dve.bn_aggr(mv[:, t, :], stats[:, t, 0:width])
                then(last)
                dve.tensor_scalar(ve[:, HT * b:HT * b + HT], mv[:, HT * b:HT * b + HT, 1], EPS, None, ALU.add)\
                    .then_inc(s["ve_ready"], 1)

            def normal(ln, b):
                dve.wait_ge(s["rstd_ready"], 2 * ln + b + 1)
                for t in tiles(b):
                    last = dve.tensor_scalar(xn[:, t, :], x[:, t, :], mv[:, t, 0:1], rstd[:, t:t + 1],
                                             ALU.subtract, ALU.mult)
                last.then_inc(s["xn_ready"], 1)

            def low(jx, b):
                dve.wait_ge(s["xhi_ready"], 2 * jx + b + 1)
                split_low(half(x_lo, b), bank[6 + b], half(x_hi, b)).then_inc(s["xlo_ready"], 1)

            def head(ln, jx):
                for b in range(B):
                    statistics(b)
                    variance(b, 6)
                for b in range(B):
                    normal(ln, b)
                for b in range(B):
                    low(jx, b)

            def shifted_statistics(layer, b):
                dve.wait_ge(s["shift_ps"], 2 * layer + b + 1)
                for k, t in enumerate(tiles(b)):
                    dve.bn_stats(stats[:, t, 0:6], x[:, t, 0:64])
                    last = dve.bn_stats(stats[:, t, 6:12], bank[6 + b][:, 64 * k:64 * k + 64])
                then(last)
                variance(b, 12)

            def shifted_norm(layer, b):
                dve.wait_ge(s["rstd_ready"], 2 * (8 + layer) + b + 1)
                for k, t in enumerate(tiles(b)):
                    dve.tensor_scalar(xn[:, t, 0:64], x[:, t, 0:64], mv[:, t, 0:1], rstd[:, t:t + 1],
                                      ALU.subtract, ALU.mult)
                    last = dve.tensor_scalar(xn[:, t, 64:P], bank[6 + b][:, 64 * k:64 * k + 64], mv[:, t, 0:1],
                                             rstd[:, t:t + 1], ALU.subtract, ALU.mult)
                last.then_inc(s["xn_ready"], 1)

            def shifted_low(layer, b):
                dve.wait_ge(s["xhi_ready"], 2 * (8 + 2 * layer) + b + 1)
                split_low(half(x_lo, b), ytmp[:, b, :], half(x_hi, b)).then_inc(s["xlo_ready"], 1)

            def x_tiles(b):
                return x[:, HT * b:HT * b + HT, :].rearrange("p t d -> p (t d)")

            def routers():
                dve.wait_ge(s["ld_rw"], 16)
                then(dve.tensor_copy(rw_hi[:, :], rw[:, :]))
                split_low(rw_lo[:, :], rw[:, :], rw_hi[:, :]).then_inc(s["rw_ready"], 1)

            def window():
                dve.wait_ge(s["ld_l2"], 48)
                pt, index = vec[:, V_PT:V_PT + B], cst[:, C_IO:C_IO + L]
                dve.tensor_copy(l2s[:, 0:2], slen[:, :])
                dve.tensor_scalar(l2s[:, 2:4], pt, 16.0, 0.0, ALU.subtract, ALU.max)
                then(dve.tensor_scalar(l2s[:, 4:6], pt, 16.0, None, ALU.add))
                then(dve.tensor_tensor(l2s[:, 4:6], l2s[:, 4:6], l2s[:, 0:2], ALU.min))
                for b in range(B):
                    dve.tensor_scalar(valid[:, b, :], index, l2s[:, 2 + b:3 + b], None, ALU.is_ge)
                    dve.tensor_scalar(neg[:, b, :], index, l2s[:, 4 + b:5 + b], None, ALU.is_le)
                    last = dve.tensor_scalar(gauss[:, b, :], index, pt[:, b:b + 1], None, ALU.subtract)
                then(last)
                then(dve.tensor_tensor(valid[:, :, :], valid[:, :, :], neg[:, :, :], ALU.mult))
                dve.tensor_scalar(neg[:, :, :], valid[:, :, :], 1.0, 1e9, ALU.subtract, ALU.mult)
                dve.tensor_tensor(gauss[:, :, :], gauss[:, :, :], gauss[:, :, :], ALU.mult).then_inc(s["gauss_d2"], 1)

            def attention(i):
                w = aw[:, i, :]
                jh = ATT_HEAD[i]

                def keys_full():
                    dve.wait_ge(s["ld_aw" if i == 0 else "ld_aw_more"], 16)
                    dve.tensor_copy(wq_hi[:, :], w[:, 0:384])
                    then(dve.tensor_copy(wo_hi[:, :], w[:, 896:1024]))
                    split_low(wq_lo[:, :], w[:, 0:384], wq_hi[:, :])
                    split_low(wo_lo[:, :], w[:, 896:1024], wo_hi[:, :]).then_inc(s["wsplit"], 1)
                    dve.wait_ge(s["k_ps"], i + 1)
                    for g in range(G):
                        last = dve.scalar_tensor_tensor(
                            out=k_f[:, g, :], in0=bank[4 + g // 3][0:96, (g % 3) * B * L:(g % 3 + 1) * B * L],
                            scalar=vec[0:96, V_BK + G * i + g:V_BK + G * i + g + 1], in1=tau_s[0:96, :],
                            op0=ALU.add, op1=ALU.mult)
                    then(last)

                def keys_stacked():
                    then(dve.tensor_copy(k_x[:, :, :], k_f[:, :, :]))
                    then(split_low(k_x[32:64, :, :], k_f[32:64, :, :], k_x[32:64, :, :]))
                    for g in range(G):
                        src = k_x[:, g, :].bitcast(F32).rearrange("p (b k) -> p b k", b=B)
                        last = dve.tensor_tensor(
                            k_st[0:96, :, g, :].rearrange("p b (j k) -> p b j k", j=HG),
                            src.unsqueeze(2).to_broadcast([96, B, HG, L]),
                            cst[0:96, C_KM:C_KM + HG].unsqueeze(1).unsqueeze(3).to_broadcast([96, B, HG, L]), ALU.mult)
                    last.then_inc(s["k_ready"], 1)
                    dve.tensor_tensor(brow[:, :], bank[5][0:1, 2 * P:3 * P], rows[0:1, i * P:(i + 1) * P], ALU.add)\
                        .then_inc(s["brow_ready"], 1)

                for b in range(B):
                    statistics(b)
                    variance(b, 6)
                keys_full()
                for b in range(B):
                    normal(jh, b)
                low(jh, 0)
                keys_stacked()
                low(jh, 1)
                def query_low(b):
                    for g in range(G):
                        n = G * b + g
                        dve.wait_ge(s["q_hi"], 8 * i + n + 1)
                        q = half(qs[64:96, g, :], b)
                        dve.scalar_tensor_tensor(out=q, in0=bank[n][64:96, :],
                                                 scalar=vec[64:96, V_BQ + G * i + g:V_BQ + G * i + g + 1],
                                                 in1=q.bitcast(F32), op0=ALU.add, op1=ALU.subtract).then_inc(s["q_lo"], 1)

                def maximum(t):
                    n = NT * i + t
                    sp_ = ps[:, 0:4, 0:GW].rearrange("p g (j k) -> p g j k", j=HG)
                    m = mx[:, t % 2, :].rearrange("p (g j) -> p g j", g=G)
                    dve.wait_ge(s["score_ps"], n + 1)
                    then(dve.tensor_reduce(m, sp_, AX.X, ALU.max))
                    if t >= 2:
                        dve.wait_ge(s["pt_ps"], 3 * (n - 1))
                    dve.tensor_tensor(e_sb[:, t % 2, 0:H * L].rearrange("p (g j k) -> p g j k", g=G, j=HG), sp_,
                                      m.unsqueeze(3).to_broadcast([P, G, HG, L]), ALU.subtract).then_inc(s["sub_done"], 1)

                def normalise(t):
                    dve.wait_ge(s["pv_ps"], NT * i + t + 1)
                    o = bank[7][:, 0:VW].rearrange("p (h d) -> p h d", h=H)
                    then(dve.reciprocal(rsum[:, t % 2, :], o[:, :, DK]))
                    dve.tensor_tensor(on[:, t, :].rearrange("p (h d) -> p h d", h=H), o[:, :, 0:DK],
                                      rsum[:, t % 2, :].unsqueeze(2).to_broadcast([P, H, DK]), ALU.mult)\
                        .then_inc(s["on_ready"], 1)

                def out_lo(b):
                    dve.wait_ge(s["oT_hi_ready"], 2 * i + b + 1)
                    split_low(oT_lo[:, :], bank[OT_BANK[b]], oT_hi[:, :]).then_inc(s["oT_lo_ready"], 1)

                def add(b):
                    dve.wait_ge(s["ao_ps"], 2 * i + b + 1)
                    dve.tensor_tensor(x_tiles(b), x_tiles(b), bank[AO_BANK[b]], ALU.add).then_inc(s["x_added"], 1)

                query_low(0)
                for t in range(NT):
                    maximum(t)
                    if t == 0:
                        query_low(1)
                    if t >= 2:
                        normalise(t - 2)
                    if i == 0 and t == 2:
                        routers()
                    if i == 0 and t == 3:
                        window()
                    if t == 6:
                        out_lo(0)
                    if t == 7:
                        add(0)
                        if i in ahead:
                            dve.wait_ge(s["x_added"], before[("att", i)] + 1)
                            statistics(0)
                            variance(0, 6)
                normalise(NT - 2)
                if i in ahead:
                    normal(ahead[i], 0)
                normalise(NT - 1)
                if i in ahead:
                    low(ahead[i], 0)
                out_lo(1)
                add(1)
                dve.wait_ge(s["x_added"], before[("att", i)] + 2)

            def feed_forward(kind, m, units, chunks):
                ub, pb, gb = unit_base[m], prod_base[m], group_base[m]
                lag = LAG[kind]

                def lower(u, full):
                    r = rows_of(kind, units[u][2])
                    k = (ub + u) % UB
                    split_low(a_lo[0:r, k, :], full[0:r, (ub + u) % 3, :], a_hi[0:r, k, :]).then_inc(s["alo_ready"], 1)

                def take_y(e, b):
                    g = group_of(kind, e, b)
                    u = max(n for n, (ee, bb, c) in enumerate(units) if (ee, bb) == (e, b))
                    dve.wait_ge(s["out_ps"], ub + u + 1)
                    w = e - {"gelu": 0, "top1": 4, "top2": 1, "geglu": 0}[kind]
                    if kind == "geglu":
                        v = V_B23 + m - 3
                        i_ = dve.tensor_scalar(half(acc, b), bank[b], vec[:, v:v + 1], None, ALU.add)
                    elif kind == "top1":
                        i_ = dve.tensor_copy(half(acc, b) if e < 4 else ytmp[:, b, :], bank[b])
                    elif w < 0:
                        i_ = dve.tensor_copy(half(acc, b), bank[b])
                    else:
                        dve.wait_ge(s["cb_ready"], cb_base[m] + w + 1)
                        if e >= 2:
                            dve.wait_ge(s["acc_added"], 14 * (m // 2) + 2 * (e - 2) + b + 1)
                        dst = half(acc, b) if e == 0 else ytmp[:, b, :]
                        if kind == "gelu":
                            i_ = dve.scalar_tensor_tensor(out=dst, in0=bank[b], scalar=vec[:, V_B2 + e:V_B2 + e + 1],
                                                          in1=half(cB[:, w % 2, :], b), op0=ALU.add, op1=ALU.mult)
                        else:
                            i_ = dve.tensor_tensor(dst, bank[b], half(cB[:, w % 2, :], b), ALU.mult)
                    i_.then_inc(s["y_taken"], 1)

                for n in range(len(units) + lag + 1):
                    if kind == "geglu" and n == 2:
                        shifted_low(m - 3, 1)
                    v = n - lag - 1
                    if v >= 0:
                        e, b, c = units[v]
                        if last_of_group(kind, chunks, e, c):
                            take_y(e, b)
                    if kind == "gelu":
                        if n < len(units):
                            g = ub + n
                            dve.wait_ge(s["gate_ready"], g + 1)
                            if n >= UB:
                                dve.wait_ge(s["out_ps"], g - UB + 1)
                            then(dve.tensor_copy(a_hi[:, g % UB, :], gate[:, g % 3, :]))
                            lower(n, gate)
                        continue
                    if kind == "top1" and n < len(units) and units[n][0] >= 4:
                        e, b, c = units[n]
                        w = e - 4
                        dve.wait_ge(s["hid_ps"], ub + n + 1)
                        dve.wait_ge(s["cb_ready"], cb_base[m] + w + 1)
                        dve.wait_ge(s["prod_ready"], pb + n - 2)
                        dve.tensor_tensor(gate[:, (ub + n) % 3, :], bank[2 + 2 * (n % 3)], half(cB[:, w % 2, :], b), ALU.mult)\
                            .then_inc(s["scaled"], 1)
                    u = n - 1 if kind == "top1" else n
                    if 0 <= u < len(units):
                        e, b, c = units[u]
                        g, r = ub + u, rows_of(kind, c)
                        dve.wait_ge(s["gate_ready"], g + 1)
                        if u >= 3:
                            dve.wait_ge(s["alo_ready"], g - 2)
                        up = bank[3 + 2 * (u % 3)][0:r, :]
                        dst, gt = prod[0:r, g % 3, :], gate[0:r, g % 3, :]
                        if kind == "geglu":
                            v = V_B1A + (m - 3) * CH3 + c
                            i_ = dve.scalar_tensor_tensor(out=dst, in0=up, scalar=vec[:, v:v + 1], in1=gt,
                                                          op0=ALU.add, op1=ALU.mult)
                        else:
                            i_ = dve.tensor_tensor(dst, gt, up, ALU.mult)
                        i_.then_inc(s["prod_ready"], 1)
                    u -= 1
                    if 0 <= u < len(units):
                        dve.wait_ge(s["ahi_ready"], pb + u + 1)
                        lower(u, prod)

            def route(m):
                ne = (8, 16, 7)[m]
                cols = (8, 16, 8)[m]
                dve.wait_ge(s["lg_ps"], 2 * m + 2)
                logits = bank[0][:, 0:NT * cols].rearrange("p (t e) -> p t e", e=cols)
                every = lambda v, n: v.unsqueeze(2).to_broadcast([P, NT, n])
                index = cst[:, C_IO:C_IO + cols].unsqueeze(1).to_broadcast([P, NT, cols])
                top = 1 if m == 1 else 2
                if m == 1:
                    then(dve.tensor_copy(lg[:, :, 0:cols], logits))
                    ranked = lg
                else:
                    if m == 2:
                        rb = vec[:, V_RB:V_RB + 8].unsqueeze(1).to_broadcast([P, NT, 8])
                        then(dve.tensor_tensor(lg[:, :, 0:8], logits, rb, ALU.add))
                        logits = lg[:, :, 0:8]
                        dve.memset(pr[:, :, 7:8], -1.0)
                    then(dve.tensor_reduce(sm[:, 0, :], logits[:, :, 0:ne], AX.X, ALU.max))
                    dve.tensor_tensor(lg[:, :, 0:ne], logits[:, :, 0:ne], every(sm[:, 0, :], ne), ALU.subtract)\
                        .then_inc(s["rt_sub"], 1)
                    dve.wait_ge(s["rt_exp"], m + 1)
                    then(dve.tensor_reduce(sm[:, 1, :], lg[:, :, 0:ne], AX.X, ALU.add))
                    then(dve.reciprocal(sm[:, 2, :], sm[:, 1, :]))
                    then(dve.tensor_tensor(pr[:, :, 0:ne], lg[:, :, 0:ne], every(sm[:, 2, :], ne), ALU.mult))
                    ranked = pr
                for t in range(NT):
                    last = dve.max(m8[:, t, :], ranked[:, t, 0:cols])
                if m == 1:
                    last.then_inc(s["rt_sub"], 1)
                    dve.wait_ge(s["rt_sub"], 2)
                else:
                    then(last)
                for t in range(NT):
                    last = dve.max_index(i8[:, t, :], m8[:, t, :], ranked[:, t, 0:cols])
                then(last)
                then(dve.tensor_copy(i8f[:, :, 0:top], i8[:, :, 0:top]))
                for k in range(top):
                    last = dve.tensor_tensor(sel[:, k, :, 0:cols], index, every(i8f[:, :, k], cols), ALU.is_equal)
                then(last)
                if m == 1:
                    dve.wait_ge(s["rt_exp"], 2)
                    then(dve.tensor_scalar(sm[:, 1, :], sm[:, 0, :], 1.0, None, ALU.add))
                    then(dve.reciprocal(sm[:, 2, :], sm[:, 1, :]))
                    dve.tensor_tensor(cw[:, :, 0:cols], sel[:, 0, :, 0:cols], every(sm[:, 2, :], cols), ALU.mult)\
                        .then_inc(s["cw_ready"], 1)
                else:
                    then(dve.tensor_tensor(sel[:, 0, :, 0:cols], sel[:, 0, :, 0:cols], sel[:, 1, :, 0:cols], ALU.add))
                    then(dve.tensor_tensor(cw[:, :, 0:cols], sel[:, 0, :, 0:cols], pr[:, :, 0:cols], ALU.mult))
                    then(dve.tensor_reduce(sm[:, 0, :], cw[:, :, 0:cols], AX.X, ALU.add))
                    then(dve.reciprocal(sm[:, 1, :], sm[:, 0, :]))
                    dve.tensor_tensor(cw[:, :, 0:cols], cw[:, :, 0:cols], every(sm[:, 1, :], cols), ALU.mult)\
                        .then_inc(s["cw_ready"], 1)

            def routed(m):
                p = plans[m]
                if m in (0, 1):
                    statistics(1)
                    variance(1, 6)
                    normal(MOE_HEAD[m], 1)
                    low(MOE_HEAD[m], 1)
                else:
                    head(MOE_HEAD[m], MOE_HEAD[m])
                route(m)
                feed_forward(p["kind"], m, p["units"], p["chunks"])
                for b in range(B):
                    dve.wait_ge(s["yT_ps"], 2 * m + b + 1)
                    i_ = dve.tensor_tensor(x_tiles(b), x_tiles(b), bank[2 + b], ALU.add)
                    if m == 1:
                        then(i_)
                        for k, t in enumerate(tiles(b)):
                            i_ = dve.scalar_tensor_tensor(out=x[:, t, :], in0=bank[4 + b][:, k * P:(k + 1) * P],
                                                          scalar=sm[:, 2, t:t + 1], in1=x[:, t, :], op0=ALU.mult, op1=ALU.add)
                    i_.then_inc(s["x_added"], 1)
                dve.wait_ge(s["x_added"], before[("moe", m)] + 2)

            def l2_attention():
                dve.wait_ge(s["ld_l2"], 48)
                dve.memset(m_hi[:, :, L:78].bitcast(F32), 0.0)
                dve.memset(m_lo[:, :, L:78].bitcast(F32), 0.0)
                dve.wait_ge(s["m_ps"], 1)
                m_ps = bank[4][:, 0:B * L].rearrange("p (b k) -> p b k", b=B)
                dve.tensor_copy(m_hi[:, :, 0:L], m_ps)
                then(dve.tensor_copy(wc_hi[:, :], l2w[:, P:3 * P]))
                split_low(wc_lo[:, :], l2w[:, P:3 * P], wc_hi[:, :])
                split_low(m_lo[:, :, 0:L], m_ps, m_hi[:, :, 0:L]).then_inc(s["m_ready"], 1)
                head(L2_HEAD, L2_HEAD)
                every = lambda v: v.unsqueeze(2).to_broadcast([P, HT, L])
                row = lambda v: v.unsqueeze(1).to_broadcast([P, HT, L])
                for b in range(B):
                    ts = slice(HT * b, HT * b + HT)
                    z = sc[:, ts, :]
                    dve.wait_ge(s["s_ps"], b + 1)
                    src = bank[b][:, 0:HT * 78].rearrange("p (t k) -> p t k", t=HT)[:, :, 0:L]
                    then(dve.tensor_tensor(z, src, row(valid[:, b, :]), ALU.mult))
                    then(dve.tensor_tensor(z, z, row(neg[:, b, :]), ALU.add))
                    then(dve.tensor_reduce(l2m[:, 0, ts], z, AX.X, ALU.max))
                    dve.tensor_tensor(z, z, every(l2m[:, 0, ts]), ALU.subtract).then_inc(s["s_sub"], 1)
                dve.wait_ge(s["gauss_ready"], 1)
                for b in range(B):
                    ts = slice(HT * b, HT * b + HT)
                    z, z2 = sc[:, ts, :], sc2[:, ts, :]
                    dve.wait_ge(s["s_exp"], b + 1)
                    then(dve.tensor_reduce(l2m[:, 1, ts], z, AX.X, ALU.add))
                    then(dve.reciprocal(l2m[:, 2, ts], l2m[:, 1, ts]))
                    then(dve.tensor_tensor(z2, z, every(l2m[:, 2, ts]), ALU.mult))
                    dve.tensor_tensor(z2, z2, row(gauss[:, b, :]), ALU.mult).then_inc(s["al_ready"], 1)
                for b in range(B):
                    dve.wait_ge(s["chi_ready"], b + 1)
                    split_low(c_lo[:, b, :], bank[4 + b], c_hi[:, b, :]).then_inc(s["clo_ready"], 1)
                for b in range(B):
                    dve.wait_ge(s["tanh_ready"], b + 1)
                    dve.tensor_tensor(x_tiles(b), x_tiles(b), th[:, b, :], ALU.add).then_inc(s["x_added"], 1)
                dve.wait_ge(s["x_added"], before[("l2x", 0)] + 2)

            def local(layer):
                m, ja, jf = 3 + layer, 7 + 2 * layer, 8 + 2 * layer
                n0 = NT * layer
                if layer == 0:
                    for b in range(B):
                        statistics(b)
                        variance(b, 6)
                    dve.tensor_copy(ident_b[:, :], ident)
                    dve.tensor_copy(mask[:, :], cst[:, C_MS:C_MS + P + WIN])
                if layer == 0:
                    dve.wait_ge(s["kept"], 1)
                    for b in range(B):
                        dve.wait_ge(s["rstd_ready"], 2 * 7 + b + 1)
                        for t in tiles(b):
                            last = dve.tensor_scalar(x[:, t, :], x[:, t, :], mv[:, t, 0:1], rstd[:, t:t + 1],
                                                     ALU.subtract, ALU.mult)
                        last.then_inc(s["xn_ready"], 1)
                def scale_tables(layer):
                    for k in range(4):
                        v = V_QS + (4 * layer + k) * LD
                        last = dve.tensor_tensor(rope[:, k, :, :], rope_raw[:, k, :, :],
                                                 vec[:, v:v + LD].unsqueeze(1).to_broadcast([P, HT, LD]), ALU.mult)
                    then(last)

                for b in range(B):
                    c0 = b * S
                    dve.memset(x_hi[64:P, c0:c0 + 1].bitcast(F32), 0.0)
                    dve.memset(x_lo[64:P, c0:c0 + 1].bitcast(F32), 0.0)
                    dve.wait_ge(s["xhi_ready"], 2 * ja + b + 1)
                    split_low(x_lo[0:64, c0:c0 + S], bank[6 + b][0:64, :], x_hi[0:64, c0:c0 + S])
                    split_low(x_lo[64:P, c0 + 1:c0 + S], bank[6 + b][64:P, 0:S - 1], x_hi[64:P, c0 + 1:c0 + S])\
                        .then_inc(s["xlo_ready"], 1)

                if layer == 0:
                    dve.wait_ge(s["ld_rope"], 16)
                    scale_tables(0)

                def rotate(t, what):
                    dve.wait_ge(s["sq_ready"], 2 * (n0 + t) + what + 1)
                    if what == 0 and t > 0:
                        dve.wait_ge(s["qk_ready"], n0 + t)
                    src = bank[6 + what].rearrange("p (h d) -> p h d", h=LH)
                    swapped = bank[6 + what].rearrange("p (h a d) -> p h a d", h=LH, a=2)[:, :, ::-1, :]
                    c, sn = rope[:, 2 * what, t % HT, :], rope[:, 2 * what + 1, t % HT, :]
                    dve.tensor_tensor(r1[:, what, :].rearrange("p (h d) -> p h d", h=LH), src,
                                      c.unsqueeze(1).to_broadcast([P, LH, LD]), ALU.mult)
                    dve.tensor_tensor(r2[:, what, :].rearrange("p (h a d) -> p h a d", h=LH, a=2), swapped,
                                      sn.rearrange("p (a d) -> p a d", a=2).unsqueeze(1).to_broadcast([P, LH, 2, LD // 2]),
                                      ALU.mult).then_inc(s[("rot_ready", "kr_ready")[what]], 1)

                def norms(t):
                    n = n0 + t
                    dve.wait_ge(s["sq_ready"], 2 * n + 2)
                    if t >= 1:
                        dve.wait_ge(s["qk_ready"], n)
                    then(dve.tensor_reduce(ssq[:, t % 2, :], sq[:, :, :].rearrange("p w (h d) -> p (w h) d", h=LH),
                                           AX.X, ALU.add))
                    dve.tensor_scalar(ssq[:, t % 2, :], ssq[:, t % 2, :], 1e-24, None, ALU.max).then_inc(s["ssq_ready"], 1)

                def query_scale(t):
                    dve.wait_ge(s["qk_ready"], n0 + t + 1)
                    if t >= 2:
                        dve.wait_ge(s["p3_ready"], 4 * (n0 + t) - 4)
                    dve.tensor_scalar(rq[:, t % 2, 0, :], rn[:, t % 2, 0:LH], QK_SCALE, None, ALU.mult)
                    then(dve.tensor_scalar(rq[:, t % 2, 1, :], rn[:, t % 2, 0:LH], -QK_SCALE, None, ALU.mult))

                def maximum(q):
                    t, pair = divmod(q, 4)
                    w = P + (WIN if t % HT else 0)
                    dve.wait_ge(s["sim_ps"], 4 * n0 + q + 1)
                    h = slice(2 * pair, 2 * pair + 2)
                    then(dve.tensor_reduce(mx3[:, t % 2, h],
                                           bank[q % 2][:, 0:384].rearrange("p (h k) -> p h k", h=2)[:, :, 0:w], AX.X, ALU.max))
                    dve.tensor_tensor(nb3[:, t % 2, h], mx3[:, t % 2, h], rq[:, t % 2, 1, h], ALU.mult)\
                        .then_inc(s["nb_ready"], 1)

                def normalise(t):
                    dve.wait_ge(s["pv3_ps"], 4 * (n0 + t) + 4)
                    if t >= 2:
                        dve.wait_ge(s["o3_ps"], n0 + t - 1)
                    then(dve.reciprocal(rs3[:, t % 2, :], sum3[:, t % 2, :]))
                    dve.tensor_tensor(on3[:, t % 2, :].rearrange("p (h d) -> p h d", h=LH),
                                      bank[4].rearrange("p (h d) -> p h d", h=LH),
                                      rs3[:, t % 2, :].unsqueeze(2).to_broadcast([P, LH, LD]), ALU.mult)\
                        .then_inc(s["on3_ready"], 1)

                def out_lo(t):
                    dve.wait_ge(s["ohi_ready"], n0 + t + 1)
                    split_low(o_lo[:, t % 2, :], bank[5], o_hi[:, t % 2, :]).then_inc(s["olo_ready"], 1)

                def add(t):
                    dve.wait_ge(s["o3_out"], n0 + t + 1)
                    dve.tensor_tensor(x[:, t, :], x[:, t, :], bank[7][:, 0:P], ALU.add).then_inc(s["x3_added"], 1)

                for t in range(2):
                    rotate(t, 0)
                    norms(t)
                    rotate(t, 1)
                query_scale(0)
                maximum(0)
                maximum(1)
                for q in range(4 * NT):
                    t, pair = divmod(q, 4)
                    if pair == 2 and t + 1 < NT:
                        query_scale(t + 1)
                    if q + 2 < 4 * NT:
                        maximum(q + 2)
                    if q % 2 == 0:
                        dve.wait_ge(s["pT3_ps"], 4 * n0 + q + 1)
                        if q >= 2:
                            dve.wait_ge(s["pv3_ps"], 4 * n0 + q - 1)
                        blk = slice(0 if t % HT else 1, 2)
                        src = bank[2].rearrange("p (h k n) -> p h k n", h=2, k=2)[:, :, blk, :]
                        dve.tensor_copy(pT3[:, 0, :, :].rearrange("p (h k) n -> p h k n", h=2)[:, :, blk, :], src)\
                            .then_inc(s["pT3_even"], 1)
                    if pair == 0 and t > 1:
                        add(t - 2)
                    if pair == 0 and t + 2 < NT:
                        rotate(t + 2, 0)
                    if pair == 0 and t > 0:
                        normalise(t - 1)
                    if pair == 1 and t + 2 < NT:
                        norms(t + 2)
                        rotate(t + 2, 1)
                    if pair == 3 and t > 0:
                        out_lo(t - 1)
                    if q == 4 * (NT - 2) and layer == 0:
                        scale_tables(1)
                    if q == 4 * (NT - 2) + 2:
                        shifted_statistics(layer, 0)
                    if q == 4 * (NT - 1):
                        shifted_norm(layer, 0)
                normalise(NT - 1)
                out_lo(NT - 1)
                add(NT - 2)
                shifted_low(layer, 0)
                add(NT - 1)
                dve.wait_ge(s["x3_added"], n0 + NT)
                shifted_statistics(layer, 1)
                shifted_norm(layer, 1)
                feed_forward("geglu", m, [(0, b, c) for b in range(B) for c in range(CH3)], CH3)
                if layer == 1:
                    dve.wait_ge(s["kept_added"], 1)
                for b in range(B):
                    dve.wait_ge(s["yT_ps"], 2 * m + b + 1)
                    dve.tensor_tensor(x_tiles(b), x_tiles(b), bank[2 + b], ALU.add).then_inc(s["x_added"], 1)
                dve.wait_ge(s["x_added"], before[("loc", layer)] + 2)

            dve.wait_ge(s["ld_cst"], 32)
            isq = 1.0 / float(np.sqrt(DK))
            dve.tensor_scalar(tau_s[:, :], vec[:, V_TAU:V_TAU + B * L], isq, None, ALU.mult)
            then(dve.tensor_scalar(del_f[:, :], vec[:, V_DEL:V_DEL + B * L], isq, None, ALU.mult))
            then(dve.tensor_copy(del_h[:, :], del_f[:, :]))
            then(split_low(del_l[:, :], del_f[:, :], del_h[:, :]))
            then(dve.tensor_scalar(del_l[:, :], del_l[:, :], cst[:, C_DM + 1:C_DM + 2], None, ALU.mult))
            then(dve.scalar_tensor_tensor(out=del_x[:, :], in0=del_h[:, :].bitcast(F32), scalar=cst[:, C_DM:C_DM + 1],
                                          in1=del_l[:, :], op0=ALU.mult, op1=ALU.add))
            for b in range(B):
                dve.tensor_copy(k_st[96:P, b, :, :].rearrange("p g (j k) -> p (g j) k", j=HG),
                                del_x[96:P, b * L:(b + 1) * L].unsqueeze(1).to_broadcast([32, H, L]))
            dve.tensor_copy(v_bd[:, :, :, DK], cst[:, C_VM:C_VM + B * NC * H].rearrange("p (c h) -> p c h", h=H))
            dve.wait_ge(s["ld_x"], 16)
            for what, i in order:
                {"att": attention, "moe": routed, "l2x": lambda i: l2_attention(), "loc": local}[what](i)



def constants():
    c = np.zeros((P, NCONST), np.float32)
    r = np.arange(P)
    c[r, C_ID + r] = 1.0
    for j in range(HG):
        c[:96, C_KM + j] = (r[:96] % 32) // DK == j
    c[96, C_DM] = 1.0
    c[97, C_DM + 1] = 1.0
    for k in range(B * NC):
        flat = (k % NC) * P + r
        for h in range(H):
            c[:, C_VM + k * H + h] = flat // L == h
    c[:, C_IO:C_IO + L + 1] = np.arange(L + 1)
    c[r[:-1], C_SH + r[1:]] = 1.0
    c[P - 1, C_SE] = 1.0
    i, j = r[:, None], np.arange(P + WIN)[None, :]
    c[:, C_MS:C_MS + P + WIN] = np.where((j >= i) & (j <= i + WIN), 0.0, -1e30)
    return c


def rotary():
    f = np.float32
    half_idx = np.arange(0, LD, 2, dtype=f)
    inv = (f(1.0) / f(10000.0) ** (half_idx / f(LD))).astype(f)
    t = np.arange(S, dtype=f)
    freqs = t[:, None] * inv[None, :]
    freqs = np.concatenate([freqs, freqs], -1)
    base = (half_idx + f(0.4 * LD)) / f(1.4 * LD)
    power = (t - f(S // 2)) / f(WIN // 2)
    scale = np.power(base[None, :].astype(f), power[:, None]).astype(f)
    scale = np.concatenate([scale, scale], -1)
    sign = np.concatenate([-np.ones(LD // 2, f), np.ones(LD // 2, f)])
    cos, sin = np.cos(freqs), np.sin(freqs) * sign
    tabs = np.stack([cos * scale, sin * scale, cos / scale, sin / scale]).astype(f)
    return np.ascontiguousarray(tabs.reshape(4, HT, P, LD).transpose(2, 0, 1, 3))


def lay_out(a):
    f = np.float32
    d = {"consts": constants(), "rope": rotary()}
    d["x"] = a["x"].reshape(NT, P, P).transpose(1, 0, 2)
    c = a["ctx_1024"]
    cT = c.transpose(2, 0, 1)
    d["ctxT"] = cT.reshape(P, B * L)
    rep = np.zeros((P, B, NC * P), f)
    rep[:, :, :H * L] = np.tile(cT, (1, 1, H))
    d["ctx_rep"] = rep
    d["ctx_n"] = c.transpose(1, 0, 2)
    att = ("L0", "L1", "L3")
    aw = np.zeros((P, 3, 1024), f)
    vec = np.zeros((P, NVEC), f)
    rows = np.zeros((1, NROW), f)

    def stack(w):
        return np.repeat(w.reshape(-1, G, 1, 32), 3, axis=2).reshape(-1, G * 96)

    for i, n in enumerate(att):
        g = lambda k: a[f"{n}_xcond_{k}"]
        aw[:, i, 0:384] = stack(g("Wq").T)
        aw[:, i, 384:768] = stack(g("Wk").T)
        aw[:, i, 768:896] = g("Wv").T
        aw[:, i, 896:1024] = g("Wo").T
        vec[0:96, V_BQ + G * i:V_BQ + G * i + G] = stack(g("bq")[None, :]).reshape(G, 96).T
        vec[0:96, V_BK + G * i:V_BK + G * i + G] = stack(g("bk")[None, :]).reshape(G, 96).T
        vec[:, V_BV + i] = g("bv")
        rows[0, i * P:(i + 1) * P] = g("bo")
    d["aw"], d["rows"] = aw, rows
    vec[:, V_B1:V_B1 + 32] = a["L0_ffn_b1"].reshape(32, P).T
    vec[:, V_B2:V_B2 + 8] = a["L0_ffn_b2"].T
    vec[:, V_LG:V_LG + DEPTH] = a["L3_ffn_ln_g"].T
    vec[:, V_LB:V_LB + DEPTH] = a["L3_ffn_ln_b"].T
    hid = a["L3_ffn_b1"].shape[1] // 2
    pad = np.zeros((DEPTH, 2, CH3 * P), f)
    pad[:, :, :hid] = a["L3_ffn_b1"].reshape(DEPTH, 2, hid)
    vec[:, V_B1A:V_B1A + DEPTH * CH3] = pad[:, 0].reshape(DEPTH * CH3, P).T
    vec[:, V_B1G:V_B1G + DEPTH * CH3] = pad[:, 1].reshape(DEPTH * CH3, P).T
    vec[:, V_B23:V_B23 + DEPTH] = a["L3_ffn_b2"].T
    vec[:, V_TAU:V_TAU + B * L] = np.repeat(a["condB_tau"], L)[None, :]
    vec[:, V_DEL:V_DEL + B * L] = a["fside_BxS2_0"].reshape(1, B * L)
    vec[:, V_PT:V_PT + B] = a["condB_pt"][None, :]
    vec[:, V_RB:V_RB + 7] = a["L2_ffn_rb"][None, :]
    for layer in range(DEPTH):
        for k, name in enumerate(("q_scale", "k_scale")):
            v = a[f"L3_ffn_{name}"][layer]
            o = V_QS + (4 * layer + 2 * k) * LD
            vec[:, o:o + LD] = v[None, :]
            vec[:, o + LD:o + 2 * LD] = np.concatenate([v[LD // 2:], v[:LD // 2]])[None, :]
    d["vec"] = vec
    rw = np.zeros((P, 32), f)
    rw[:, 0:8] = a["L0_ffn_Wr"]
    rw[:, 8:24] = a["L1_ffn_router_w"].T
    rw[:, 24:31] = a["L2_ffn_wr"].T
    d["rw"] = rw
    wc = a["L2_xcond_W_c"].T
    d["l2w"] = np.concatenate([a["L2_xcond_W_a"].T, wc[:P], wc[P:]], axis=1)
    d["slen"] = np.repeat(a["_lenS2"][None, :], P, axis=0)
    w2 = a["L0_ffn_W2"].reshape(8, 4, P, P).transpose(0, 2, 1, 3).reshape(8, P, 4 * P)
    d["w0"] = np.concatenate([a["L0_ffn_W1"], w2], axis=2)
    w = np.zeros((20, P, 384), f)
    w[4:, :, 0:256] = a["L1_ffn_gate_up_proj"]
    w[4:, :, 256:384] = a["L1_ffn_down_proj"]
    for e in range(4):
        r = slice(e * P, (e + 1) * P)
        w[e, :, 0:128] = a["L1_ffn_shared_gate_w"][r].T
        w[e, :, 128:256] = a["L1_ffn_shared_up_w"][r].T
        w[e, :, 256:384] = a["L1_ffn_shared_down_w"][:, r].T
    d["w1"] = w
    w = np.zeros((8, P, 1088), f)
    for e in range(8):
        gw, uw, dw = ((a["L2_ffn_sg"], a["L2_ffn_su"], a["L2_ffn_sd"]) if e == 0 else
                      (a["L2_ffn_rg"][e - 1], a["L2_ffn_ru"][e - 1], a["L2_ffn_rd"][e - 1]))
        w[e, :, 0:352] = gw.T
        w[e, :, 352:704] = uw.T
        for k in range(3):
            part = dw[:, k * P:(k + 1) * P].T
            w[e, :part.shape[0], 704 + k * P:704 + (k + 1) * P] = part
    d["w2"] = w
    w = np.zeros((DEPTH, P, L3W), f)
    w[:, :, 0:3 * INNER] = a["L3_ffn_wqkv"]
    w[:, :, 3 * INNER:4 * INNER] = a["L3_ffn_wo"].reshape(DEPTH, 4, P, P).transpose(0, 2, 1, 3).reshape(DEPTH, P, INNER)
    w[:, :, 4 * INNER:4 * INNER + hid] = a["L3_ffn_w1"][:, :, :hid]
    w[:, :, 4 * INNER + CH3 * P:4 * INNER + CH3 * P + hid] = a["L3_ffn_w1"][:, :, hid:]
    w2 = np.zeros((DEPTH, CH3 * P, P), f)
    w2[:, :hid] = a["L3_ffn_w2"]
    w[:, :, 4 * INNER + 2 * CH3 * P:] = w2.reshape(DEPTH, CH3, P, P).transpose(0, 2, 1, 3).reshape(DEPTH, P, CH3 * P)
    d["w3"] = w
    return {k: np.ascontiguousarray(v) for k, v in d.items()}


STAGES = 9


def kernel(**inputs):
    import concourse.bacc as bacc
    from concourse.bass_utils import run_bass_kernel_spmd

    nc = bacc.Bacc("TRN2", target_bir_lowering=False, num_devices=1)
    arrays = {f"in_{k}": v for k, v in lay_out({k: np.asarray(v) for k, v in inputs.items()}).items()}
    d = {k[3:]: nc.dram_tensor(k, v.shape, mybir.dt.from_np(v.dtype), kind="ExternalInput").ap() for k, v in arrays.items()}
    out = nc.dram_tensor("out", (P, NT, P), F32, kind="ExternalOutput").ap()
    build(nc, d, out, STAGES)
    r = run_bass_kernel_spmd(nc, [arrays], core_ids=[0])
    return np.asarray(r.results[0]["out"]).transpose(1, 0, 2).reshape(B, S, P)
```

```python
from contextlib import ExitStack

import numpy as np
import concourse.bass as bass
from concourse import mybir

F32 = mybir.dt.float32
F32R = mybir.dt.float32r
BF16 = mybir.dt.bfloat16
U32 = mybir.dt.uint32
I32 = mybir.dt.int32
ACT = mybir.ActivationFunctionType
ALU = mybir.AluOpType
AX = mybir.AxisListType

P = 128
B = 2
S = 512
T = B * S
NT = T // P
HT = NT // B
L = 77
EPS = 1e-5

H = 16
DK = P // H
G = 4
HG = H // G
GW = HG * L
NC = -(-H * L // P)
VW = H * (DK + 1)
VG = B * NC // 4

RING = 3
WMAX = 1088
UB = 4

LH = 8
LD = 64
INNER = LH * LD
WIN = 64
QK_SCALE = 8.0
DEPTH = 2
CH3 = 3
L3W = 3 * INNER + 4 * P + 2 * CH3 * P + CH3 * P

C_ID = 0
C_KM = C_ID + P
C_DM = C_KM + HG
C_VM = C_DM + 2
C_IO = C_VM + B * NC * H
C_SH = C_IO + L + 1
C_SE = C_SH + P
C_MS = C_SE + P
NCONST = C_MS + P + WIN

V_BQ = 0
V_BK = V_BQ + 3 * G
V_BV = V_BK + 3 * G
V_B1 = V_BV + 3
V_B2 = V_B1 + 32
V_LG = V_B2 + 8
V_LB = V_LG + DEPTH
V_B1A = V_LB + DEPTH
V_B1G = V_B1A + DEPTH * CH3
V_B23 = V_B1G + DEPTH * CH3
V_TAU = V_B23 + DEPTH
V_DEL = V_TAU + B * L
V_PT = V_DEL + B * L
V_RB = V_PT + B
V_QS = V_RB + 8
NVEC = V_QS + DEPTH * 4 * LD
NROW = 3 * P

MOE = ("gelu", "top1", "top2")


def moe_plan():
    plans = []
    first = 0
    for kind, experts, chunks in (("gelu", 8, 4), ("top1", 4 + 16, 1), ("top2", 8, 3)):
        units = [(e, b, c) for e in range(experts) for b in range(B) for c in range(chunks)]
        plans.append(dict(kind=kind, experts=experts, chunks=chunks, first=first, units=units))
        first += experts
    return plans, first


class Count:

    def __init__(self, engine, semaphore):
        self.engine, self.semaphore, self.value = engine, semaphore, 0

    def done(self, instruction):
        self.value += 1
        instruction.then_inc(self.semaphore, 1)

    def wait(self):
        self.engine.wait_ge(self.semaphore, self.value)


def build(nc, d, out):
    plans, n_ring = moe_plan()
    ctx = ExitStack()
    with ctx:
        def sb(name, shape, dt=F32, where=None):
            return (where or ctx).enter_context(nc.sbuf_tensor(name, shape, dt))

        def sem(name):
            return ctx.enter_context(nc.semaphore(name))

        ps = ctx.enter_context(nc.psum_tensor("ps", [P, 8, S], F32))
        bank = [ps[:, i, :] for i in range(8)]

        x = sb("x", [P, NT, P])
        xn = sb("xn", [P, NT, P])
        x_hi = sb("x_hi", [P, T], F32R)
        x_lo = sb("x_lo", [P, T], F32R)
        cst = sb("cst", [P, NCONST])
        vec = sb("vec", [P, NVEC])
        ident = cst[:, C_ID:C_ID + P]
        stats = sb("stats", [P, NT, 12])
        mv = sb("mv", [P, NT, 2])
        ve = sb("ve", [P, NT])
        rstd = sb("rstd", [P, NT])
        mhalf = sb("mhalf", [P, 16])
        gate = sb("gate", [P, 3, S])
        prod = sb("prod", [P, 3, S])
        a_hi = sb("a_hi", [P, UB, S], F32R)
        a_lo = sb("a_lo", [P, UB, S], F32R)
        acc = sb("acc", [P, T])
        ytmp = sb("ytmp", [P, 2, S])

        early = ExitStack()
        w_raw = sb("w_raw", [P, RING, WMAX], F32, early)
        w_hi = sb("w_hi", [P, RING, WMAX], F32R, early)
        w_lo = sb("w_lo", [P, RING, WMAX], F32R, early)
        aw = sb("aw", [P, 3, 1024], F32, early)
        rows = sb("rows", [1, NROW], F32, early)
        ones = sb("ones", [1, P], F32, early)
        ctxT = sb("ctxT", [P, B * L], F32, early)
        ctx_rep = sb("ctx_rep", [P, B, NC * P], F32, early)
        wq_hi = sb("wq_hi", [P, G * 96], F32R, early)
        wq_lo = sb("wq_lo", [P, G * 96], F32R, early)
        wo_hi = sb("wo_hi", [P, P], F32R, early)
        wo_lo = sb("wo_lo", [P, P], F32R, early)
        tau_s = sb("tau_s", [P, B * L], F32, early)
        del_f = sb("del_f", [P, B * L], F32, early)
        del_h = sb("del_h", [P, B * L], F32R, early)
        del_l = sb("del_l", [P, B * L], F32, early)
        del_x = sb("del_x", [P, B * L], F32, early)
        k_f = sb("k_f", [96, G, B * L], F32, early)
        k_x = sb("k_x", [96, G, B * L], F32R, early)
        k_st = sb("k_st", [P, B, G, GW], F32R, early)
        v_bd = sb("v_bd", [P, B * NC, H, DK + 1], F32, early)
        brow = sb("brow", [1, P], F32, early)
        rw_hi = sb("rw_hi", [P, 32], F32R, early)
        rw_lo = sb("rw_lo", [P, 32], F32R, early)
        rw = sb("rw", [P, 32], F32, early)
        l2w = sb("l2w", [P, 3 * P], F32, early)
        ctx_n = sb("ctx_n", [L, B, P], F32, early)
        slen = sb("slen", [P, B], I32, early)
        l2s = sb("l2s", [P, 8], F32, early)
        valid = sb("valid", [P, B, L], F32, early)
        gauss = sb("gauss", [P, B, L], F32, early)
        neg = sb("neg", [P, B, L], F32, early)

        att = ExitStack()
        qs = sb("qs", [P, G, T], F32R, att)
        e_sb = sb("e_sb", [P, 2, NC * P], F32, att)
        pT = sb("pT", [P, 2, NC * P], F32, att)
        mx = sb("mx", [P, 2, H], F32, att)
        rsum = sb("rsum", [P, 2, H], F32, att)
        on = sb("on", [P, NT, P], F32, att)
        oT_hi = sb("oT_hi", [P, S], F32R, att)
        oT_lo = sb("oT_lo", [P, S], F32R, att)
        att.close()
        l2x = ExitStack()
        wc_hi = sb("wc_hi", [P, 2 * P], F32R, l2x)
        wc_lo = sb("wc_lo", [P, 2 * P], F32R, l2x)
        m_hi = sb("m_hi", [P, B, 78], F32R, l2x)
        m_lo = sb("m_lo", [P, B, 78], F32R, l2x)
        sc = sb("sc", [P, NT, L], F32, l2x)
        sc2 = sb("sc2", [P, NT, L], F32, l2x)
        l2m = sb("l2m", [P, 3, NT], F32, l2x)
        alT = sb("alT", [L, B, S], F32, l2x)
        c_hi = sb("c_hi", [P, B, S], F32R, l2x)
        c_lo = sb("c_lo", [P, B, S], F32R, l2x)
        th = sb("th", [P, B, S], F32, l2x)
        l2x.close()
        moe = ExitStack()
        lg = sb("lg", [P, NT, 16], F32, moe)
        pr = sb("pr", [P, NT, 16], F32, moe)
        m8 = sb("m8", [P, NT, 8], F32, moe)
        i8 = sb("i8", [P, NT, 8], U32, moe)
        i8f = sb("i8f", [P, NT, 8], F32, moe)
        sel = sb("sel", [P, 2, NT, 16], F32, moe)
        cw = sb("cw", [P, NT, 16], F32, moe)
        sm = sb("sm", [P, 4, NT], F32, moe)
        cT = sb("cT", [16, T], F32, moe)
        crow = sb("crow", [P, 4, T], F32, moe)
        cB = sb("cB", [P, 2, T], F32, moe)
        moe.close()
        early.close()

        late = ExitStack()
        w3_raw = sb("w3_raw", [P, RING * WMAX], F32, late)
        w3_hi = sb("w3_hi", [P, RING * WMAX], F32R, late)
        w3_lo = sb("w3_lo", [P, RING * WMAX], F32R, late)
        kept = sb("kept", [P, NT, P], F32, late)
        rope_raw = sb("rope_raw", [P, 4, HT, LD], F32, late)
        w3b_hi = sb("w3b_hi", [P, L3W - 3 * INNER], F32R, late)
        w3b_lo = sb("w3b_lo", [P, L3W - 3 * INNER], F32R, late)
        ident_b = sb("ident_b", [P, P], BF16, late)
        mask = sb("mask", [P, P + WIN], BF16, late)
        rope = sb("rope", [P, 4, HT, LD], F32, late)
        kT = sb("kT", [P, 4, T], F32, late)
        qT = sb("qT", [P, 2, LH, P], F32, late)
        v_all = sb("v_all", [P, NT, INNER], F32, late)
        sq = sb("sq", [P, 2, INNER], F32, late)
        r1 = sb("r1", [P, 2, INNER], F32, late)
        r2 = sb("r2", [P, 2, INNER], F32, late)
        qk = sb("qk", [P, 2, 2, INNER], F32, late)
        ssq = sb("ssq", [P, 2, 2 * LH], F32, late)
        rn = sb("rn", [P, 2, 2 * LH], F32, late)
        rq = sb("rq", [P, 2, 2, LH], F32, late)
        mx3 = sb("mx3", [P, 2, LH], F32, late)
        nb3 = sb("nb3", [P, 2, LH], F32, late)
        sum3 = sb("sum3", [P, 2, LH], F32, late)
        rs3 = sb("rs3", [P, 2, LH], F32, late)
        p3 = sb("p3", [P, 2, 2, 2 * P], F32, late)
        pT3 = sb("pT3", [P, 2, 4, P], F32, late)
        on3 = sb("on3", [P, 2, INNER], F32, late)
        o_hi = sb("o_hi", [P, 2, INNER], F32R, late)
        o_lo = sb("o_lo", [P, 2, INNER], F32R, late)
        late.close()

        s = {n: sem(n) for n in (
            "ld_cst", "ld_vec", "ld_x", "ld_ctx", "ld_rep", "ld_bo", "ld_aw", "ld_aw_more", "ld_rw", "ld_l2", "ld_w0", "ld_w1", "ld_w2", "ld_row", "ld_w3", "ld_rope",
            "stored",
            "dve_step", "act_step", "pool_step",
            "pool_set", "gauss_d2", "gauss_ready", "rw_ready",
            "ve_ready", "rstd_ready", "xn_ready", "xT_ps", "xhi_ready", "xlo_ready",
            "k_ps", "k_ready", "v_ps", "v_taken", "v_ready", "brow_ready", "wsplit", "wo_split",
            "q_ps", "q_hi", "q_lo", "score_ps", "sub_done", "exp_done", "pt_ps", "pt_ready", "pv_ps", "on_ready",
            "oT_ps", "oT_hi_ready", "oT_lo_ready", "ao_ps", "x_added",
            "m_ps", "m_ready", "s_ps", "s_sub", "s_exp", "al_ready", "al_ps", "alT_ready", "c_ps", "chi_ready",
            "clo_ready", "t_ps", "tanh_ready",
            "lg_ps", "rt_sub", "rt_exp", "cw_ready", "cT_ps", "cT_ready", "cb_ready",
            "whi_ready", "wlo_ready", "hid_ps", "scaled", "gate_ready", "prod_ready", "ahi_ready", "alo_ready",
            "out_ps", "y_taken", "acc_added", "yT_ps", "shared_ps", "shared_added",
            "w3hi_ready", "w3lo_ready", "q3_ps", "k3_ps", "v3_ps", "sq_ready", "v3_ready", "rot_ready", "kr_ready",
            "ssq_ready", "first_sum", "pool_rn", "qk_ready", "qkT_ps", "qkT_ready", "sim_ps", "nb_ready", "p3_ready",
            "pT3_ps", "pT3_even", "pT3_odd", "pv3_ps", "on3_ready", "o3_ps", "ohi_ready", "olo_ready", "o3_out", "x3_added",
            "shift_ps", "hF_ready", "kept", "kept_added",
        )}
        s_w = [s["ld_w0"], s["ld_w1"], s["ld_w2"]]

        ATT_HEAD = (0, 2, 6)
        MOE_HEAD = (1, 3, 5)
        L2_HEAD = 4
        order = [("att", 0), ("moe", 0), ("att", 1), ("moe", 1), ("l2x", 0), ("moe", 2), ("att", 2),
                 ("loc", 0), ("loc", 1)]
        WIDTH = (1024, 384, 1088)
        before = {st: 2 * n for n, st in enumerate(order)}
        n_units = [len(p["units"]) for p in plans]
        unit_base = [sum(n_units[:m]) for m in range(3)] + [sum(n_units), sum(n_units) + B * CH3]
        prod_base = [0, 0, n_units[1], n_units[1] + n_units[2], n_units[1] + n_units[2] + B * CH3]
        group_base = [0, 16, 20, 36, 38]
        cb_base = [0, 8, 24]
        units_through = {}
        for m, p in enumerate(plans):
            for e in range(p["experts"]):
                units_through[p["first"] + e] = unit_base[m] + (e + 1) * B * p["chunks"]
        V_BANK = (2, 3, 6, 7, 0)
        OT_BANK, AO_BANK = (6, 0), (6, 1)
        v_stage = [gate[:, 0, :], gate[:, 1, :], gate[:, 2, :], ytmp[:, 0, :], ytmp[:, 1, :]]
        ahead = {0: MOE_HEAD[0], 1: MOE_HEAD[1]}
        after_moe = {0: 2, 1: L2_HEAD, 2: 6}
        def pair_bank(kind, n):
            return (2, 0, 6)[n % 3] if kind == "geglu" else 2 + 2 * (n % 3)

        def y_bank(kind, b):
            return 4 + b if kind == "geglu" else b

        LAG = {"gelu": 2, "top1": 3, "top2": 2, "geglu": 2}

        def half(t, b):
            return t[:, b * S:(b + 1) * S]

        def tiles(b):
            return range(HT * b, HT * (b + 1))

        def first_of_group(kind, e, c):
            return c == 0 and (kind != "top1" or e in (0, 4))

        def last_of_group(kind, chunks, e, c):
            return c == chunks - 1 and (kind != "top1" or e in (3, 19))

        def group_of(kind, e, b):
            if kind == "top1":
                return (0 if e < 4 else 2) + b
            return 2 * e + b

        def rows_of(kind, c):
            return 96 if kind == "top2" and c == 2 else P

        def hid_cols(kind, c, up):
            if kind == "gelu":
                return c * P
            if kind == "top1":
                return up * P
            return up * 352 + c * P

        def out_cols(kind, c):
            return {"gelu": 512, "top1": 256, "top2": 704}[kind] + c * P

        def w3_parts(layer, c0, width):
            if layer == 1 and c0 >= 3 * INNER:
                w = slice(c0 - 3 * INNER, c0 - 3 * INNER + width)
                return w3b_hi[:, w], w3b_lo[:, w]
            return w3_hi[:, c0:c0 + width], w3_lo[:, c0:c0 + width]

        block = ctx.enter_context(nc.Block())

        @block.sync
        def _(sp):
            sp.dma_start(ctxT[:, :], d["ctxT"]).then_inc(s["ld_ctx"], 16)
            sp.dma_start(aw[:, 0, :], d["aw"][:, 0, :]).then_inc(s["ld_aw"], 16)
            sp.dma_start(vec[:, :], d["vec"]).then_inc(s["ld_vec"], 16)
            sp.dma_start(cst[:, :], d["consts"]).then_inc(s["ld_cst"], 16)
            sp.dma_start(ctx_rep[:, :, :], d["ctx_rep"]).then_inc(s["ld_rep"], 16)
            sp.dma_start(x[:, :, :], d["x"]).then_inc(s["ld_x"], 16)
            sp.dma_start(rows[:, :], d["rows"]).then_inc(s["ld_bo"], 16)
            sp.dma_start(rw[:, :], d["rw"]).then_inc(s["ld_rw"], 16)
            sp.dma_start(aw[:, 1:3, :], d["aw"][:, 1:3, :]).then_inc(s["ld_aw_more"], 16)
            sp.dma_start(l2w[:, :], d["l2w"]).then_inc(s["ld_l2"], 16)
            sp.dma_start(ctx_n[:, :, :], d["ctx_n"]).then_inc(s["ld_l2"], 16)
            sp.dma_start(slen[:, :], d["slen"]).then_inc(s["ld_l2"], 16)
            for n in range(n_ring):
                if n >= RING:
                    sp.wait_ge(s["wlo_ready"], n - RING + 1)
                m = 0 if n < 8 else 1 if n < 28 else 2
                width = WIDTH[m]
                src = d["w" + str(m)][n - plans[m]["first"]]
                sp.dma_start(w_raw[:, n % RING, 0:width], src).then_inc(s_w[n % RING], 16)
            for layer in range(DEPTH):
                if layer == 0:
                    sp.wait_ge(s["wlo_ready"], n_ring)
                    sp.wait_ge(s["out_ps"], sum(n_units))
                else:
                    sp.wait_ge(s["w3lo_ready"], 2)
                sp.dma_start(w3_raw[:, 0:3 * INNER], d["w3"][layer, :, 0:3 * INNER]).then_inc(s["ld_w3"], 16)
                sp.dma_start(w3_raw[:, 3 * INNER:L3W], d["w3"][layer, :, 3 * INNER:L3W]).then_inc(s["ld_w3"], 16)
                if layer == 0:
                    sp.dma_start(rope_raw[:, :, :, :], d["rope"]).then_inc(s["ld_rope"], 16)
            for b in range(B):
                sp.wait_ge(s["x_added"], 2 * len(order) - B + b + 1)
                sp.dma_start(out[:, 4 * b:4 * b + 4, :], x[:, 4 * b:4 * b + 4, :]).then_inc(s["stored"], 16)
            sp.wait_ge(s["stored"], 16 * B)

        @block.tensor
        def _(pe):
            def three(dst, a_h, a_l, b_h, b_l, start=True, stop=True):
                pe.matmul(dst, a_h, b_h, start=start, stop=False)
                pe.matmul(dst, a_l, b_h, start=False, stop=False)
                return pe.matmul(dst, a_h, b_l, start=False, stop=stop)

            def turn_x(ln, jx, b):
                pe.wait_ge(s["xn_ready"], 2 * ln + b + 1)
                for k, t in enumerate(tiles(b)):
                    last = pe.transpose(bank[6 + b][:, k * P:(k + 1) * P], xn[:, t, :], ident)
                last.then_inc(s["xT_ps"], 1)

            def keys_values(i, part):
                if part == 0:
                    pe.wait_ge(s["ld_aw" if i == 0 else "ld_aw_more"], 16)
                    for g in range(G):
                        pe.matmul(bank[4 + g // 3][0:96, (g % 3) * B * L:(g % 3 + 1) * B * L],
                                  aw[:, i, 384 + 96 * g:480 + 96 * g], ctxT[:, :], start=True, stop=True)
                    if i == 0:
                        pe.wait_ge(s["ld_vec"], 16)
                    pe.matmul(bank[5][0:1, 2 * P:3 * P], vec[:, V_BV + i:V_BV + i + 1], aw[:, i, 896:1024],
                              start=True, stop=True).then_inc(s["k_ps"], 1)
                    if i == 0:
                        pe.wait_ge(s["ld_rep"], 16)
                for vg in range(3) if part == 0 else range(3, VG):
                    for q in range(4):
                        c = 4 * vg + q
                        last = pe.matmul(bank[V_BANK[vg]][:, q * P:(q + 1) * P],
                                         ctx_rep[:, c // NC, (c % NC) * P:(c % NC + 1) * P],
                                         aw[:, i, 768:896], start=True, stop=True)
                    last.then_inc(s["v_ps"], 1)

            def attention(i):
                j = ATT_HEAD[i]
                if i == 0:
                    pe.wait_ge(s["ld_ctx"], 16)
                    keys_values(0, 0)
                    keys_values(0, 1)
                    pe.wait_ge(s["ld_cst"], 16)
                    pe.wait_ge(s["pool_set"], 2)
                    pe.wait_ge(s["v_taken"], 3)
                    turn_x(j, j, 0)

                def queries(b):
                    pe.wait_ge(s["wsplit"], i + 1)
                    pe.wait_ge(s["xlo_ready"], 2 * j + b + 1)
                    if b == 1:
                        pe.wait_ge(s["brow_ready"], i + 1)
                    for g in range(G):
                        w = slice(96 * g, 96 * g + 96)
                        three(bank[4 * b + g][0:96, :], wq_hi[:, w], wq_lo[:, w], half(x_hi, b), half(x_lo, b))\
                            .then_inc(s["q_ps"], 1)

                def scores(t):
                    if t == 0:
                        pe.wait_ge(s["q_lo"], 8 * i + 4)
                        pe.wait_ge(s["k_ready"], i + 1)
                        pe.wait_ge(s["pool_set"], 3 + i)
                    else:
                        pe.wait_ge(s["sub_done"], NT * i + t)
                    for g in range(G):
                        last = pe.matmul(bank[g][:, 0:GW], qs[:, g, t * P:(t + 1) * P], k_st[:, t // HT, g, :],
                                         start=True, stop=True)
                    last.then_inc(s["score_ps"], 1)

                def turn(t, parts):
                    if t == 0:
                        pe.wait_ge(s["q_lo"], 8 * i + 8)
                    pe.wait_ge(s["exp_done"], NT * i + t + 1)
                    for k in parts:
                        n = 3 * (NT * i + t) + k
                        if 3 * t + k >= 2:
                            pe.wait_ge(s["pt_ready"], n - 1)
                        for c in range(4 * k, min(4 * k + 4, NC)):
                            last = pe.transpose(bank[4 + n % 2][:, (c % 4) * P:(c % 4 + 1) * P],
                                                e_sb[:, t % 2, c * P:(c + 1) * P], ident)
                        last.then_inc(s["pt_ps"], 1)

                def values(t):
                    pe.wait_ge(s["pt_ready"], 3 * (NT * i + t) + 3)
                    if t == 0:
                        pe.wait_ge(s["v_ready"], VG * (i + 1))
                    if t > 0:
                        pe.wait_ge(s["on_ready"], NT * i + t)
                    for c in range(NC):
                        last = pe.matmul(bank[7][:, 0:VW], pT[:, t % 2, c * P:(c + 1) * P],
                                         v_bd[:, (t // HT) * NC + c, :, :].rearrange("p h d -> p (h d)"),
                                         start=(c == 0), stop=(c == NC - 1))
                    last.then_inc(s["pv_ps"], 1)

                def turn_out(b):
                    pe.wait_ge(s["on_ready"], NT * i + HT * b + HT)
                    for k, t in enumerate(tiles(b)):
                        last = pe.transpose(bank[OT_BANK[b]][:, k * P:(k + 1) * P], on[:, t, :], ident)
                    last.then_inc(s["oT_ps"], 1)

                def project(b):
                    pe.wait_ge(s["brow_ready"], i + 1)
                    pe.wait_ge(s["wo_split"], i + 1)
                    if b == 0:
                        pe.wait_ge(s["oT_lo_ready"], 2 * i + 1)
                    for k in range(HT):
                        c = slice(k * P, (k + 1) * P)
                        pe.matmul(bank[AO_BANK[b]][:, c], ones[:, :], brow[:, :], start=True, stop=False)
                        if k == 0:
                            pe.wait_ge(s["oT_lo_ready"], 2 * i + b + 1)
                        last = three(bank[AO_BANK[b]][:, c], oT_hi[:, c], oT_lo[:, c], wo_hi[:, :], wo_lo[:, :], start=False)
                    last.then_inc(s["ao_ps"], 1)

                pe.wait_ge(s["v_taken"], VG * (i + 1))
                queries(0)
                turn_x(j, j, 1)
                scores(0)
                queries(1)
                for t in range(NT):
                    if t + 1 < NT:
                        scores(t + 1)
                    turn(t, (0, 1))
                    if t > 0:
                        values(t - 1)
                    turn(t, (2,))
                    if t == 5:
                        turn_out(0)
                    if t == 6:
                        project(0)
                values(NT - 1)
                if i in ahead:
                    pe.wait_ge(s["x_added"], before[("att", i)] + 1)
                    turn_x(ahead[i], ahead[i], 0)
                if i == 2:
                    turn_stream(0, 0)
                turn_out(1)
                project(1)

            def turn_last(m, b):
                pe.wait_ge(s["y_taken"], group_base[m] + b + 1)
                for k in range(HT):
                    last = pe.transpose(bank[2 + b][:, k * P:(k + 1) * P], acc[:, (HT * b + k) * P:(HT * b + k + 1) * P], ident)
                last.then_inc(s["yT_ps"], 1)

            def turn_stream(layer, b):
                if layer == 0:
                    pe.wait_ge(s["xn_ready"], 2 * 7 + b + 1)
                else:
                    pe.wait_ge(s["x_added"], before[("loc", 1)] - B + b + 1)
                for k, t in enumerate(tiles(b)):
                    last = pe.transpose(bank[4][:, k * P:(k + 1) * P], x[:, t, :], ident)
                last.then_inc(s["xT_ps"], 1)

            def turn_y(m, b):
                if m == 1:
                    pe.wait_ge(s["y_taken"], group_base[m] + 3 + b)
                else:
                    pe.wait_ge(s["acc_added"], 14 * (m // 2) + 13 + b)
                src = ytmp[:, b, :] if m == 1 else half(acc, b)
                for k in range(HT):
                    last = pe.transpose(bank[b][:, k * P:(k + 1) * P], src[:, k * P:(k + 1) * P], ident)
                last.then_inc(s["yT_ps"], 1)

            def hidden(kind, m, jx, units, hid_w, n):
                e, b, c = units[n]
                r = rows_of(kind, c)
                if kind == "geglu":
                    pe.wait_ge(s["xlo_ready"], 2 * jx + b + 1)
                else:
                    pe.wait_ge(s["wlo_ready"], plans[m]["first"] + e + 1)
                if n >= 3 and kind == "gelu":
                    pe.wait_ge(s["gate_ready"], unit_base[m] + n - 2)
                elif n >= 3:
                    pe.wait_ge(s["prod_ready"], prod_base[m] + n - 2)
                for up in range(1 if kind == "gelu" else 2):
                    h, lo = hid_w(e, c, up)
                    last = three(bank[pair_bank(kind, n) + up][0:r, :], h, lo, half(x_hi, b), half(x_lo, b))
                last.then_inc(s["hid_ps"], 1)

            def feed_forward(kind, m, jx, units, chunks, hid_w, out_w, ahead=0):
                lag, ub, gb = LAG[kind], unit_base[m], group_base[m]
                for n in range(len(units) + lag):
                    if n == 2 and kind == "geglu":
                        turn_x(m + 5, jx, 1)
                        pe.wait_ge(s["hF_ready"], 2 * (m - 3) + 2)
                    if ahead <= n < len(units):
                        hidden(kind, m, jx, units, hid_w, n)
                    if n == 2 and kind != "geglu":
                        pe.wait_ge(s["cw_ready"], m + 1)
                        ne = 16 if kind == "top1" else 8
                        for hb in range(B):
                            for k, t in enumerate(tiles(hb)):
                                last = pe.transpose(bank[hb][0:ne, k * P:(k + 1) * P], cw[:, t, 0:ne], ident)
                            last.then_inc(s["cT_ps"], 1)
                    if n == len(units) and kind == "top1":
                        pe.wait_ge(s["prod_ready"], prod_base[m] + n - 2)
                        for hb in range(B):
                            for k in range(HT):
                                last = pe.transpose(bank[2 + 2 * ((n - 3) % 3) + hb][:, k * P:(k + 1) * P],
                                                    half(acc, hb)[:, k * P:(k + 1) * P], ident)
                            last.then_inc(s["shared_ps"], 1)
                    if n == len(units) and kind in ("gelu", "top2"):
                        turn_y(m, 0)
                    if n == len(units) and kind == "geglu":
                        pe.wait_ge(s["prod_ready"], prod_base[m] + n - 2)
                        turn_last(m, 0)
                    if n >= lag:
                        u = n - lag
                        e, b, c = units[u]
                        r = rows_of(kind, c)
                        pe.wait_ge(s["alo_ready"], ub + u + 1)
                        first = first_of_group(kind, e, c)
                        if first:
                            before_it = group_of(kind, e, b) - 2
                            if before_it >= 0 and kind != "geglu":
                                pe.wait_ge(s["y_taken"], gb + before_it + 1)
                            elif kind != "geglu":
                                pe.wait_ge(s["cT_ready"], 2 * m + 2)
                        h, lo = out_w(e, c, r)
                        k = (ub + u) % UB
                        three(bank[y_bank(kind, b)], h, lo, a_hi[0:r, k, :], a_lo[0:r, k, :], start=first,
                              stop=last_of_group(kind, chunks, e, c)).then_inc(s["out_ps"], 1)

            def routed(m):
                p = plans[m]
                kind, jx = p["kind"], MOE_HEAD[m]
                ne, r0 = ((8, 0), (16, 8), (8, 24))[m]

                def router(b):
                    pe.wait_ge(s["xlo_ready"], 2 * jx + b + 1)
                    for t in tiles(b):
                        c = slice(t * P, (t + 1) * P)
                        last = three(bank[0][:, t * ne:(t + 1) * ne], x_hi[:, c], x_lo[:, c],
                                     rw_hi[:, r0:r0 + ne], rw_lo[:, r0:r0 + ne])
                    last.then_inc(s["lg_ps"], 1)

                pe.wait_ge(s["rw_ready"], 1)
                router(0)
                turn_x(jx, jx, 1)
                router(1)

                def hid_w(e, c, up):
                    slot, c0 = (p["first"] + e) % RING, hid_cols(kind, c, up)
                    w = slice(c0, c0 + rows_of(kind, c))
                    return w_hi[:, slot, w], w_lo[:, slot, w]

                def out_w(e, c, r):
                    slot, c0 = (p["first"] + e) % RING, out_cols(kind, c)
                    return w_hi[0:r, slot, c0:c0 + P], w_lo[0:r, slot, c0:c0 + P]

                feed_forward(kind, m, jx, p["units"], p["chunks"], hid_w, out_w)
                if kind == "top1":
                    turn_y(m, 0)
                else:
                    if kind == "gelu":
                        pe.wait_ge(s["gate_ready"], unit_base[m] + n_units[m])
                    else:
                        pe.wait_ge(s["prod_ready"], prod_base[m] + n_units[m])
                    keys_values(1 + m // 2, 0)
                turn_y(m, 1)
                if m == 1:
                    pe.wait_ge(s["prod_ready"], prod_base[m] + n_units[m])
                    pe.wait_ge(s["ld_l2"], 48)
                    pe.matmul(bank[3][:, 0:B * L], l2w[:, 0:P], ctxT[:, :], start=True, stop=True).then_inc(s["m_ps"], 1)
                else:
                    pe.wait_ge(s["v_taken"], VG * (1 + m // 2) + 3)
                turn_x(after_moe[m], after_moe[m], 0)
                if m != 1:
                    pe.wait_ge(s["x_added"], before[("moe", m)] + 1)
                    keys_values(1 + m // 2, 1)

            def l2_attention():
                j = L2_HEAD
                pe.wait_ge(s["x_added"], before[("l2x", 0)])
                turn_x(j, j, 1)
                pe.wait_ge(s["m_ready"], 1)
                for b in range(B):
                    pe.wait_ge(s["xlo_ready"], 2 * j + b + 1)
                    for k, t in enumerate(tiles(b)):
                        c = slice(t * P, (t + 1) * P)
                        last = three(bank[b][:, k * 78:(k + 1) * 78], x_hi[:, c], x_lo[:, c], m_hi[:, b, :], m_lo[:, b, :])
                    last.then_inc(s["s_ps"], 1)
                for b in range(B):
                    pe.wait_ge(s["al_ready"], b + 1)
                    for k, t in enumerate(tiles(b)):
                        last = pe.transpose(bank[2 + b][0:L, k * P:(k + 1) * P], sc2[:, t, :], ident)
                    last.then_inc(s["al_ps"], 1)
                    pe.wait_ge(s["alT_ready"], b + 1)
                    pe.matmul(bank[4 + b], ctx_n[:, b, :], alT[:, b, :], start=True, stop=True).then_inc(s["c_ps"], 1)
                for b in range(B):
                    pe.wait_ge(s["clo_ready"], b + 1)
                    for k, t in enumerate(tiles(b)):
                        c, c0 = slice(t * P, (t + 1) * P), slice(k * P, (k + 1) * P)
                        three(bank[6 + b][:, c0], c_hi[:, b, c0], c_lo[:, b, c0], wc_hi[:, 0:P], wc_lo[:, 0:P], stop=False)
                        last = three(bank[6 + b][:, c0], x_hi[:, c], x_lo[:, c], wc_hi[:, P:2 * P], wc_lo[:, P:2 * P],
                                     start=False)
                    last.then_inc(s["t_ps"], 1)
                pe.wait_ge(s["tanh_ready"], 1)
                turn_x(MOE_HEAD[2], MOE_HEAD[2], 0)

            def local(layer):
                m = 3 + layer
                ja, jf = 7 + 2 * layer, 8 + 2 * layer
                n0 = NT * layer

                def proj(t, what):
                    c = slice(t * P, (t + 1) * P)
                    if what == 0:
                        pe.wait_ge(s["xlo_ready"], 2 * ja + (2 if t >= HT else 1))
                        pe.wait_ge(s["w3lo_ready"], 2 * layer + 1)
                        if t > 0:
                            pe.wait_ge(s["v3_ready"], n0 + t)
                    if what == 1 and t > 0:
                        pe.wait_ge(s["kr_ready"], n0 + t)
                    if what == 1 and t > 3:
                        pe.wait_ge(s["x3_added"], n0 + t - 3)
                    if what == 2:
                        pe.wait_ge(s["rot_ready"], n0 + t + 1)
                    three(bank[7 if what == 1 else 6], x_hi[:, c], x_lo[:, c],
                          *w3_parts(layer, what * INNER, INNER))\
                        .then_inc(s[("q3_ps", "k3_ps", "v3_ps")[what]], 1)

                def turn_qk(t, what):
                    if t == 0 and what == 0:
                        pe.wait_ge(s["first_sum"], layer + 1)
                    elif what == 0 or t == 0:
                        pe.wait_ge(s["qk_ready"], n0 + t + 1)
                    if 2 * t + what > 0:
                        pe.wait_ge(s["qkT_ready"], 2 * (n0 + t) + what)
                    if what == 0 and t > 2:
                        pe.wait_ge(s["olo_ready"], n0 + t - 2)
                    for c in range(4):
                        last = pe.transpose(bank[5][:, c * P:(c + 1) * P], qk[:, t % 2, what, c * P:(c + 1) * P], ident)
                    last.then_inc(s["qkT_ps"], 1)

                def sim(q):
                    t, pair = divmod(q, 4)
                    w = P + (WIN if t % HT else 0)
                    g = 4 * n0 + q
                    if pair == 0:
                        pe.wait_ge(s["qkT_ready"], 2 * (n0 + t) + 2)
                    if q >= 2:
                        pe.wait_ge(s["p3_ready"], g - 1)
                    for hh in range(2):
                        dst = bank[q % 2][:, hh * 192:hh * 192 + w]
                        pe.matmul(dst, ident_b[:, :], mask[:, P + WIN - w:P + WIN], start=True, stop=False)
                        last = pe.matmul(dst, qT[:, t % 2, 2 * pair + hh, :], kT[:, pair, (t + 1) * P - w:(t + 1) * P],
                                         start=False, stop=True)
                    last.then_inc(s["sim_ps"], 1)

                def turn_p(q):
                    t, pair = divmod(q, 4)
                    g = 4 * n0 + q
                    pe.wait_ge(s["p3_ready"], g + 1)
                    if q >= 2:
                        pe.wait_ge(s["pT3_odd" if q % 2 else "pT3_even"], g // 2)
                    for hh in range(2):
                        for blk in range(0 if t % HT else 1, 2):
                            k = 2 * hh + blk
                            last = pe.transpose(bank[2 + q % 2][:, k * P:(k + 1) * P],
                                                p3[:, q % 2, hh, blk * P:(blk + 1) * P], ident)
                    last.then_inc(s["pT3_ps"], 1)

                def pv(q):
                    t, pair = divmod(q, 4)
                    g = 4 * n0 + q
                    pe.wait_ge(s["pT3_odd" if q % 2 else "pT3_even"], g // 2 + 1)
                    pe.wait_ge(s["v3_ready"], n0 + t + 1)
                    if q == 0:
                        pe.wait_ge(s["xlo_ready"], 2 * ja + 2)
                    if pair == 0 and t > 0:
                        pe.wait_ge(s["on3_ready"], n0 + t)
                    for hh in range(2):
                        h = 2 * pair + hh
                        blks = range(0 if t % HT else 1, 2)
                        for blk in blks:
                            last = pe.matmul(bank[4][:, h * LD:(h + 1) * LD], pT3[:, q % 2, 2 * hh + blk, :],
                                             v_all[:, t - 1 + blk, h * LD:(h + 1) * LD],
                                             start=(blk == blks[0]), stop=(blk == 1))
                    last.then_inc(s["pv3_ps"], 1)

                def turn_o(t):
                    pe.wait_ge(s["on3_ready"], n0 + t + 1)
                    pe.wait_ge(s["qkT_ready"], 2 * (n0 + min(t + 2, NT - 1)) + 2)
                    if t > 0:
                        pe.wait_ge(s["olo_ready"], n0 + t)
                    for c in range(4):
                        last = pe.transpose(bank[5][:, c * P:(c + 1) * P], on3[:, t % 2, c * P:(c + 1) * P], ident)
                    last.then_inc(s["o3_ps"], 1)

                def out3(t):
                    pe.wait_ge(s["olo_ready"], n0 + t + 1)
                    pe.wait_ge(s["w3lo_ready"], 2 * layer + 2)
                    pe.wait_ge(s["kr_ready"], n0 + min(t + 4, NT))
                    if t > 0:
                        pe.wait_ge(s["x3_added"], n0 + t)
                    for c in range(4):
                        cc = slice(c * P, (c + 1) * P)
                        last = three(bank[7][:, 0:P], o_hi[:, t % 2, cc], o_lo[:, t % 2, cc],
                                     *w3_parts(layer, 3 * INNER + c * P, P), start=(c == 0), stop=(c == 3))
                    last.then_inc(s["o3_out"], 1)

                def shift(b):
                    pe.wait_ge(s["x3_added"], n0 + HT * (b + 1))
                    if b == 0:
                        pe.wait_ge(s["v3_ready"], n0 + NT)
                    pe.matmul(bank[6 + b][:, 0:HT * 64], cst[:, C_SH:C_SH + P], x[:, HT * b:HT * b + HT, 64:P],
                              start=True, stop=False)
                    pe.matmul(bank[6 + b][:, 64:HT * 64], cst[:, C_SE:C_SE + P], x[:, HT * b:HT * b + HT - 1, 64:P],
                              start=False, stop=True).then_inc(s["shift_ps"], 1)

                for what in range(3):
                    proj(0, what)
                proj(1, 0)
                proj(1, 1)
                turn_qk(0, 0)
                turn_stream(layer, 1)
                proj(1, 2)
                turn_qk(0, 1)
                pe.wait_ge(s["pool_set"], 6)
                sim(0)
                sim(1)
                proj(2, 0)
                for q in range(4 * NT):
                    t, pair = divmod(q, 4)
                    if q + 2 < 4 * NT and pair != 2:
                        sim(q + 2)
                    turn_p(q)
                    if q + 2 < 4 * NT and pair == 2:
                        sim(q + 2)
                    if q >= 1:
                        pv(q - 1)
                    if pair < 2 and t + 1 < NT:
                        turn_qk(t + 1, pair)
                    if pair == 2 and t > 0:
                        turn_o(t - 1)
                    if pair < 2 and t + 2 < NT:
                        proj(t + 2, 1 + pair)
                    if q == 4 * (NT - 2) + 1:
                        shift(0)
                    if q == 4 * (NT - 1) + 1:
                        turn_x(8 + layer, jf, 0)
                    if pair == 3 and t + 3 < NT:
                        proj(t + 3, 0)
                    if pair == 3 and t > 0:
                        out3(t - 1)
                pv(4 * NT - 1)
                def hid_w(e, c, up):
                    return w3_parts(layer, 4 * INNER + ((1 - up) * CH3 + c) * P, P)

                def out_w(e, c, r):
                    return w3_parts(layer, 4 * INNER + (2 * CH3 + c) * P, P)

                units = [(0, b, c) for b in range(B) for c in range(CH3)]
                hidden("geglu", m, jf, units, hid_w, 0)
                hidden("geglu", m, jf, units, hid_w, 1)
                turn_o(NT - 1)
                out3(NT - 1)
                shift(1)
                feed_forward("geglu", m, jf, units, CH3, hid_w, out_w, ahead=2)
                if layer == 0:
                    turn_stream(1, 0)
                turn_last(m, 1)

            for what, i in order:
                {"att": attention, "moe": routed, "l2x": lambda i: l2_attention(), "loc": local}[what](i)

        @block.scalar
        def _(act):
            step = Count(act, s["act_step"])

            def split_w(n):
                m = 0 if n < 8 else 1 if n < 28 else 2
                act.wait_ge(s_w[n % RING], 16 * (n // RING + 1))
                if n >= RING:
                    act.wait_ge(s["out_ps"], units_through[n - RING])
                act.activation(w_hi[:, n % RING, 0:WIDTH[m]], w_raw[:, n % RING, 0:WIDTH[m]], ACT.Copy)\
                    .then_inc(s["whi_ready"], 1)

            def head(jx, halves=range(B)):
                for b in halves:
                    act.wait_ge(s["xT_ps"], 2 * jx + b + 1)
                    act.activation(half(x_hi, b), bank[6 + b], ACT.Copy).then_inc(s["xhi_ready"], 1)

            def split_w3(layer, part):
                w = (slice(0, 3 * INNER), slice(3 * INNER, L3W))[part]
                act.wait_ge(s["ld_w3"], 32 * (layer + 1))
                act.activation(w3_parts(layer, w.start, w.stop - w.start)[0], w3_raw[:, w], ACT.Copy)\
                    .then_inc(s["w3hi_ready"], 1)

            def attention(i):
                for vg in range(VG):
                    act.wait_ge(s["v_ps"], VG * i + vg + 1)
                    act.activation(v_stage[vg], bank[V_BANK[vg]], ACT.Copy).then_inc(s["v_taken"], 1)
                    if vg == 2:
                        head(ATT_HEAD[i], (0,))
                for n in range(2 * G):
                    b, g = divmod(n, G)
                    if n == G:
                        head(ATT_HEAD[i], (1,))
                    if n == G and i == 0:
                        split_w(0)
                    act.wait_ge(s["q_ps"], 8 * i + n + 1)
                    act.activation(half(qs[0:96, g, :], b), bank[n][0:96, :], ACT.Identity,
                                   bias=vec[0:96, V_BQ + G * i + g:V_BQ + G * i + g + 1]).then_inc(s["q_hi"], 1)

                def out_hi(b):
                    act.wait_ge(s["oT_ps"], 2 * i + b + 1)
                    if b == 1:
                        act.wait_ge(s["ao_ps"], 2 * i + 1)
                    act.activation(oT_hi[:, :], bank[OT_BANK[b]], ACT.Copy).then_inc(s["oT_hi_ready"], 1)

                def exponentials(t):
                    act.wait_ge(s["sub_done"], NT * i + t + 1)
                    act.activation(e_sb[:, t % 2, 0:H * L], e_sb[:, t % 2, 0:H * L], ACT.Exp).then_inc(s["exp_done"], 1)

                def take_p(t, k):
                    n = 3 * (NT * i + t) + k
                    w = min(4, NC - 4 * k) * P
                    act.wait_ge(s["pt_ps"], n + 1)
                    act.activation(pT[:, t % 2, 4 * k * P:4 * k * P + w], bank[4 + n % 2][:, 0:w], ACT.Copy)\
                        .then_inc(s["pt_ready"], 1)

                exponentials(0)
                for t in range(NT):
                    if t >= 2:
                        act.wait_ge(s["pv_ps"], NT * i + t - 1)
                    take_p(t, 0)
                    take_p(t, 1)
                    if t + 1 < NT:
                        exponentials(t + 1)
                    take_p(t, 2)
                    if t == 5:
                        out_hi(0)
                    if i == 2 and t in (2, 3):
                        split_w3(0, t - 2)
                if i in ahead:
                    head(ahead[i], (0,))
                if i == 2:
                    keep(0)
                    take_stream(0, 0)
                out_hi(1)

            def keep(b):
                act.wait_ge(s["x_added"], before[("att", 2)] + b + 1)
                ts = slice(HT * b, HT * b + HT)
                act.activation(kept[:, ts, :], x[:, ts, :], ACT.Copy).then_inc(s["kept"], 1)

            def take_stream(layer, b):
                act.wait_ge(s["xT_ps"], 2 * (7 + 2 * layer) + b + 1)
                act.activation(x_hi[0:64, b * S:(b + 1) * S], bank[4][0:64, :], ACT.Copy)
                act.activation(x_hi[64:P, b * S + 1:(b + 1) * S], bank[4][64:P, 0:S - 1], ACT.Copy)\
                    .then_inc(s["xhi_ready"], 1)

            def take_h(layer, b):
                jf = 8 + 2 * layer
                act.wait_ge(s["xT_ps"], 2 * jf + b + 1)
                act.activation(ytmp[:, b, :], bank[6 + b], ACT.Identity, bias=vec[:, V_LB + layer:V_LB + layer + 1],
                               scale=vec[:, V_LG + layer:V_LG + layer + 1]).then_inc(s["hF_ready"], 1)
                act.wait_ge(s["hF_ready"], 2 * layer + b + 1)
                act.activation(half(x_hi, b), ytmp[:, b, :], ACT.Copy).then_inc(s["xhi_ready"], 1)

            def feed_forward(kind, m, units):
                ub, pb = unit_base[m], prod_base[m]
                for n in range(len(units) + 1):
                    if kind == "geglu" and n == 2:
                        take_h(m - 3, 1)
                    if n < len(units):
                        e, b, c = units[n]
                        r = rows_of(kind, c)
                        g = ub + n
                        if kind != "geglu" and b == 0 and c == 0 and plans[m]["first"] + e + 1 < n_ring:
                            split_w(plans[m]["first"] + e + 1)
                        routed_top1 = kind == "top1" and e >= 4
                        if routed_top1:
                            act.wait_ge(s["scaled"], n - 8 + 1)
                        else:
                            act.wait_ge(s["hid_ps"], g + 1)
                        if n >= 3 and not routed_top1:
                            if kind == "gelu":
                                act.wait_ge(s["alo_ready"], g - 2)
                            else:
                                act.wait_ge(s["prod_ready"], pb + n - 2)
                        src = gate[0:r, g % 3, :] if routed_top1 else bank[pair_bank(kind, n)][0:r, :]
                        if kind == "gelu":
                            act.activation(gate[:, g % 3, :], src, ACT.Gelu,
                                           bias=vec[:, V_B1 + 4 * e + c:V_B1 + 4 * e + c + 1]).then_inc(s["gate_ready"], 1)
                        elif kind == "geglu":
                            v = V_B1G + (m - 3) * CH3 + c
                            act.activation(gate[:, g % 3, :], src, ACT.Gelu, bias=vec[:, v:v + 1]).then_inc(s["gate_ready"], 1)
                        else:
                            act.activation(gate[0:r, g % 3, :], src, ACT.Silu).then_inc(s["gate_ready"], 1)
                    if kind != "gelu" and n >= 1:
                        u = n - 1
                        r = rows_of(kind, units[u][2])
                        act.wait_ge(s["prod_ready"], pb + u + 1)
                        if u >= UB:
                            act.wait_ge(s["out_ps"], ub + u - UB + 1)
                        act.activation(a_hi[0:r, (ub + u) % UB, :], prod[0:r, (ub + u) % 3, :], ACT.Copy)\
                            .then_inc(s["ahi_ready"], 1)
                    if n == 2 and kind != "geglu":
                        ne = 16 if kind == "top1" else 8
                        for hb in range(B):
                            act.wait_ge(s["cT_ps"], 2 * m + hb + 1)
                            act.activation(half(cT[0:ne, :], hb), bank[hb][0:ne, :], ACT.Copy).then_inc(s["cT_ready"], 1)
                        act.wait_ge(s["cT_ready"], 2 * m + 2)
                        for r in range(4):
                            act.dma_start(crow[32 * r:32 * r + 1, 0:ne // 4, :], cT[r:ne:4, :]).then_inc(s["ld_row"], 16)

            def routed(m):
                head(MOE_HEAD[m], (1,) if m in (0, 1) else (0, 1))
                act.wait_ge(s["rt_sub"], m + 1)
                if m == 1:
                    act.activation(sm[:, 0, :], m8[:, :, 0], ACT.Exp, scale=-1.0).then_inc(s["rt_exp"], 1)
                else:
                    ne = 8 if m == 0 else 7
                    act.activation(lg[:, :, 0:ne], lg[:, :, 0:ne], ACT.Exp).then_inc(s["rt_exp"], 1)
                feed_forward(plans[m]["kind"], m, plans[m]["units"])

            def l2_attention():
                head(L2_HEAD)
                for b in range(B):
                    act.wait_ge(s["s_sub"], b + 1)
                    ts = slice(HT * b, HT * b + HT)
                    act.activation(sc[:, ts, :], sc[:, ts, :], ACT.Exp).then_inc(s["s_exp"], 1)
                for b in range(B):
                    act.wait_ge(s["al_ps"], b + 1)
                    act.activation(alT[:, b, :], bank[2 + b][0:L, :], ACT.Copy).then_inc(s["alT_ready"], 1)
                    act.wait_ge(s["c_ps"], b + 1)
                    act.activation(c_hi[:, b, :], bank[4 + b], ACT.Copy).then_inc(s["chi_ready"], 1)
                for b in range(B):
                    act.wait_ge(s["t_ps"], b + 1)
                    act.activation(th[:, b, :], bank[6 + b], ACT.Tanh).then_inc(s["tanh_ready"], 1)

            def local(layer):
                m, ja, jf = 3 + layer, 7 + 2 * layer, 8 + 2 * layer
                if layer == 0:
                    keep(1)
                n0 = NT * layer

                def square(t, what):
                    act.wait_ge(s[("q3_ps", "k3_ps")[what]], n0 + t + 1)
                    if t > 0 and what == 0:
                        act.wait_ge(s["ssq_ready"], n0 + t)
                    act.activation(sq[:, what, :], bank[6 + what], ACT.Square).then_inc(s["sq_ready"], 1)

                def take_v(t):
                    act.wait_ge(s["v3_ps"], n0 + t + 1)
                    act.activation(v_all[:, t, :], bank[6], ACT.Copy).then_inc(s["v3_ready"], 1)

                def take_qk(t, what):
                    act.wait_ge(s["qkT_ps"], 2 * (n0 + t) + what + 1)
                    src = bank[5].rearrange("p (c n) -> p c n", c=4)
                    if what:
                        act.activation(kT[:, :, t * P:(t + 1) * P], src, ACT.Copy).then_inc(s["qkT_ready"], 1)
                        return
                    if t == 0:
                        act.wait_ge(s["pool_set"], 6)
                    act.activation(qT[0:LD, t % 2, 0:LH:2, :], src[0:LD], ACT.Copy)
                    act.activation(qT[LD:P, t % 2, 1:LH:2, :], src[LD:P], ACT.Copy).then_inc(s["qkT_ready"], 1)

                def exps(q):
                    t, pair = divmod(q, 4)
                    w = P + (WIN if t % HT else 0)
                    g = 4 * n0 + q
                    act.wait_ge(s["nb_ready"], g + 1)
                    if q >= 2:
                        act.wait_ge(s["pT3_ps"], g - 1)
                    for hh in range(2):
                        h = 2 * pair + hh
                        last = act.activation(p3[:, q % 2, hh, 2 * P - w:2 * P], bank[q % 2][:, hh * 192:hh * 192 + w],
                                              ACT.Exp, bias=nb3[:, t % 2, h:h + 1], scale=rq[:, t % 2, 0, h:h + 1],
                                              accum_out=sum3[:, t % 2, h:h + 1])
                    last.then_inc(s["p3_ready"], 1)

                def take_p(q):
                    t = q // 4
                    act.wait_ge(s["pT3_ps"], 4 * n0 + q + 1)
                    if q >= 2:
                        act.wait_ge(s["pv3_ps"], 4 * n0 + q - 1)
                    blk = slice(0 if t % HT else 1, 2)
                    src = bank[3].rearrange("p (h k n) -> p h k n", h=2, k=2)[:, :, blk, :]
                    act.activation(pT3[:, 1, :, :].rearrange("p (h k) n -> p h k n", h=2)[:, :, blk, :], src, ACT.Copy)\
                        .then_inc(s["pT3_odd"], 1)

                def out_hi(t):
                    act.wait_ge(s["o3_ps"], n0 + t + 1)
                    if t >= 2:
                        act.wait_ge(s["o3_out"], n0 + t - 1)
                    act.activation(o_hi[:, t % 2, :], bank[5], ACT.Copy).then_inc(s["ohi_ready"], 1)

                square(0, 0)
                square(0, 1)
                take_v(0)
                square(1, 0)
                square(1, 1)
                take_qk(0, 0)
                take_v(1)
                take_qk(0, 1)
                take_stream(layer, 1)
                for q in range(4 * NT):
                    t, pair = divmod(q, 4)
                    exps(q)
                    if pair == 0 and t >= 2:
                        out_hi(t - 2)
                    if pair == 2 and t + 1 < NT:
                        take_qk(t + 1, 0)
                    if q and q % 2 == 0:
                        take_p(q - 1)
                    if pair == 1 and t + 2 < NT:
                        square(t + 2, 0)
                    if pair == 2 and t + 2 < NT:
                        square(t + 2, 1)
                    if pair == 3 and t + 1 < NT:
                        take_qk(t + 1, 1)
                    if pair == 3 and t + 2 < NT:
                        take_v(t + 2)
                    if q in (4 * (NT - 2), 4 * (NT - 2) + 1) and layer == 0:
                        split_w3(1, q % 2)
                take_p(4 * NT - 1)
                out_hi(NT - 2)
                take_h(layer, 0)
                out_hi(NT - 1)
                feed_forward("geglu", m, [(0, b, c) for b in range(B) for c in range(CH3)])
                if layer == 0:
                    take_stream(1, 0)

            for what, i in order:
                {"att": attention, "moe": routed, "l2x": lambda i: l2_attention(), "loc": local}[what](i)
                if (what, i) == ("att", 0):
                    act.wait_ge(s["gauss_d2"], 1)
                    act.activation(gauss[:, :, :], gauss[:, :, :], ACT.Exp, scale=-1.0 / 128.0)\
                        .then_inc(s["gauss_ready"], 1)

        @block.gpsimd
        def _(pool):
            step = Count(pool, s["pool_step"])

            def split_w(n):
                m = 0 if n < 8 else 1 if n < 28 else 2
                pool.wait_ge(s["whi_ready"], n + 1)
                w = slice(0, WIDTH[m])
                pool.tensor_tensor(w_lo[:, n % RING, w], w_raw[:, n % RING, w], w_hi[:, n % RING, w].bitcast(F32),
                                   ALU.subtract).then_inc(s["wlo_ready"], 1)

            def norm(ln, halves=range(B)):
                for b in halves:
                    pool.wait_ge(s["ve_ready"], 2 * ln + b + 1)
                    pool.tensor_tensor(rstd[:, HT * b:HT * b + HT], ve[:, HT * b:HT * b + HT], mhalf[:, 0:HT], ALU.pow)\
                        .then_inc(s["rstd_ready"], 1)

            def split_w3(layer, part):
                w = (slice(0, 3 * INNER), slice(3 * INNER, L3W))[part]
                pool.wait_ge(s["w3hi_ready"], 2 * layer + part + 1)
                hi, lo = w3_parts(layer, w.start, w.stop - w.start)
                pool.tensor_tensor(lo, w3_raw[:, w], hi.bitcast(F32), ALU.subtract)\
                    .then_inc(s["w3lo_ready"], 1)

            def attention(i):
                if i > 0:
                    norm(ATT_HEAD[i])
                    pool.wait_ge(s["x_added"], before[("att", i)])
                step.done(pool.memset(e_sb[:, :, H * L:NC * P], 0.0))
                step.wait()
                pool.memset(qs[96:P, :, :].bitcast(F32), 1.0).then_inc(s["pool_set"], 1)
                pool.wait_ge(s["pool_set"], 3 + i)
                if i == 0:
                    norm(ATT_HEAD[0])
                if i == 0:
                    pool.wait_ge(s["ld_cst"], 16)
                for vg in range(VG):
                    pool.wait_ge(s["v_taken"], VG * i + vg + 1)
                    src = v_stage[vg].rearrange("p (c h d) -> p c h d", c=4, h=H)
                    m = cst[:, C_VM + 4 * vg * H:C_VM + 4 * (vg + 1) * H].rearrange("p (c h) -> p c h", c=4)
                    for q in range(4):
                        last = pool.tensor_tensor(v_bd[:, 4 * vg + q, :, 0:DK], src[:, q, :, :],
                                                  m[:, q, :].unsqueeze(2).to_broadcast([P, H, DK]), ALU.mult)
                    last.then_inc(s["v_ready"], 1)
                if i == 2:
                    split_w3(0, 0)
                    split_w3(0, 1)
                    norm(7, (0,))
                if i in ahead:
                    if i == 0:
                        split_w(0)
                    norm(ahead[i], (0,))

            def routed(m):
                p = plans[m]
                kind, gb, cb = p["kind"], group_base[m], cb_base[m]
                norm(MOE_HEAD[m], (1,) if m in (0, 1) else (0, 1))
                skip = {"gelu": 0, "top1": 4, "top2": 1}[kind]

                def weights_of(e):
                    w = e - skip
                    if w == 0:
                        pool.wait_ge(s["ld_row"], 64 * (m + 1))
                    if w >= 2:
                        if kind == "top1":
                            pool.wait_ge(s["scaled"], 2 * (w - 1))
                        else:
                            pool.wait_ge(s["y_taken"], gb + 2 * (e - 1))
                    pool.wait_ge(s["wlo_ready"], min(p["first"] + max(e - 1, 0) + 2, n_ring))
                    if kind != "top1" and e >= 3:
                        pool.wait_ge(s["acc_added"], 14 * (m // 2) + 2 * (e - 2))
                    pool.partition_broadcast(cB[:, w % 2, :], crow[32 * (w % 4):32 * (w % 4) + 1, w // 4, :], P)\
                        .then_inc(s["cb_ready"], 1)
                    pool.wait_ge(s["cb_ready"], cb + w + 1)

                def add(e, b):
                    pool.wait_ge(s["y_taken"], gb + 2 * e + b + 1)
                    pool.tensor_tensor(half(acc, b), half(acc, b), ytmp[:, b, :], ALU.add).then_inc(s["acc_added"], 1)

                for e in range(p["experts"]):
                    if p["first"] + e + 1 < n_ring:
                        split_w(p["first"] + e + 1)
                    if e == 0 and skip == 0:
                        weights_of(0)
                    if kind != "top1" and e - 1 >= 1:
                        add(e - 1, 0)
                        add(e - 1, 1)
                    if e + 1 >= skip and e + 1 < p["experts"]:
                        weights_of(e + 1)
                if kind != "top1":
                    add(p["experts"] - 1, 0)
                    add(p["experts"] - 1, 1)

            def local(layer):
                n0 = NT * layer
                if layer == 0:
                    norm(7, (1,))
                    pool.wait_ge(s["x_added"], before[("loc", 0)])
                    step.done(pool.memset(p3[:, :, :, 0:WIN], 0.0))
                    step.wait()
                    pool.memset(qT[:, :, :, :], 0.0).then_inc(s["pool_set"], 1)
                for t in range(NT):
                    n = n0 + t
                    pool.wait_ge(s["ssq_ready"], n + 1)
                    last = pool.tensor_tensor(rn[:, t % 2, :], ssq[:, t % 2, :], mhalf[:, 0:2 * LH], ALU.pow)
                    if t == 0:
                        last.then_inc(s["pool_rn"], 1)
                    if t == 0:
                        pool.wait_ge(s["first_sum"], layer + 1)
                        pool.wait_ge(s["pool_rn"], layer + 1)
                    else:
                        pool.wait_ge(s["kr_ready"], n + 1)
                        if t >= 2:
                            pool.wait_ge(s["qkT_ps"], 2 * n - 2)
                        step.done(pool.tensor_tensor(qk[:, t % 2, :, :], r1[:, :, :], r2[:, :, :], ALU.add))
                        step.wait()
                    k = qk[:, t % 2, 1, :].rearrange("p (h d) -> p h d", h=LH)
                    pool.tensor_tensor(k, k, rn[:, t % 2, LH:2 * LH].unsqueeze(2).to_broadcast([P, LH, LD]), ALU.mult)\
                        .then_inc(s["qk_ready"], 1)
                norm(8 + layer, (0,))
                if layer == 0:
                    split_w3(1, 0)
                    split_w3(1, 1)
                norm(8 + layer, (1,))
                if layer == 1:
                    pool.wait_ge(s["xn_ready"], 2 * 9 + 2)
                    pool.wait_ge(s["kept"], 2)
                    pool.tensor_tensor(x[:, :, :], x[:, :, :], kept[:, :, :], ALU.add).then_inc(s["kept_added"], 1)

            pool.memset(mhalf[:, :], -0.5).then_inc(s["pool_set"], 1)
            pool.memset(ones[:, :], 1.0).then_inc(s["pool_set"], 1)
            pool.wait_ge(s["pool_set"], 2)
            for what, i in order:
                {"att": attention, "moe": routed, "l2x": lambda i: norm(L2_HEAD), "loc": local}[what](i)

        @block.vector
        def _(dve):
            step = Count(dve, s["dve_step"])

            def then(instruction):
                step.done(instruction)
                step.wait()

            def split_low(dst, full, upper):
                return dve.tensor_tensor(dst, full, upper.bitcast(F32), ALU.subtract)

            def statistics(b, updates=None):
                if updates:
                    dve.wait_ge(s["x_added"], updates)
                for t in tiles(b):
                    last = dve.bn_stats(stats[:, t, 0:6], x[:, t, :])
                then(last)

            def variance(b, width):
                for t in tiles(b):
                    last = dve.bn_aggr(mv[:, t, :], stats[:, t, 0:width])
                then(last)
                dve.tensor_scalar(ve[:, HT * b:HT * b + HT], mv[:, HT * b:HT * b + HT, 1], EPS, None, ALU.add)\
                    .then_inc(s["ve_ready"], 1)

            def normal(ln, b):
                dve.wait_ge(s["rstd_ready"], 2 * ln + b + 1)
                for t in tiles(b):
                    last = dve.tensor_scalar(xn[:, t, :], x[:, t, :], mv[:, t, 0:1], rstd[:, t:t + 1],
                                             ALU.subtract, ALU.mult)
                last.then_inc(s["xn_ready"], 1)

            def low(jx, b):
                dve.wait_ge(s["xhi_ready"], 2 * jx + b + 1)
                split_low(half(x_lo, b), bank[6 + b], half(x_hi, b)).then_inc(s["xlo_ready"], 1)

            def head(ln):
                statistics(1)
                variance(1, 6)
                low(ln, 0)
                normal(ln, 1)
                low(ln, 1)

            def normal_stream(b):
                dve.wait_ge(s["kept"], b + 1)
                dve.wait_ge(s["rstd_ready"], 2 * 7 + b + 1)
                for t in tiles(b):
                    last = dve.tensor_scalar(x[:, t, :], x[:, t, :], mv[:, t, 0:1], rstd[:, t:t + 1],
                                             ALU.subtract, ALU.mult)
                last.then_inc(s["xn_ready"], 1)

            def low_stream(layer, b):
                c0 = b * S
                dve.memset(x_hi[64:P, c0:c0 + 1].bitcast(F32), 0.0)
                dve.memset(x_lo[64:P, c0:c0 + 1].bitcast(F32), 0.0)
                dve.wait_ge(s["xhi_ready"], 2 * (7 + 2 * layer) + b + 1)
                split_low(x_lo[0:64, c0:c0 + S], bank[4][0:64, :], x_hi[0:64, c0:c0 + S])
                split_low(x_lo[64:P, c0 + 1:c0 + S], bank[4][64:P, 0:S - 1], x_hi[64:P, c0 + 1:c0 + S])\
                    .then_inc(s["xlo_ready"], 1)

            def shifted_statistics(layer, b):
                dve.wait_ge(s["shift_ps"], 2 * layer + b + 1)
                for k, t in enumerate(tiles(b)):
                    dve.bn_stats(stats[:, t, 0:6], x[:, t, 0:64])
                    last = dve.bn_stats(stats[:, t, 6:12], bank[6 + b][:, 64 * k:64 * k + 64])
                then(last)
                variance(b, 12)

            def shifted_norm(layer, b):
                dve.wait_ge(s["rstd_ready"], 2 * (8 + layer) + b + 1)
                for k, t in enumerate(tiles(b)):
                    dve.tensor_scalar(xn[:, t, 0:64], x[:, t, 0:64], mv[:, t, 0:1], rstd[:, t:t + 1],
                                      ALU.subtract, ALU.mult)
                    last = dve.tensor_scalar(xn[:, t, 64:P], bank[6 + b][:, 64 * k:64 * k + 64], mv[:, t, 0:1],
                                             rstd[:, t:t + 1], ALU.subtract, ALU.mult)
                last.then_inc(s["xn_ready"], 1)

            def shifted_low(layer, b):
                dve.wait_ge(s["xhi_ready"], 2 * (8 + 2 * layer) + b + 1)
                split_low(half(x_lo, b), ytmp[:, b, :], half(x_hi, b)).then_inc(s["xlo_ready"], 1)

            def x_tiles(b):
                return x[:, HT * b:HT * b + HT, :].rearrange("p t d -> p (t d)")

            def routers():
                dve.wait_ge(s["ld_rw"], 16)
                then(dve.tensor_copy(rw_hi[:, :], rw[:, :]))
                split_low(rw_lo[:, :], rw[:, :], rw_hi[:, :]).then_inc(s["rw_ready"], 1)

            def window():
                dve.wait_ge(s["ld_l2"], 48)
                pt, index = vec[:, V_PT:V_PT + B], cst[:, C_IO:C_IO + L]
                dve.tensor_copy(l2s[:, 0:2], slen[:, :])
                dve.tensor_scalar(l2s[:, 2:4], pt, 16.0, 0.0, ALU.subtract, ALU.max)
                then(dve.tensor_scalar(l2s[:, 4:6], pt, 16.0, None, ALU.add))
                then(dve.tensor_tensor(l2s[:, 4:6], l2s[:, 4:6], l2s[:, 0:2], ALU.min))
                for b in range(B):
                    dve.tensor_scalar(valid[:, b, :], index, l2s[:, 2 + b:3 + b], None, ALU.is_ge)
                    dve.tensor_scalar(neg[:, b, :], index, l2s[:, 4 + b:5 + b], None, ALU.is_le)
                    last = dve.tensor_scalar(gauss[:, b, :], index, pt[:, b:b + 1], None, ALU.subtract)
                then(last)
                then(dve.tensor_tensor(valid[:, :, :], valid[:, :, :], neg[:, :, :], ALU.mult))
                dve.tensor_scalar(neg[:, :, :], valid[:, :, :], 1.0, 1e9, ALU.subtract, ALU.mult)
                dve.tensor_tensor(gauss[:, :, :], gauss[:, :, :], gauss[:, :, :], ALU.mult).then_inc(s["gauss_d2"], 1)

            def split_queries(i):
                dve.wait_ge(s["ld_aw" if i == 0 else "ld_aw_more"], 16)
                then(dve.tensor_copy(wq_hi[:, :], aw[:, i, 0:384]))
                split_low(wq_lo[:, :], aw[:, i, 0:384], wq_hi[:, :]).then_inc(s["wsplit"], 1)

            def attention(i):
                w = aw[:, i, :]
                jh = ATT_HEAD[i]

                def keys_full():
                    dve.wait_ge(s["k_ps"], i + 1)
                    for g in range(G):
                        last = dve.scalar_tensor_tensor(
                            out=k_f[:, g, :], in0=bank[4 + g // 3][0:96, (g % 3) * B * L:(g % 3 + 1) * B * L],
                            scalar=vec[0:96, V_BK + G * i + g:V_BK + G * i + g + 1], in1=tau_s[0:96, :],
                            op0=ALU.add, op1=ALU.mult)
                    if i == 0:
                        dve.wait_ge(s["ld_bo"], 16)
                    dve.tensor_tensor(brow[:, :], bank[5][0:1, 2 * P:3 * P], rows[0:1, i * P:(i + 1) * P], ALU.add)\
                        .then_inc(s["brow_ready"], 1)
                    then(last)

                def keys_stacked():
                    then(dve.tensor_copy(k_x[:, :, :], k_f[:, :, :]))
                    then(split_low(k_x[32:64, :, :], k_f[32:64, :, :], k_x[32:64, :, :]))
                    for h in range(HG):
                        last = dve.tensor_scalar(k_st[0:96, :, :, h * L:(h + 1) * L],
                                                 k_x[:, :, :].bitcast(F32).rearrange("p g (b k) -> p b g k", b=B),
                                                 cst[0:96, C_KM + h:C_KM + h + 1], None, ALU.mult)
                    last.then_inc(s["k_ready"], 1)

                if i == 0:
                    keys_full()
                    dve.wait_ge(s["ld_x"], 16)
                    statistics(0)
                    variance(0, 6)
                    statistics(1)
                    variance(1, 6)
                    normal(jh, 0)
                    normal(jh, 1)
                    low(jh, 0)
                else:
                    statistics(1)
                    variance(1, 6)
                    low(jh, 0)
                    keys_full()
                    normal(jh, 1)
                keys_stacked()

                def query_low(b):
                    for g in range(G):
                        n = G * b + g
                        dve.wait_ge(s["q_hi"], 8 * i + n + 1)
                        q = half(qs[64:96, g, :], b)
                        dve.scalar_tensor_tensor(out=q, in0=bank[n][64:96, :],
                                                 scalar=vec[64:96, V_BQ + G * i + g:V_BQ + G * i + g + 1],
                                                 in1=q.bitcast(F32), op0=ALU.add, op1=ALU.subtract).then_inc(s["q_lo"], 1)

                def maximum(t):
                    n = NT * i + t
                    sp_ = ps[:, 0:4, 0:GW].rearrange("p g (j k) -> p g j k", j=HG)
                    m = mx[:, t % 2, :].rearrange("p (g j) -> p g j", g=G)
                    dve.wait_ge(s["score_ps"], n + 1)
                    then(dve.tensor_reduce(m, sp_, AX.X, ALU.max))
                    if t >= 2:
                        dve.wait_ge(s["pt_ps"], 3 * (n - 1))
                    dve.tensor_tensor(e_sb[:, t % 2, 0:H * L].rearrange("p (g j k) -> p g j k", g=G, j=HG), sp_,
                                      m.unsqueeze(3).to_broadcast([P, G, HG, L]), ALU.subtract).then_inc(s["sub_done"], 1)

                def normalise(t):
                    dve.wait_ge(s["pv_ps"], NT * i + t + 1)
                    o = bank[7][:, 0:VW].rearrange("p (h d) -> p h d", h=H)
                    then(dve.reciprocal(rsum[:, t % 2, :], o[:, :, DK]))
                    dve.tensor_tensor(on[:, t, :].rearrange("p (h d) -> p h d", h=H), o[:, :, 0:DK],
                                      rsum[:, t % 2, :].unsqueeze(2).to_broadcast([P, H, DK]), ALU.mult)\
                        .then_inc(s["on_ready"], 1)

                def out_lo(b):
                    dve.wait_ge(s["oT_hi_ready"], 2 * i + b + 1)
                    split_low(oT_lo[:, :], bank[OT_BANK[b]], oT_hi[:, :]).then_inc(s["oT_lo_ready"], 1)

                def add(b):
                    dve.wait_ge(s["ao_ps"], 2 * i + b + 1)
                    dve.tensor_tensor(x_tiles(b), x_tiles(b), bank[AO_BANK[b]], ALU.add).then_inc(s["x_added"], 1)

                query_low(0)
                low(jh, 1)
                for t in range(NT):
                    maximum(t)
                    if t == 0:
                        query_low(1)
                    if t == 1:
                        then(dve.tensor_copy(wo_hi[:, :], w[:, 896:1024]))
                        split_low(wo_lo[:, :], w[:, 896:1024], wo_hi[:, :]).then_inc(s["wo_split"], 1)
                    if t >= 2:
                        normalise(t - 2)
                    if t == 4 and i < 2:
                        dve.wait_ge(s["q_ps"], 8 * i + 8)
                        split_queries(i + 1)
                    if i == 0 and t == 2:
                        routers()
                    if i == 0 and t == 3:
                        window()
                    if t == 6:
                        out_lo(0)
                    if t == 7:
                        add(0)
                        if i in ahead or i == 2:
                            dve.wait_ge(s["x_added"], before[("att", i)] + 1)
                            statistics(0)
                            variance(0, 6)
                normalise(NT - 2)
                if i in ahead:
                    normal(ahead[i], 0)
                elif i == 2:
                    normal_stream(0)
                normalise(NT - 1)
                if i in ahead:
                    low(ahead[i], 0)
                elif i == 2:
                    low_stream(0, 0)
                out_lo(1)
                add(1)
                dve.wait_ge(s["x_added"], before[("att", i)] + 2)

            def add_last(m, b):
                if m == 4:
                    dve.wait_ge(s["kept_added"], 1)
                dve.wait_ge(s["yT_ps"], 2 * m + b + 1)
                dve.tensor_tensor(x_tiles(b), x_tiles(b), bank[2 + b], ALU.add).then_inc(s["x_added"], 1)

            def add_routed(m, b):
                dve.wait_ge(s["yT_ps"], 2 * m + b + 1)
                if m != 1:
                    dve.tensor_tensor(x_tiles(b), x_tiles(b), bank[b], ALU.add).then_inc(s["x_added"], 1)
                    return
                dve.wait_ge(s["shared_added"], b + 1)
                for k, t in enumerate(tiles(b)):
                    last = dve.scalar_tensor_tensor(out=x[:, t, :], in0=bank[b][:, k * P:(k + 1) * P],
                                                    scalar=sm[:, 2, t:t + 1], in1=x[:, t, :], op0=ALU.mult, op1=ALU.add)
                last.then_inc(s["x_added"], 1)

            def feed_forward(kind, m, units, chunks):
                ub, pb, gb = unit_base[m], prod_base[m], group_base[m]
                lag = LAG[kind]

                def lower(u, full):
                    r = rows_of(kind, units[u][2])
                    k = (ub + u) % UB
                    split_low(a_lo[0:r, k, :], full[0:r, (ub + u) % 3, :], a_hi[0:r, k, :]).then_inc(s["alo_ready"], 1)

                def take_y(e, b):
                    g = group_of(kind, e, b)
                    u = max(n for n, (ee, bb, c) in enumerate(units) if (ee, bb) == (e, b))
                    dve.wait_ge(s["out_ps"], ub + u + 1)
                    w = e - {"gelu": 0, "top1": 4, "top2": 1, "geglu": 0}[kind]
                    if kind == "geglu":
                        v = V_B23 + m - 3
                        i_ = dve.tensor_scalar(half(acc, b), bank[y_bank(kind, b)], vec[:, v:v + 1], None, ALU.add)
                    elif kind == "top1":
                        i_ = dve.tensor_copy(half(acc, b) if e < 4 else ytmp[:, b, :], bank[b])
                    elif w < 0:
                        i_ = dve.tensor_copy(half(acc, b), bank[b])
                    else:
                        dve.wait_ge(s["cb_ready"], cb_base[m] + w + 1)
                        if e >= 2:
                            dve.wait_ge(s["acc_added"], 14 * (m // 2) + 2 * (e - 2) + b + 1)
                        dst = half(acc, b) if e == 0 else ytmp[:, b, :]
                        if kind == "gelu":
                            i_ = dve.scalar_tensor_tensor(out=dst, in0=bank[b], scalar=vec[:, V_B2 + e:V_B2 + e + 1],
                                                          in1=half(cB[:, w % 2, :], b), op0=ALU.add, op1=ALU.mult)
                        else:
                            i_ = dve.tensor_tensor(dst, bank[b], half(cB[:, w % 2, :], b), ALU.mult)
                    i_.then_inc(s["y_taken"], 1)

                for n in range(len(units) + lag + 1):
                    if kind == "geglu" and n == 2:
                        shifted_low(m - 3, 1)
                    v = n - lag - 1
                    if n == len(units) + lag and kind in ("gelu", "top2"):
                        add_routed(m, 0)
                    if n == len(units) + lag and kind == "geglu":
                        add_last(m, 0)
                    if v >= 0:
                        e, b, c = units[v]
                        if last_of_group(kind, chunks, e, c):
                            take_y(e, b)
                    if n == len(units) + 1 and kind == "top1":
                        for hb in range(B):
                            dve.wait_ge(s["shared_ps"], hb + 1)
                            dve.tensor_tensor(x_tiles(hb), x_tiles(hb), bank[2 + 2 * ((n - 4) % 3) + hb], ALU.add)\
                                .then_inc(s["shared_added"], 1)
                    if kind == "gelu":
                        if n < len(units):
                            g = ub + n
                            dve.wait_ge(s["gate_ready"], g + 1)
                            if n >= UB:
                                dve.wait_ge(s["out_ps"], g - UB + 1)
                            then(dve.tensor_copy(a_hi[:, g % UB, :], gate[:, g % 3, :]))
                            lower(n, gate)
                        continue
                    if kind == "top1" and n < len(units) and units[n][0] >= 4:
                        e, b, c = units[n]
                        w = e - 4
                        dve.wait_ge(s["hid_ps"], ub + n + 1)
                        dve.wait_ge(s["cb_ready"], cb_base[m] + w + 1)
                        dve.wait_ge(s["prod_ready"], pb + n - 2)
                        dve.tensor_tensor(gate[:, (ub + n) % 3, :], bank[pair_bank(kind, n)], half(cB[:, w % 2, :], b), ALU.mult)\
                            .then_inc(s["scaled"], 1)
                    u = n - 1 if kind == "top1" else n
                    if 0 <= u < len(units):
                        e, b, c = units[u]
                        g, r = ub + u, rows_of(kind, c)
                        dve.wait_ge(s["gate_ready"], g + 1)
                        if u >= 3:
                            dve.wait_ge(s["alo_ready"], g - 2)
                        up = bank[pair_bank(kind, u) + 1][0:r, :]
                        dst, gt = prod[0:r, g % 3, :], gate[0:r, g % 3, :]
                        if kind == "geglu":
                            v = V_B1A + (m - 3) * CH3 + c
                            i_ = dve.scalar_tensor_tensor(out=dst, in0=up, scalar=vec[:, v:v + 1], in1=gt,
                                                          op0=ALU.add, op1=ALU.mult)
                        else:
                            i_ = dve.tensor_tensor(dst, gt, up, ALU.mult)
                        i_.then_inc(s["prod_ready"], 1)
                    u -= 1
                    if 0 <= u < len(units):
                        dve.wait_ge(s["ahi_ready"], pb + u + 1)
                        lower(u, prod)

            def route(m):
                ne = (8, 16, 7)[m]
                cols = (8, 16, 8)[m]
                dve.wait_ge(s["lg_ps"], 2 * m + 2)
                logits = bank[0][:, 0:NT * cols].rearrange("p (t e) -> p t e", e=cols)
                every = lambda v, n: v.unsqueeze(2).to_broadcast([P, NT, n])
                index = cst[:, C_IO:C_IO + cols].unsqueeze(1).to_broadcast([P, NT, cols])
                top = 1 if m == 1 else 2
                if m == 1:
                    then(dve.tensor_copy(lg[:, :, 0:cols], logits))
                    ranked = lg
                else:
                    if m == 2:
                        rb = vec[:, V_RB:V_RB + 8].unsqueeze(1).to_broadcast([P, NT, 8])
                        then(dve.tensor_tensor(lg[:, :, 0:8], logits, rb, ALU.add))
                        logits = lg[:, :, 0:8]
                        dve.memset(pr[:, :, 7:8], -1.0)
                    then(dve.tensor_reduce(sm[:, 0, :], logits[:, :, 0:ne], AX.X, ALU.max))
                    dve.tensor_tensor(lg[:, :, 0:ne], logits[:, :, 0:ne], every(sm[:, 0, :], ne), ALU.subtract)\
                        .then_inc(s["rt_sub"], 1)
                    dve.wait_ge(s["rt_exp"], m + 1)
                    then(dve.tensor_reduce(sm[:, 1, :], lg[:, :, 0:ne], AX.X, ALU.add))
                    then(dve.reciprocal(sm[:, 2, :], sm[:, 1, :]))
                    then(dve.tensor_tensor(pr[:, :, 0:ne], lg[:, :, 0:ne], every(sm[:, 2, :], ne), ALU.mult))
                    ranked = pr
                for t in range(NT):
                    last = dve.max(m8[:, t, :], ranked[:, t, 0:cols])
                if m == 1:
                    last.then_inc(s["rt_sub"], 1)
                    dve.wait_ge(s["rt_sub"], 2)
                else:
                    then(last)
                for t in range(NT):
                    last = dve.max_index(i8[:, t, :], m8[:, t, :], ranked[:, t, 0:cols])
                then(last)
                then(dve.tensor_copy(i8f[:, :, 0:top], i8[:, :, 0:top]))
                for k in range(top):
                    last = dve.tensor_tensor(sel[:, k, :, 0:cols], index, every(i8f[:, :, k], cols), ALU.is_equal)
                then(last)
                if m == 1:
                    dve.wait_ge(s["rt_exp"], 2)
                    then(dve.tensor_scalar(sm[:, 1, :], sm[:, 0, :], 1.0, None, ALU.add))
                    then(dve.reciprocal(sm[:, 2, :], sm[:, 1, :]))
                    dve.tensor_tensor(cw[:, :, 0:cols], sel[:, 0, :, 0:cols], every(sm[:, 2, :], cols), ALU.mult)\
                        .then_inc(s["cw_ready"], 1)
                else:
                    then(dve.tensor_tensor(sel[:, 0, :, 0:cols], sel[:, 0, :, 0:cols], sel[:, 1, :, 0:cols], ALU.add))
                    then(dve.tensor_tensor(cw[:, :, 0:cols], sel[:, 0, :, 0:cols], pr[:, :, 0:cols], ALU.mult))
                    then(dve.tensor_reduce(sm[:, 0, :], cw[:, :, 0:cols], AX.X, ALU.add))
                    then(dve.reciprocal(sm[:, 1, :], sm[:, 0, :]))
                    dve.tensor_tensor(cw[:, :, 0:cols], cw[:, :, 0:cols], every(sm[:, 1, :], cols), ALU.mult)\
                        .then_inc(s["cw_ready"], 1)

            def routed(m):
                p = plans[m]
                if m in (0, 1):
                    statistics(1)
                    variance(1, 6)
                    normal(MOE_HEAD[m], 1)
                    low(MOE_HEAD[m], 1)
                else:
                    head(MOE_HEAD[m])
                route(m)
                feed_forward(p["kind"], m, p["units"], p["chunks"])
                if m == 1:
                    add_routed(m, 0)
                statistics(0, before[("moe", m)] + 1)
                variance(0, 6)
                normal(after_moe[m], 0)
                add_routed(m, 1)
                dve.wait_ge(s["x_added"], before[("moe", m)] + 2)

            def l2_attention():
                dve.wait_ge(s["ld_l2"], 48)
                dve.memset(m_hi[:, :, L:78].bitcast(F32), 0.0)
                dve.memset(m_lo[:, :, L:78].bitcast(F32), 0.0)
                statistics(1)
                variance(1, 6)
                low(L2_HEAD, 0)
                normal(L2_HEAD, 1)
                dve.wait_ge(s["m_ps"], 1)
                m_ps = bank[3][:, 0:B * L].rearrange("p (b k) -> p b k", b=B)
                dve.tensor_copy(m_hi[:, :, 0:L], m_ps)
                then(dve.tensor_copy(wc_hi[:, :], l2w[:, P:3 * P]))
                split_low(wc_lo[:, :], l2w[:, P:3 * P], wc_hi[:, :])
                split_low(m_lo[:, :, 0:L], m_ps, m_hi[:, :, 0:L]).then_inc(s["m_ready"], 1)
                low(L2_HEAD, 1)
                every = lambda v: v.unsqueeze(2).to_broadcast([P, HT, L])
                row = lambda v: v.unsqueeze(1).to_broadcast([P, HT, L])
                for b in range(B):
                    ts = slice(HT * b, HT * b + HT)
                    z = sc[:, ts, :]
                    dve.wait_ge(s["s_ps"], b + 1)
                    src = bank[b][:, 0:HT * 78].rearrange("p (t k) -> p t k", t=HT)[:, :, 0:L]
                    then(dve.tensor_tensor(z, src, row(valid[:, b, :]), ALU.mult))
                    then(dve.tensor_tensor(z, z, row(neg[:, b, :]), ALU.add))
                    then(dve.tensor_reduce(l2m[:, 0, ts], z, AX.X, ALU.max))
                    dve.tensor_tensor(z, z, every(l2m[:, 0, ts]), ALU.subtract).then_inc(s["s_sub"], 1)
                dve.wait_ge(s["gauss_ready"], 1)
                for b in range(B):
                    ts = slice(HT * b, HT * b + HT)
                    z, z2 = sc[:, ts, :], sc2[:, ts, :]
                    dve.wait_ge(s["s_exp"], b + 1)
                    then(dve.tensor_reduce(l2m[:, 1, ts], z, AX.X, ALU.add))
                    then(dve.reciprocal(l2m[:, 2, ts], l2m[:, 1, ts]))
                    then(dve.tensor_tensor(z2, z, every(l2m[:, 2, ts]), ALU.mult))
                    dve.tensor_tensor(z2, z2, row(gauss[:, b, :]), ALU.mult).then_inc(s["al_ready"], 1)
                for b in range(B):
                    dve.wait_ge(s["chi_ready"], b + 1)
                    split_low(c_lo[:, b, :], bank[4 + b], c_hi[:, b, :]).then_inc(s["clo_ready"], 1)
                for b in range(B):
                    dve.wait_ge(s["tanh_ready"], b + 1)
                    dve.tensor_tensor(x_tiles(b), x_tiles(b), th[:, b, :], ALU.add).then_inc(s["x_added"], 1)
                    if b == 0:
                        statistics(0, before[("l2x", 0)] + 1)
                        variance(0, 6)
                        normal(MOE_HEAD[2], 0)
                dve.wait_ge(s["x_added"], before[("l2x", 0)] + 2)

            def local(layer):
                m, ja, jf = 3 + layer, 7 + 2 * layer, 8 + 2 * layer
                n0 = NT * layer
                if layer == 0:
                    statistics(1)
                    variance(1, 6)
                    dve.tensor_copy(ident_b[:, :], ident)
                    dve.tensor_copy(mask[:, :], cst[:, C_MS:C_MS + P + WIN])

                def scale_tables(layer):
                    for k in range(4):
                        v = V_QS + (4 * layer + k) * LD
                        last = dve.tensor_tensor(rope[:, k, :, :], rope_raw[:, k, :, :],
                                                 vec[:, v:v + LD].unsqueeze(1).to_broadcast([P, HT, LD]), ALU.mult)
                    then(last)

                if layer == 0:
                    dve.wait_ge(s["ld_rope"], 16)
                    scale_tables(0)

                def rotate(t, what):
                    dve.wait_ge(s["sq_ready"], 2 * (n0 + t) + what + 1)
                    if what == 0 and t > 1:
                        dve.wait_ge(s["qk_ready"], n0 + t)
                    src = bank[6 + what].rearrange("p (h d) -> p h d", h=LH)
                    swapped = bank[6 + what].rearrange("p (h a d) -> p h a d", h=LH, a=2)[:, :, ::-1, :]
                    c, sn = rope[:, 2 * what, t % HT, :], rope[:, 2 * what + 1, t % HT, :]
                    dve.tensor_tensor(r1[:, what, :].rearrange("p (h d) -> p h d", h=LH), src,
                                      c.unsqueeze(1).to_broadcast([P, LH, LD]), ALU.mult)
                    dve.tensor_tensor(r2[:, what, :].rearrange("p (h a d) -> p h a d", h=LH, a=2), swapped,
                                      sn.rearrange("p (a d) -> p a d", a=2).unsqueeze(1).to_broadcast([P, LH, 2, LD // 2]),
                                      ALU.mult).then_inc(s[("rot_ready", "kr_ready")[what]], 1)

                def norms(t):
                    n = n0 + t
                    dve.wait_ge(s["sq_ready"], 2 * n + 2)
                    if t >= 2:
                        dve.wait_ge(s["qk_ready"], n)
                    then(dve.tensor_reduce(ssq[:, t % 2, :], sq[:, :, :].rearrange("p w (h d) -> p (w h) d", h=LH),
                                           AX.X, ALU.add))
                    dve.tensor_scalar(ssq[:, t % 2, :], ssq[:, t % 2, :], 1e-24, None, ALU.max).then_inc(s["ssq_ready"], 1)

                def query_scale(t):
                    dve.wait_ge(s["qk_ready"], n0 + t + 1)
                    if t >= 2:
                        dve.wait_ge(s["p3_ready"], 4 * (n0 + t) - 4)
                    dve.tensor_scalar(rq[:, t % 2, 0, :], rn[:, t % 2, 0:LH], QK_SCALE, None, ALU.mult)
                    then(dve.tensor_scalar(rq[:, t % 2, 1, :], rn[:, t % 2, 0:LH], -QK_SCALE, None, ALU.mult))

                def maximum(q):
                    t, pair = divmod(q, 4)
                    w = P + (WIN if t % HT else 0)
                    dve.wait_ge(s["sim_ps"], 4 * n0 + q + 1)
                    h = slice(2 * pair, 2 * pair + 2)
                    then(dve.tensor_reduce(mx3[:, t % 2, h],
                                           bank[q % 2][:, 0:384].rearrange("p (h k) -> p h k", h=2)[:, :, 0:w], AX.X, ALU.max))
                    dve.tensor_tensor(nb3[:, t % 2, h], mx3[:, t % 2, h], rq[:, t % 2, 1, h], ALU.mult)\
                        .then_inc(s["nb_ready"], 1)

                def normalise(t):
                    dve.wait_ge(s["pv3_ps"], 4 * (n0 + t) + 4)
                    if t >= 2:
                        dve.wait_ge(s["o3_ps"], n0 + t - 1)
                    then(dve.reciprocal(rs3[:, t % 2, :], sum3[:, t % 2, :]))
                    dve.tensor_tensor(on3[:, t % 2, :].rearrange("p (h d) -> p h d", h=LH),
                                      bank[4].rearrange("p (h d) -> p h d", h=LH),
                                      rs3[:, t % 2, :].unsqueeze(2).to_broadcast([P, LH, LD]), ALU.mult)\
                        .then_inc(s["on3_ready"], 1)

                def out_lo(t):
                    dve.wait_ge(s["ohi_ready"], n0 + t + 1)
                    split_low(o_lo[:, t % 2, :], bank[5], o_hi[:, t % 2, :]).then_inc(s["olo_ready"], 1)

                def add(t):
                    dve.wait_ge(s["o3_out"], n0 + t + 1)
                    dve.tensor_tensor(x[:, t, :], x[:, t, :], bank[7][:, 0:P], ALU.add).then_inc(s["x3_added"], 1)

                for t in range(2):
                    rotate(t, 0)
                    norms(t)
                    rotate(t, 1)
                    if t == 0:
                        dve.wait_ge(s["kr_ready"], n0 + 1)
                        dve.tensor_tensor(qk[:, 0, :, :], r1[:, :, :], r2[:, :, :], ALU.add).then_inc(s["first_sum"], 1)
                        dve.wait_ge(s["first_sum"], layer + 1)
                        if layer == 0:
                            normal_stream(1)
                query_scale(0)
                maximum(0)
                maximum(1)
                low_stream(layer, 1)
                for q in range(4 * NT):
                    t, pair = divmod(q, 4)
                    if pair == 2 and t + 1 < NT:
                        query_scale(t + 1)
                    if q + 2 < 4 * NT:
                        maximum(q + 2)
                    if q % 2 == 0:
                        dve.wait_ge(s["pT3_ps"], 4 * n0 + q + 1)
                        if q >= 2:
                            dve.wait_ge(s["pv3_ps"], 4 * n0 + q - 1)
                        blk = slice(0 if t % HT else 1, 2)
                        src = bank[2].rearrange("p (h k n) -> p h k n", h=2, k=2)[:, :, blk, :]
                        dve.tensor_copy(pT3[:, 0, :, :].rearrange("p (h k) n -> p h k n", h=2)[:, :, blk, :], src)\
                            .then_inc(s["pT3_even"], 1)
                    if pair == 0 and t > 1:
                        add(t - 2)
                    if pair == 0 and t + 2 < NT:
                        rotate(t + 2, 0)
                    if pair == 0 and t > 0:
                        normalise(t - 1)
                    if pair == 1 and t + 2 < NT:
                        norms(t + 2)
                        rotate(t + 2, 1)
                    if pair == 3 and t > 0:
                        out_lo(t - 1)
                    if q == 4 * (NT - 2) and layer == 0:
                        scale_tables(1)
                    if q == 4 * (NT - 2) + 2:
                        shifted_statistics(layer, 0)
                    if q == 4 * (NT - 1):
                        shifted_norm(layer, 0)
                shifted_low(layer, 0)
                normalise(NT - 1)
                out_lo(NT - 1)
                add(NT - 2)
                add(NT - 1)
                dve.wait_ge(s["x3_added"], n0 + NT)
                shifted_statistics(layer, 1)
                shifted_norm(layer, 1)
                feed_forward("geglu", m, [(0, b, c) for b in range(B) for c in range(CH3)], CH3)
                if layer == 0:
                    low_stream(1, 0)
                add_last(m, 1)
                dve.wait_ge(s["x_added"], before[("loc", layer)] + 2)

            split_queries(0)
            dve.wait_ge(s["ld_vec"], 16)
            dve.wait_ge(s["ld_cst"], 16)
            isq = 1.0 / float(np.sqrt(DK))
            dve.tensor_scalar(tau_s[:, :], vec[:, V_TAU:V_TAU + B * L], isq, None, ALU.mult)
            then(dve.tensor_scalar(del_f[:, :], vec[:, V_DEL:V_DEL + B * L], isq, None, ALU.mult))
            then(dve.tensor_copy(del_h[:, :], del_f[:, :]))
            then(split_low(del_l[:, :], del_f[:, :], del_h[:, :]))
            then(dve.tensor_scalar(del_l[:, :], del_l[:, :], cst[:, C_DM + 1:C_DM + 2], None, ALU.mult))
            then(dve.scalar_tensor_tensor(out=del_x[:, :], in0=del_h[:, :].bitcast(F32), scalar=cst[:, C_DM:C_DM + 1],
                                          in1=del_l[:, :], op0=ALU.mult, op1=ALU.add))
            for b in range(B):
                dve.tensor_copy(k_st[96:P, b, :, :].rearrange("p g (j k) -> p (g j) k", j=HG),
                                del_x[96:P, b * L:(b + 1) * L].unsqueeze(1).to_broadcast([32, H, L]))
            dve.tensor_copy(v_bd[:, :, :, DK], cst[:, C_VM:C_VM + B * NC * H].rearrange("p (c h) -> p c h", h=H))
            for what, i in order:
                {"att": attention, "moe": routed, "l2x": lambda i: l2_attention(), "loc": local}[what](i)



def constants():
    c = np.zeros((P, NCONST), np.float32)
    r = np.arange(P)
    c[r, C_ID + r] = 1.0
    for j in range(HG):
        c[:96, C_KM + j] = (r[:96] % 32) // DK == j
    c[96, C_DM] = 1.0
    c[97, C_DM + 1] = 1.0
    for k in range(B * NC):
        flat = (k % NC) * P + r
        for h in range(H):
            c[:, C_VM + k * H + h] = flat // L == h
    c[:, C_IO:C_IO + L + 1] = np.arange(L + 1)
    c[r[:-1], C_SH + r[1:]] = 1.0
    c[P - 1, C_SE] = 1.0
    i, j = r[:, None], np.arange(P + WIN)[None, :]
    c[:, C_MS:C_MS + P + WIN] = np.where((j >= i) & (j <= i + WIN), 0.0, -1e30)
    return c


def rotary():
    f = np.float32
    half_idx = np.arange(0, LD, 2, dtype=f)
    inv = (f(1.0) / f(10000.0) ** (half_idx / f(LD))).astype(f)
    t = np.arange(S, dtype=f)
    freqs = t[:, None] * inv[None, :]
    freqs = np.concatenate([freqs, freqs], -1)
    base = (half_idx + f(0.4 * LD)) / f(1.4 * LD)
    power = (t - f(S // 2)) / f(WIN // 2)
    scale = np.power(base[None, :].astype(f), power[:, None]).astype(f)
    scale = np.concatenate([scale, scale], -1)
    sign = np.concatenate([-np.ones(LD // 2, f), np.ones(LD // 2, f)])
    cos, sin = np.cos(freqs), np.sin(freqs) * sign
    tabs = np.stack([cos * scale, sin * scale, cos / scale, sin / scale]).astype(f)
    return np.ascontiguousarray(tabs.reshape(4, HT, P, LD).transpose(2, 0, 1, 3))


def lay_out(a):
    f = np.float32
    d = {"consts": constants(), "rope": rotary()}
    d["x"] = a["x"].reshape(NT, P, P).transpose(1, 0, 2)
    c = a["ctx_1024"]
    cT = c.transpose(2, 0, 1)
    d["ctxT"] = cT.reshape(P, B * L)
    rep = np.zeros((P, B, NC * P), f)
    rep[:, :, :H * L] = np.tile(cT, (1, 1, H))
    d["ctx_rep"] = rep
    d["ctx_n"] = c.transpose(1, 0, 2)
    att = ("L0", "L1", "L3")
    aw = np.zeros((P, 3, 1024), f)
    vec = np.zeros((P, NVEC), f)
    rows = np.zeros((1, NROW), f)

    def stack(w):
        return np.repeat(w.reshape(-1, G, 1, 32), 3, axis=2).reshape(-1, G * 96)

    for i, n in enumerate(att):
        g = lambda k: a[f"{n}_xcond_{k}"]
        aw[:, i, 0:384] = stack(g("Wq").T)
        aw[:, i, 384:768] = stack(g("Wk").T)
        aw[:, i, 768:896] = g("Wv").T
        aw[:, i, 896:1024] = g("Wo").T
        vec[0:96, V_BQ + G * i:V_BQ + G * i + G] = stack(g("bq")[None, :]).reshape(G, 96).T
        vec[0:96, V_BK + G * i:V_BK + G * i + G] = stack(g("bk")[None, :]).reshape(G, 96).T
        vec[:, V_BV + i] = g("bv")
        rows[0, i * P:(i + 1) * P] = g("bo")
    d["aw"], d["rows"] = aw, rows
    vec[:, V_B1:V_B1 + 32] = a["L0_ffn_b1"].reshape(32, P).T
    vec[:, V_B2:V_B2 + 8] = a["L0_ffn_b2"].T
    vec[:, V_LG:V_LG + DEPTH] = a["L3_ffn_ln_g"].T
    vec[:, V_LB:V_LB + DEPTH] = a["L3_ffn_ln_b"].T
    hid = a["L3_ffn_b1"].shape[1] // 2
    pad = np.zeros((DEPTH, 2, CH3 * P), f)
    pad[:, :, :hid] = a["L3_ffn_b1"].reshape(DEPTH, 2, hid)
    vec[:, V_B1A:V_B1A + DEPTH * CH3] = pad[:, 0].reshape(DEPTH * CH3, P).T
    vec[:, V_B1G:V_B1G + DEPTH * CH3] = pad[:, 1].reshape(DEPTH * CH3, P).T
    vec[:, V_B23:V_B23 + DEPTH] = a["L3_ffn_b2"].T
    vec[:, V_TAU:V_TAU + B * L] = np.repeat(a["condB_tau"], L)[None, :]
    vec[:, V_DEL:V_DEL + B * L] = a["fside_BxS2_0"].reshape(1, B * L)
    vec[:, V_PT:V_PT + B] = a["condB_pt"][None, :]
    vec[:, V_RB:V_RB + 7] = a["L2_ffn_rb"][None, :]
    for layer in range(DEPTH):
        for k, name in enumerate(("q_scale", "k_scale")):
            v = a[f"L3_ffn_{name}"][layer]
            o = V_QS + (4 * layer + 2 * k) * LD
            vec[:, o:o + LD] = v[None, :]
            vec[:, o + LD:o + 2 * LD] = np.concatenate([v[LD // 2:], v[:LD // 2]])[None, :]
    d["vec"] = vec
    rw = np.zeros((P, 32), f)
    rw[:, 0:8] = a["L0_ffn_Wr"]
    rw[:, 8:24] = a["L1_ffn_router_w"].T
    rw[:, 24:31] = a["L2_ffn_wr"].T
    d["rw"] = rw
    wc = a["L2_xcond_W_c"].T
    d["l2w"] = np.concatenate([a["L2_xcond_W_a"].T, wc[:P], wc[P:]], axis=1)
    d["slen"] = np.repeat(a["_lenS2"][None, :], P, axis=0)
    w2 = a["L0_ffn_W2"].reshape(8, 4, P, P).transpose(0, 2, 1, 3).reshape(8, P, 4 * P)
    d["w0"] = np.concatenate([a["L0_ffn_W1"], w2], axis=2)
    w = np.zeros((20, P, 384), f)
    w[4:, :, 0:256] = a["L1_ffn_gate_up_proj"]
    w[4:, :, 256:384] = a["L1_ffn_down_proj"]
    for e in range(4):
        r = slice(e * P, (e + 1) * P)
        w[e, :, 0:128] = a["L1_ffn_shared_gate_w"][r].T
        w[e, :, 128:256] = a["L1_ffn_shared_up_w"][r].T
        w[e, :, 256:384] = a["L1_ffn_shared_down_w"][:, r].T
    d["w1"] = w
    w = np.zeros((8, P, 1088), f)
    for e in range(8):
        gw, uw, dw = ((a["L2_ffn_sg"], a["L2_ffn_su"], a["L2_ffn_sd"]) if e == 0 else
                      (a["L2_ffn_rg"][e - 1], a["L2_ffn_ru"][e - 1], a["L2_ffn_rd"][e - 1]))
        w[e, :, 0:352] = gw.T
        w[e, :, 352:704] = uw.T
        for k in range(3):
            part = dw[:, k * P:(k + 1) * P].T
            w[e, :part.shape[0], 704 + k * P:704 + (k + 1) * P] = part
    d["w2"] = w
    w = np.zeros((DEPTH, P, L3W), f)
    w[:, :, 0:3 * INNER] = a["L3_ffn_wqkv"]
    w[:, :, 3 * INNER:4 * INNER] = a["L3_ffn_wo"].reshape(DEPTH, 4, P, P).transpose(0, 2, 1, 3).reshape(DEPTH, P, INNER)
    w[:, :, 4 * INNER:4 * INNER + hid] = a["L3_ffn_w1"][:, :, :hid]
    w[:, :, 4 * INNER + CH3 * P:4 * INNER + CH3 * P + hid] = a["L3_ffn_w1"][:, :, hid:]
    w2 = np.zeros((DEPTH, CH3 * P, P), f)
    w2[:, :hid] = a["L3_ffn_w2"]
    w[:, :, 4 * INNER + 2 * CH3 * P:] = w2.reshape(DEPTH, CH3, P, P).transpose(0, 2, 1, 3).reshape(DEPTH, P, CH3 * P)
    d["w3"] = w
    return {k: np.ascontiguousarray(v) for k, v in d.items()}


def kernel(**inputs):
    import concourse.bacc as bacc
    from concourse.bass_utils import run_bass_kernel_spmd

    nc = bacc.Bacc("TRN2", target_bir_lowering=False, num_devices=1)
    arrays = {f"in_{k}": v for k, v in lay_out({k: np.asarray(v) for k, v in inputs.items()}).items()}
    d = {k[3:]: nc.dram_tensor(k, v.shape, mybir.dt.from_np(v.dtype), kind="ExternalInput").ap() for k, v in arrays.items()}
    out = nc.dram_tensor("out", (P, NT, P), F32, kind="ExternalOutput").ap()
    build(nc, d, out)
    r = run_bass_kernel_spmd(nc, [arrays], core_ids=[0])
    return np.asarray(r.results[0]["out"]).transpose(1, 0, 2).reshape(B, S, P)
```
